# Optimizing a Trainium2 kernel written in Bass

```python
import numpy as np
import jax
import jax.numpy as jnp

def _softmax(x, axis=-1):
    return jax.nn.softmax(x, axis=axis)

def _gelu(x):
    return jax.nn.gelu(x, approximate=True)

def _silu(x):
    return jax.nn.silu(x)

def _sigmoid(x):
    return jax.nn.sigmoid(x)

def _layernorm(x, axis=-1, eps=1e-05):
    m = jnp.mean(x, axis=axis, keepdims=True)
    v = jnp.var(x, axis=axis, keepdims=True)
    return (x - m) / jnp.sqrt(v + eps)

def _scatter_add(tgt, idx, src, axis=0):
    return tgt.at[idx].add(src)

def _segment_sum(src, seg, n):
    return jax.ops.segment_sum(src, seg, n)
kernel_name = 'mk_decoder_postln_d1_seqx_r4_db32fb'

def setup_inputs(seed: int=0):
    np.random.seed(seed)
    _w = jnp.asarray

    def _rec_inputs():
        import jax
        import jax.numpy as jnp
        _rk = jax.random.key(seed)
        x = -9.806e-05 + 1 * jax.random.normal(jax.random.fold_in(_rk, 1), (8, 256, 256), jnp.float32)
        _lenS = 256 - jax.random.randint(jax.random.fold_in(_rk, 7), (8,), 0, max(1, 256 // 4) + 1, jnp.int32)
        _lenS2 = 120 - jax.random.randint(jax.random.fold_in(_rk, 8), (8,), 0, max(1, 120 // 4) + 1, jnp.int32)
        _ctx_1024P = jax.random.normal(jax.random.fold_in(_rk, 11), (8, 16, 256), jnp.float32)
        _ctx_1024c = jax.random.dirichlet(jax.random.fold_in(_rk, 511), 0.3 * jnp.ones((16,), jnp.float32), (8, 120))
        _ctx_1024t = jnp.einsum('bsk,bkd->bsd', _ctx_1024c, _ctx_1024P)
        _ctx_1024t = _ctx_1024t * jax.lax.rsqrt(jnp.mean(jnp.square(_ctx_1024t)) + 1e-12) * 0.953939
        ctx_1024 = -1.52775e-05 + 0.999936 * (_ctx_1024t + 0.3 * jax.random.normal(jax.random.fold_in(_rk, 611), (8, 120, 256), jnp.float32))
        return (x, ctx_1024)
    x, ctx_1024 = _rec_inputs()

    def _L0_attn_setup():
        import jax, jax.numpy as jnp
        import numpy as np
        DIM = 256
        HEADS = 16
        HEAD_DIM = 64
        key = jax.random.key(seed)
        ks = jax.random.split(key, 6)
        inner = HEADS * HEAD_DIM
        s = 0.02
        return {'x': jax.random.normal(ks[0], (2, 512, DIM), dtype=jnp.float32), 'Wq': jax.random.normal(ks[1], (DIM, inner), dtype=jnp.float32) * s, 'Wk': jax.random.normal(ks[2], (DIM, inner), dtype=jnp.float32) * s, 'Wv': jax.random.normal(ks[3], (DIM, inner), dtype=jnp.float32) * s, 'Wo': jax.random.normal(ks[4], (inner, DIM), dtype=jnp.float32) * s, 'bo': jax.random.normal(ks[5], (DIM,), dtype=jnp.float32) * s}
    _L0_attn_all = _L0_attn_setup()
    _L0_attn_in = {k: v for k, v in _L0_attn_all.items() if k in ('Wq', 'Wk', 'Wv', 'Wo', 'bo')}
    del _L0_attn_all

    def _L0_xattn_setup():
        import jax, jax.numpy as jnp
        import numpy as np
        D = 256
        NUM_ITERS = 3
        EPS = 1e-06
        SCALE = D ** (-0.5)

        def rmsnorm(x, w, eps=EPS):
            return x * jax.lax.rsqrt(jnp.mean(x * x, axis=-1, keepdims=True) + eps) * w

        def gru_cell(x, h, wih, whh, bih, bhh):
            gx = x @ wih.T + bih
            gh = h @ whh.T + bhh
            xr, xz, xn = jnp.split(gx, 3, axis=-1)
            hr, hz, hn = jnp.split(gh, 3, axis=-1)
            r = jax.nn.sigmoid(xr + hr)
            z = jax.nn.sigmoid(xz + hz)
            n = jnp.tanh(xn + r * hn)
            return (1.0 - z) * n + z * h
        key = jax.random.key(seed)
        ks = jax.random.split(key, 8)
        B, K, M, d = (8, 64, 1024, D)
        w_std = d ** (-0.5)
        return {'slots': jax.random.normal(ks[0], (B, K, d), jnp.float32), 'P': jax.random.normal(ks[1], (B, M, d), jnp.float32), 'Wq': jax.random.normal(ks[2], (d, d), jnp.float32) * w_std, 'Wk': jax.random.normal(ks[3], (d, d), jnp.float32) * w_std, 'Wv': jax.random.normal(ks[4], (d, d), jnp.float32) * w_std, 'gru_wih': jax.random.normal(ks[5], (3 * d, d), jnp.float32) * w_std, 'gru_whh': jax.random.normal(ks[6], (3 * d, d), jnp.float32) * w_std, 'gru_bih': jnp.zeros((3 * d,), jnp.float32), 'gru_bhh': jnp.zeros((3 * d,), jnp.float32), 'slot_norm_w': jnp.ones((d,), jnp.float32), 'input_norm_w': jnp.ones((d,), jnp.float32)}
    _L0_xattn_all = _L0_xattn_setup()
    _L0_xattn_in = {k: v for k, v in _L0_xattn_all.items() if k in ('Wq', 'Wk', 'Wv', 'gru_wih', 'gru_whh', 'gru_bih', 'gru_bhh', 'slot_norm_w', 'input_norm_w')}
    del _L0_xattn_all

    def _L0_ffn_setup():
        import jax, jax.numpy as jnp
        import numpy as np
        TOP_K = 2

        def _mlp(x, w1, b1, w2, b2):
            h = jax.nn.gelu(jnp.einsum('bsd,di->bsi', x, w1) + b1)
            return jnp.einsum('bsi,id->bsd', h, w2) + b2
        key = jax.random.key(seed)
        ks = jax.random.split(key, 8)
        B, S, D, I, E = (2, 512, 256, 1024, 8)
        s_in = 1.0 / np.sqrt(D)
        s_mid = 1.0 / np.sqrt(I)
        return {'x': jax.random.normal(ks[0], (B, S, D), jnp.float32), 'gate_w': jax.random.normal(ks[1], (D, E), jnp.float32) * s_in, 'gate_b': jnp.zeros((E,), jnp.float32), 'sh_w1': jax.random.normal(ks[2], (D, I), jnp.float32) * s_in, 'sh_b1': jnp.zeros((I,), jnp.float32), 'sh_w2': jax.random.normal(ks[3], (I, D), jnp.float32) * s_mid, 'sh_b2': jnp.zeros((D,), jnp.float32), 'ew1': jax.random.normal(ks[4], (E, D, I), jnp.float32) * s_in, 'eb1': jnp.zeros((E, I), jnp.float32), 'ew2': jax.random.normal(ks[5], (E, I, D), jnp.float32) * s_mid, 'eb2': jnp.zeros((E, D), jnp.float32)}
    _L0_ffn_all = _L0_ffn_setup()
    _L0_ffn_in = {k: v for k, v in _L0_ffn_all.items() if k in ('gate_w', 'gate_b', 'sh_w1', 'sh_b1', 'sh_w2', 'sh_b2', 'ew1', 'eb1', 'ew2', 'eb2')}
    del _L0_ffn_all
    return {'x': x, 'ctx_1024': ctx_1024, 'L0_attn_Wq': _L0_attn_in['Wq'], 'L0_attn_Wk': _L0_attn_in['Wk'], 'L0_attn_Wv': _L0_attn_in['Wv'], 'L0_attn_Wo': _L0_attn_in['Wo'], 'L0_attn_bo': _L0_attn_in['bo'], 'L0_xattn_Wq': _L0_xattn_in['Wq'], 'L0_xattn_Wk': _L0_xattn_in['Wk'], 'L0_xattn_Wv': _L0_xattn_in['Wv'], 'L0_xattn_gru_wih': _L0_xattn_in['gru_wih'], 'L0_xattn_gru_whh': _L0_xattn_in['gru_whh'], 'L0_xattn_gru_bih': _L0_xattn_in['gru_bih'], 'L0_xattn_gru_bhh': _L0_xattn_in['gru_bhh'], 'L0_xattn_slot_norm_w': _L0_xattn_in['slot_norm_w'], 'L0_xattn_input_norm_w': _L0_xattn_in['input_norm_w'], 'L0_ffn_gate_w': _L0_ffn_in['gate_w'], 'L0_ffn_gate_b': _L0_ffn_in['gate_b'], 'L0_ffn_sh_w1': _L0_ffn_in['sh_w1'], 'L0_ffn_sh_b1': _L0_ffn_in['sh_b1'], 'L0_ffn_sh_w2': _L0_ffn_in['sh_w2'], 'L0_ffn_sh_b2': _L0_ffn_in['sh_b2'], 'L0_ffn_ew1': _L0_ffn_in['ew1'], 'L0_ffn_eb1': _L0_ffn_in['eb1'], 'L0_ffn_ew2': _L0_ffn_in['ew2'], 'L0_ffn_eb2': _L0_ffn_in['eb2']}

def reference(x, ctx_1024, L0_attn_Wq, L0_attn_Wk, L0_attn_Wv, L0_attn_Wo, L0_attn_bo, L0_xattn_Wq, L0_xattn_Wk, L0_xattn_Wv, L0_xattn_gru_wih, L0_xattn_gru_whh, L0_xattn_gru_bih, L0_xattn_gru_bhh, L0_xattn_slot_norm_w, L0_xattn_input_norm_w, L0_ffn_gate_w, L0_ffn_gate_b, L0_ffn_sh_w1, L0_ffn_sh_b1, L0_ffn_sh_w2, L0_ffn_sh_b2, L0_ffn_ew1, L0_ffn_eb1, L0_ffn_ew2, L0_ffn_eb2):
    import jax
    import jax.numpy as jnp

    def _L0_attn_ref(x, Wq, Wk, Wv, Wo, bo):
        import jax, jax.numpy as jnp
        import numpy as np
        DIM = 256
        HEADS = 16
        HEAD_DIM = 64
        N, S, _ = x.shape
        scale = 1.0 / np.sqrt(HEAD_DIM).astype(np.float32)
        q = (x @ Wq).reshape(N, S, HEADS, HEAD_DIM).transpose(0, 2, 1, 3)
        k = (x @ Wk).reshape(N, S, HEADS, HEAD_DIM).transpose(0, 2, 1, 3)
        v = (x @ Wv).reshape(N, S, HEADS, HEAD_DIM).transpose(0, 2, 1, 3)
        logits = jnp.einsum('nhid,nhjd->nhij', q, k) * scale
        causal = 1000000000.0 * (jnp.tril(jnp.ones((S, S), dtype=logits.dtype)) - 1.0)
        logits = logits + causal[None, None, :, :]
        attn = jax.nn.softmax(logits, axis=-1)
        out = jnp.einsum('nhij,nhjd->nhid', attn, v)
        out = out.transpose(0, 2, 1, 3).reshape(N, S, HEADS * HEAD_DIM)
        return out @ Wo + bo

    def _L0_xattn_ref(slots, P, Wq, Wk, Wv, gru_wih, gru_whh, gru_bih, gru_bhh, slot_norm_w, input_norm_w):
        import jax, jax.numpy as jnp
        import numpy as np
        D = 256
        NUM_ITERS = 3
        EPS = 1e-06
        SCALE = D ** (-0.5)

        def rmsnorm(x, w, eps=EPS):
            return x * jax.lax.rsqrt(jnp.mean(x * x, axis=-1, keepdims=True) + eps) * w

        def gru_cell(x, h, wih, whh, bih, bhh):
            gx = x @ wih.T + bih
            gh = h @ whh.T + bhh
            xr, xz, xn = jnp.split(gx, 3, axis=-1)
            hr, hz, hn = jnp.split(gh, 3, axis=-1)
            r = jax.nn.sigmoid(xr + hr)
            z = jax.nn.sigmoid(xz + hz)
            n = jnp.tanh(xn + r * hn)
            return (1.0 - z) * n + z * h
        Pn = rmsnorm(P, input_norm_w)
        k_proj = Pn @ Wk.T
        v_proj = Pn @ Wv.T
        for _ in range(NUM_ITERS):
            sn = rmsnorm(slots, slot_norm_w)
            q_proj = sn @ Wq.T
            scores = jnp.einsum('bkd,bmd->bkm', q_proj, k_proj) * SCALE
            attn = jax.nn.softmax(scores, axis=-2)
            attn = attn / (jnp.sum(attn, axis=-1, keepdims=True) + EPS)
            updates = jnp.einsum('bkm,bmd->bkd', attn, v_proj)
            slots = gru_cell(updates, slots, gru_wih, gru_whh, gru_bih, gru_bhh)
        return slots

    def _L0_ffn_ref(x, gate_w, gate_b, sh_w1, sh_b1, sh_w2, sh_b2, ew1, eb1, ew2, eb2):
        import jax, jax.numpy as jnp
        import numpy as np
        TOP_K = 2

        def _mlp(x, w1, b1, w2, b2):
            h = jax.nn.gelu(jnp.einsum('bsd,di->bsi', x, w1) + b1)
            return jnp.einsum('bsi,id->bsd', h, w2) + b2
        E = ew1.shape[0]
        router_probs = jax.nn.softmax(jnp.einsum('bsd,de->bse', x, gate_w) + gate_b, axis=-1)
        expert_values, expert_indices = jax.lax.top_k(router_probs, k=TOP_K)
        expert_values = expert_values / (jnp.sum(expert_values, axis=-1, keepdims=True) + 1e-09)
        h = jax.nn.gelu(jnp.einsum('bsd,edi->bsei', x, ew1) + eb1)
        all_outputs = jnp.einsum('bsei,eid->bsed', h, ew2) + eb2
        one_hot = jax.nn.one_hot(expert_indices, E, dtype=x.dtype)
        weights_E = (one_hot * expert_values[..., None]).sum(axis=2)
        moe_out = jnp.einsum('bse,bsed->bsd', weights_E, all_outputs)
        return x + _mlp(x, sh_w1, sh_b1, sh_w2, sh_b2) + moe_out
    x = _layernorm(x + _L0_attn_ref(x, L0_attn_Wq, L0_attn_Wk, L0_attn_Wv, L0_attn_Wo, L0_attn_bo), axis=-1)
    x = _layernorm(x + _L0_xattn_ref(x, ctx_1024, L0_xattn_Wq, L0_xattn_Wk, L0_xattn_Wv, L0_xattn_gru_wih, L0_xattn_gru_whh, L0_xattn_gru_bih, L0_xattn_gru_bhh, L0_xattn_slot_norm_w, L0_xattn_input_norm_w), axis=-1)
    x = _layernorm(x + _L0_ffn_ref(x, L0_ffn_gate_w, L0_ffn_gate_b, L0_ffn_sh_w1, L0_ffn_sh_b1, L0_ffn_sh_w2, L0_ffn_sh_b2, L0_ffn_ew1, L0_ffn_eb1, L0_ffn_ew2, L0_ffn_eb2), axis=-1)
    return x

_drawn_inputs = setup_inputs


def setup_inputs(seed=0):
    import zlib

    import numpy as np

    out = dict(_drawn_inputs(seed))
    spreads = {'L0_xattn_gru_bih': (0.0, 0.1),
     'L0_xattn_gru_bhh': (0.0, 0.1),
     'L0_xattn_slot_norm_w': (1.0, 0.2),
     'L0_xattn_input_norm_w': (1.0, 0.2),
     'L0_ffn_gate_b': (0.0, 0.1),
     'L0_ffn_sh_b1': (0.0, 0.1),
     'L0_ffn_sh_b2': (0.0, 0.1),
     'L0_ffn_eb1': (0.0, 0.35),
     'L0_ffn_eb2': (0.0, 0.1)}
    factors = {'L0_attn_Wq': 7.615, 'L0_attn_Wk': 7.924}
    for name, (base, spread) in spreads.items():
        noise = np.random.default_rng([zlib.crc32(name.encode()), seed]).standard_normal(out[name].shape)
        drawn = base * np.exp(spread * noise) if base else spread * noise
        out[name] = jnp.asarray(drawn.astype(out[name].dtype))
    for name, factor in factors.items():
        out[name] = (out[name] * factor).astype(out[name].dtype)
    return out
```

```python
from contextlib import ExitStack

import concourse.bass as bass
from concourse import mybir

F32 = mybir.dt.float32
F16 = mybir.dt.float16
BF16 = mybir.dt.bfloat16
U32 = mybir.dt.uint32
ALU = mybir.AluOpType
ACT = mybir.ActivationFunctionType
AX = mybir.AxisListType.X
ds = bass.ds

P = 128
WS = 64.0
LN_EPS = 1e-5
RMS_EPS = 1e-6
SUM_EPS = 1e-6
TOP_EPS = 1e-9


class Stage:

    def __init__(self, nc, ctx, name, steps=("done",), unit=1, ahead=1):
        self.sem = ctx.enter_context(nc.semaphore(name))
        self.steps, self.unit, self.ahead = list(steps), unit, ahead
        nc.gpsimd.sem_inc(self.sem, unit * len(self.steps) * ahead)

    def did(self, step, instruction):
        assert step in self.steps
        instruction.then_inc(self.sem, self.unit)

    def at(self, item, step=None):
        i = len(self.steps) - 1 if step is None else self.steps.index(step)
        return item * (self.unit * len(self.steps)) + self.unit * (len(self.steps) * self.ahead + i + 1)


def need(engine, stage, item, step=None):
    value = stage.at(item, step)
    if isinstance(value, int) and value <= 0:
        return
    engine.wait_ge(stage.sem, value)


def settle(engine, spare):
    engine.sem_inc(spare, 1)


def three_passes(pe, out, pairs, **kw):
    products = [(w[i], a[j]) for w, a in pairs for i, j in ((0, 0), (0, 1), (1, 0))]
    for n, (w, a) in enumerate(products):
        last = pe.matmul(out, w, a, start=n == 0, stop=n == len(products) - 1, **kw)
    return last


def decoder_layer(nc, a, out):
    PE, SC, VE, PO, SY = nc.tensor, nc.scalar, nc.vector, nc.gpsimd, nc.sync
    NB, S, D = a["x"].shape
    M = a["ctx_1024"].shape[1]
    INNER = a["L0_attn_Wq"].shape[1]
    HD = 64
    E, _, I = a["L0_ffn_ew1"].shape
    T = NB * S
    NT, DC, IC = T // P, D // P, I // P
    PAIRS = INNER // P
    G3 = 3 * D
    GT = 512
    NG = T // GT
    BG = GT // S
    ITERS = 3
    TG = GT // P
    SCALE = float(HD) ** -0.5
    XSCALE = float(D) ** -0.5
    top = ExitStack()
    with top:
        def sb(ctx, name, shape, dt=F32):
            return ctx.enter_context(nc.sbuf_tensor(name, shape, dt))

        ps = top.enter_context(nc.psum_tensor("ps", [P, 8, 512], F32))

        def stage(ctx, name, *steps, unit=1, ahead=1):
            return Stage(nc, ctx, name, steps or ("done",), unit, ahead)

        spare = {e: top.enter_context(nc.semaphore(f"spare_{k}")) for e, k in ((SC, "sc"), (VE, "ve"))}

        ident = sb(top, "ident", [P, P])
        ones = sb(top, "ones", [P, P])
        maskf = sb(top, "maskf", [P, P])
        mask = sb(top, "mask", [P, P], BF16)
        identb = sb(top, "identb", [P, P], BF16)
        powh = sb(top, "powh", [P, 8])
        iota = sb(top, "iota", [P, E])
        iotai = sb(top, "iotai", [P, E], mybir.dt.int32)
        xs = sb(top, "xs", [P, NT, D])
        xT = [sb(top, f"xT{i}", [P, DC, T], F16) for i in range(2)]
        slots = sb(top, "slots", [P, DC, T])

        const = stage(top, "const", "ident0", "mask0", "ones", "ident", "mask", "powh", "iota")
        constv = stage(top, "constv", "mask", "identb", "iota")
        nc.all_engine_barrier()
        const.did("ident0", PO.memset(ident[:, :], 0.0))
        const.did("mask0", PO.memset(maskf[:, :], 0.0))
        const.did("ones", PO.memset(ones[:, :], 1.0))
        need(PO, const, 0, "ones")
        const.did("ident", PO.affine_select(out=ident[:, :], in_=ident[:, :], compare_op=ALU.not_equal, fill=1.0,
                                            base=0, pattern=[[-1, P]], channel_multiplier=1))
        const.did("mask", PO.affine_select(out=maskf[:, :], in_=maskf[:, :], compare_op=ALU.is_ge,
                                           fill=-1e9 / SCALE, base=0, pattern=[[-1, P]], channel_multiplier=1))
        const.did("powh", PO.memset(powh[:, :], -0.5))
        const.did("iota", PO.iota(iotai[:, :], pattern=[[1, E]], base=0, channel_multiplier=0))
        need(VE, const, 0)
        constv.did("mask", VE.tensor_copy(mask[:, :], maskf[:, :]))
        constv.did("identb", VE.tensor_copy(identb[:, :], ident[:, :]))
        constv.did("iota", VE.tensor_copy(iota[:, :], iotai[:, :]))

        def cut(v, hi, lo, src, chain, names, scale=WS):
            chain.did(names[0], v.tensor_scalar(hi, src, scale, None, ALU.mult))
            return chain, names[1], (lambda: v.scalar_tensor_tensor(lo, src, scale, hi, ALU.mult, ALU.subtract))

        with ExitStack() as c:
            wqkv = [sb(c, f"wqkv{i}", [P, DC, 3, INNER], F16) for i in range(2)]
            wo = [sb(c, f"wo{i}", [P, PAIRS, D], F16) for i in range(2)]
            wst = [sb(c, f"wst{i}", [P, DC, INNER]) for i in range(2)]
            xin = [sb(c, f"xin{i}", [P, S // P, D]) for i in range(2)]
            bo = sb(c, "bo", [P, D])
            qpad = sb(c, "qpad", [P, 2, S])
            kT = sb(c, "kT", [P, S])
            v_sb = [sb(c, f"v{i}", [P, S // P, P]) for i in range(2)]
            prob = sb(c, "prob", [P, 2, 384])
            pT = sb(c, "pT", [P, 2, 384])
            oT = [sb(c, f"oT{i}", [P, PAIRS, S], F16) for i in range(2)]
            mx = sb(c, "mx", [P, 2, 2])
            nmx = sb(c, "nmx", [P, 2, 2])
            den = sb(c, "den", [P, 2, 2])
            rden = sb(c, "rden", [P, 2, 2])
            bst = sb(c, "bst", [P, 2, 6])
            mv = sb(c, "mv", [P, 2, 2])
            ve = sb(c, "ve", [P, 2])
            rstd = sb(c, "rstd", [P, 2])

            ld_w = [stage(c, f"ld_w{i}", unit=16) for i in range(2)]
            ld_x = [stage(c, f"ld_x{i}", unit=16) for i in range(2)]
            ld_xs = stage(c, "ld_xs", unit=16)
            ld_bo = stage(c, "ld_bo", unit=16)
            w_cut = stage(c, "w_cut", "hi", "lo")
            x_tr = stage(c, "x_tr", ahead=2)
            x_hi = stage(c, "x_hi", ahead=2)
            x_lo = stage(c, "x_lo", ahead=2)
            bo_add = stage(c, "bo_add")
            zero = stage(c, "zero", "qpad", "oT_hi", "oT_lo")
            nc.all_engine_barrier()

            SY.dma_start(xs[:, :, :], a["x"].rearrange("b (t p) d -> p (b t) d", p=P)).then_inc(ld_xs.sem, 16)
            bo_row = a["L0_attn_bo"].rearrange("(o d) -> o d", o=1)
            SY.dma_start(bo[:, :], bo_row.broadcast_to((P, D))).then_inc(ld_bo.sem, 16)
            zero.did("qpad", VE.memset(qpad[:, :, :], 0.0))
            srcs = [a[f"L0_attn_W{k}"].rearrange("(c p) n -> p c n", p=P) for k in "qkv"]
            srcs.append(a["L0_attn_Wo"].rearrange("(s p) n -> p s n", p=P))
            for n, src in enumerate(srcs):
                need(SC, w_cut, n - 2)
                st = wst[n % 2]
                dst = st[:, :, :] if n < 3 else st[:, :, :].rearrange("p c n -> p (c n)").rearrange(
                    "p (s n) -> p s n", s=PAIRS)
                SC.dma_start(dst, src).then_inc(ld_w[n % 2].sem, 16)
            for n in range(4):
                need(VE, ld_w[n % 2], n // 2)
                st = wst[n % 2]
                if n < 3:
                    hi, lo, src = wqkv[0][:, :, n, :], wqkv[1][:, :, n, :], st[:, :, :]
                else:
                    src = st[:, :, :].rearrange("p c n -> p (c n)")
                    hi, lo = (w[:, :, :].rearrange("p s n -> p (s n)") for w in wo)
                w_cut.did("hi", VE.tensor_scalar(hi, src, WS, None, ALU.mult))
                need(VE, w_cut, n, "hi")
                w_cut.did("lo", VE.scalar_tensor_tensor(lo, src, WS, hi, ALU.mult, ALU.subtract))
            need(PO, ld_xs, 0)
            need(PO, ld_bo, 0)
            bo_add.did("done", PO.tensor_tensor(
                xs[:, :, :], xs[:, :, :], bo[:, :].unsqueeze(1).broadcast_to((P, NT, D)), ALU.add))

            need(PE, const, 0, "ident")
            xv = a["x"].rearrange("b (t p) d -> b p t d", p=P)
            with nc.Fori(0, NB // 2) as i:
                for u in range(2):
                    b = i * 2 + u
                    need(SY, x_tr, b - 2)
                    SY.dma_start(xin[u][:, :, :], xv[b]).then_inc(ld_x[u].sem, 16)
                    need(PE, ld_x[u], i)
                    need(PE, x_lo, b - 2)
                    need(PE, x_hi, b - 2)
                    for ch in range(DC):
                        for t in range(S // P):
                            tr = PE.transpose(ps[:, u, ch * S + t * P:ch * S + t * P + P],
                                              xin[u][:, t, ch * P:ch * P + P], ident[:, :])
                    x_tr.did("done", tr)
                    pv = ps[:, u, :].rearrange("p (c t) -> p c t", c=DC)
                    need(SC, x_tr, b)
                    x_hi.did("done", SC.copy(xT[0][:, :, ds(b * S, S)], pv))
                    need(VE, x_hi, b)
                    x_lo.did("done", VE.tensor_tensor(xT[1][:, :, ds(b * S, S)], pv,
                                                      xT[0][:, :, ds(b * S, S)], ALU.subtract))

            qk_mm = stage(c, "qk_mm")
            v_mm = stage(c, "v_mm")
            s_mm = stage(c, "s_mm")
            pt_mm = stage(c, "pt_mm")
            o_mm = stage(c, "o_mm")
            y_mm = stage(c, "y_mm")
            qkv_ev = stage(c, "qkv_ev", "k", "q0", "q1", "v")
            smax = stage(c, "smax", "q0", "q1", "neg")
            expo = stage(c, "expo", "h0q0", "h0q1", "h1q0", "h1q1")
            norm = stage(c, "norm", "recip", "h0q0", "h0q1", "h1q0", "h1q1")
            pt_ev = stage(c, "pt_ev")
            o_ev = stage(c, "o_ev", "hi", "lo")
            ln = stage(c, "ln", "add", "st0", "st1", "ag0", "ag1", "eps", "out0", "out1")
            ln_pow = stage(c, "ln_pow")
            nc.all_engine_barrier()

            def project(n, b, p):
                need(PE, qkv_ev, n - 1)
                cols = ds(p * P, P)
                for k in range(2):
                    w = [[wqkv[h][:, ch, k, cols] for h in range(2)] for ch in range(DC)]
                    x = [[xT[h][:, ch, ds(b * S, S)] for h in range(2)] for ch in range(DC)]
                    mm = three_passes(PE, ps[:, 0, k * S:(k + 1) * S], list(zip(w, x)))
                qk_mm.did("done", mm)
                for t in range(S // P):
                    x = [[xT[h][:, ch, ds(b * S + t * P, P)] for h in range(2)] for ch in range(DC)]
                    w = [[wqkv[h][:, ch, 2, cols] for h in range(2)] for ch in range(DC)]
                    mm = three_passes(PE, ps[:, 1, t * P:(t + 1) * P], list(zip(x, w)))
                v_mm.did("done", mm)

            def evacuate_project(n, u):
                need(SC, qk_mm, n)
                need(SC, s_mm, n - 1)
                qkv_ev.did("k", SC.mul(kT[:, :], ps[:, 0, S:2 * S], 1 / WS))
                for h in range(2):
                    r = slice(HD * h, HD * h + HD)
                    qkv_ev.did(f"q{h}", SC.mul(qpad[r, h, :], ps[r, 0, 0:S], 1 / WS))
                need(SC, v_mm, n)
                need(SC, o_mm, n - 2)
                qkv_ev.did("v", SC.mul(v_sb[u][:, :, :], ps[:, 1, 0:S].rearrange("p (t n) -> p t n", n=P), 1 / WS))

            def scores(m):
                need(PE, qkv_ev, m, "q1")
                need(PE, expo, m - 1)
                for h in range(2):
                    for t in range(2):
                        o = ps[:, 2 + h, 0:P] if t == 0 else ps[:, 2 + h, P:3 * P]
                        PE.matmul(o, qpad[:, h, t * P:t * P + P], kT[:, 0:(t + 1) * P], start=True, stop=False)
                        mm = PE.matmul(ps[:, 2 + h, 2 * P * t:2 * P * t + P], identb[:, :], mask[:, :],
                                       start=False, stop=True)
                s_mm.did("done", mm)

            sv = ps[:, 2:4, :]

            def softmax(m):
                need(VE, s_mm, m)
                need(VE, expo, m - 1)
                smax.did("q0", VE.tensor_reduce(mx[:, :, 0:1], sv[:, :, 0:P], AX, ALU.max))
                smax.did("q1", VE.tensor_reduce(mx[:, :, 1:2], sv[:, :, P:3 * P], AX, ALU.max))
                need(VE, smax, m, "q1")
                smax.did("neg", VE.tensor_scalar(nmx[:, :, :], mx[:, :, :], -SCALE, None, ALU.mult))
                need(SC, smax, m)
                need(SC, pt_mm, m - 1)
                need(SC, norm, m - 1)
                for h in range(2):
                    for t in range(2):
                        r = slice(0, P) if t == 0 else slice(P, 3 * P)
                        expo.did(f"h{h}q{t}", SC.activation(prob[:, h, r], sv[:, h, r], ACT.Exp,
                                                            bias=nmx[:, h, t:t + 1], scale=SCALE,
                                                            accum_out=den[:, h, t:t + 1]))

            def normalise(m):
                need(VE, expo, m)
                norm.did("recip", VE.reciprocal(rden[:, :, :], den[:, :, :]))
                need(VE, norm, m, "recip")
                for h in range(2):
                    for t in range(2):
                        r = slice(0, P) if t == 0 else slice(P, 3 * P)
                        norm.did(f"h{h}q{t}", VE.tensor_scalar(prob[:, h, r], prob[:, h, r], rden[:, h, t:t + 1],
                                                               None, ALU.mult))

            def transpose_prob(m):
                need(PE, norm, m)
                need(PE, pt_ev, m - 1)
                for h in range(2):
                    for blk in range(3):
                        mm = PE.transpose(ps[:, 4 + h, blk * P:blk * P + P], prob[:, h, blk * P:blk * P + P],
                                          ident[:, :])
                pt_mm.did("done", mm)
                need(VE, pt_mm, m)
                need(VE, o_mm, m - 1)
                pt_ev.did("done", VE.tensor_copy(pT[:, :, :], ps[:, 4:6, 0:384]))

            def weigh_values(m, u, slot, batch):
                need(PE, pt_ev, m)
                need(PE, qkv_ev, m)
                need(PE, o_ev, m - 1)
                for t in range(2):
                    for h in range(2):
                        r = slice(HD * h, HD * h + HD)
                        mm = PE.matmul(ps[r, 7, t * P:S], v_sb[u][:, t, r],
                                       pT[:, h, 256 * t:256 + P * t], start=t == 0, stop=t == 1,
                                       skip_group_check=True)
                o_mm.did("done", mm)
                need(VE, o_mm, m)
                need(VE, y_mm, batch - 1)
                hi, lo = (o[:, ds(slot, 1), :].squeeze(1) if not isinstance(slot, int) else o[:, slot, :] for o in oT)
                o_ev.did("hi", VE.tensor_copy(hi, ps[:, 7, 0:S]))
                need(VE, o_ev, m, "hi")
                o_ev.did("lo", VE.tensor_tensor(lo, ps[:, 7, 0:S], hi, ALU.subtract))

            def output_projection(b, last_item):
                need(PE, o_ev, last_item)
                need(PE, ln, b - 1, "add")
                for t in range(2):
                    o = [[oT[h][:, s, t * P:t * P + P] for h in range(2)] for s in range(PAIRS)]
                    w = [[wo[h][:, s, :] for h in range(2)] for s in range(PAIRS)]
                    mm = three_passes(PE, ps[:, 6, t * D:t * D + D], list(zip(o, w)))
                y_mm.did("done", mm)
                need(VE, y_mm, b)
                y = xs[:, ds(b * 2, 2), :] if not isinstance(b, int) else xs[:, 2 * b:2 * b + 2, :]
                tile = [xs[:, b * 2 + t, :] for t in range(2)]
                need(VE, ln, b - 1)
                need(VE, ln_pow, b - 1)
                ln.did("add", VE.scalar_tensor_tensor(y, ps[:, 6, :].rearrange("p (t n) -> p t n", n=D), 1 / WS, y,
                                                      ALU.mult, ALU.add))
                need(VE, ln, b, "add")
                settle(VE, spare[VE])
                for t in range(2):
                    ln.did(f"st{t}", VE.bn_stats(bst[:, t, :], tile[t]))
                need(VE, ln, b, "st1")
                settle(VE, spare[VE])
                for t in range(2):
                    ln.did(f"ag{t}", VE.bn_aggr(mv[:, t, :], bst[:, t, :]))
                need(VE, ln, b, "ag1")
                ln.did("eps", VE.tensor_scalar(ve[:, :].unsqueeze(2), mv[:, :, 1:2], LN_EPS, None, ALU.add))
                need(PO, ln, b, "eps")
                ln_pow.did("done", PO.tensor_tensor(rstd[:, :], ve[:, :], powh[:, 0:2], ALU.pow))
                need(VE, ln_pow, b)
                for t in range(2):
                    ln.did(f"out{t}", VE.tensor_scalar(tile[t], tile[t], mv[:, t, 0:1], rstd[:, t:t + 1],
                                                       ALU.subtract, ALU.mult))

            def step(n, u, b, p, qkv=True, mid=True, pv=True, pv_slot=None, pv_batch=None):
                if mid:
                    scores(n - 1)
                    softmax(n - 1)
                if pv:
                    weigh_values(n - 2, u, pv_slot, pv_batch)
                if qkv:
                    project(n, b, p)
                    evacuate_project(n, u)
                if mid:
                    normalise(n - 1)
                    transpose_prob(n - 1)

            need(PE, w_cut, 3)
            need(PE, constv, 0)
            need(PE, zero, 0, "qpad")
            need(VE, bo_add, 0)
            need(PE, x_lo, NB - 1)

            def inner(b):
                with nc.Fori(1, PAIRS // 2) as k:
                    for u in range(2):
                        step(b * PAIRS + k * 2 + u, u, b, k * 2 + u, pv_slot=k * 2 + (u - 2), pv_batch=b)

            step(0, 0, 0, 0, mid=False, pv=False)
            step(1, 1, 0, 1, pv=False)
            inner(0)
            with nc.Fori(1, NB) as b:
                for u in range(2):
                    step(b * PAIRS + u, u, b, u, pv_slot=PAIRS - 2 + u, pv_batch=b - 1)
                output_projection(b - 1, b * PAIRS - 1)
                inner(b)
            N = NB * PAIRS
            step(N, 0, None, None, qkv=False, pv_slot=PAIRS - 2, pv_batch=NB - 1)
            step(N + 1, 1, None, None, qkv=False, mid=False, pv_slot=PAIRS - 1, pv_batch=NB - 1)
            output_projection(NB - 1, N - 1)
            nc.all_engine_barrier()

        with ExitStack() as c:
            whh = [sb(c, f"whh{i}", [P, DC, G3], F16) for i in range(2)]
            vw = [sb(c, f"vw{i}", [P, NB, G3], F16) for i in range(2)]
            kq = [sb(c, f"kq{i}", [P, DC, NB * M], F16) for i in range(2)]
            b_tz = sb(c, "b_tz", [P, 6])
            bih = sb(c, "bih", [P, 6])
            bhh = sb(c, "bhh", [P, 6])
            with ExitStack() as q:
                wk, wq, wv = (sb(q, f"x_{k}", [P, DC, D]) for k in ("wk", "wq", "wv"))
                wn = [sb(q, f"gw{i}", [P, G3 // P, D]) for i in range(2)]
                wihT = sb(q, "wihT", [P, DC, G3])
                whhT = sb(q, "whhT", [P, DC, G3])
                wa = sb(q, "wa", [P, DC, D])
                wb = sb(q, "wb", [P, DC, G3])
                ctxt = sb(q, "ctxt", [P, NB, D])
                pnT = sb(q, "pnT", [P, DC, NB * M])
                kqf = sb(q, "kqf", [P, NB * M])
                vwf = sb(q, "vwf", [P, G3])
                sqc = sb(q, "sqc", [P, D])
                ssc = sb(q, "ssc", [P, NB])
                rc = sb(q, "rc", [P, NB])
                nw = sb(q, "nw", [P, 2, DC])
                snw = sb(q, "snw", [P, DC])
                ld = stage(q, "x_ld", unit=16)
                line = stage(q, "x_line")
                nc.all_engine_barrier()
                loads = [
                    (wk[:, :, :], a["L0_xattn_Wk"].rearrange("(c p) n -> p c n", p=P)),
                    (wq[:, :, :], a["L0_xattn_Wq"].rearrange("(c p) n -> p c n", p=P)),
                    (wv[:, :, :], a["L0_xattn_Wv"].rearrange("(c p) n -> p c n", p=P)),
                    (wn[0][:, :, :], a["L0_xattn_gru_wih"].rearrange("(c p) n -> p c n", p=P)),
                    (wn[1][:, :, :], a["L0_xattn_gru_whh"].rearrange("(c p) n -> p c n", p=P)),
                    (ctxt[0:M, :, :], a["ctx_1024"].rearrange("b m d -> m b d")),
                    (bih[:, :], a["L0_xattn_gru_bih"].rearrange("(c p) -> p c", p=P)),
                    (bhh[:, :], a["L0_xattn_gru_bhh"].rearrange("(c p) -> p c", p=P)),
                    (nw[:, 0, :], a["L0_xattn_input_norm_w"].rearrange("(c p) -> p c", p=P)),
                    (nw[:, 1, :], a["L0_xattn_slot_norm_w"].rearrange("(c p) -> p c", p=P)),
                ]
                for n, (dst, src) in enumerate(loads):
                    SY.dma_start(dst, src, allow_slow_non_contiguous=n >= 6).then_inc(ld.sem, 16)
                for eng in (PE, SC, VE):
                    need(eng, ld, len(loads) - 1)
                count = [0]

                def after(engine):
                    need(engine, line, count[0] - 1)

                def made(ins):
                    line.did("done", ins)
                    count[0] += 1

                def run(engine, make):
                    after(engine)
                    made(make())

                run(VE, lambda: VE.tensor_tensor(b_tz[:, :], bih[:, :], bhh[:, :], ALU.add))
                run(VE, lambda: VE.tensor_scalar(b_tz[:, :], b_tz[:, :], 0.5, None, ALU.mult))
                run(VE, lambda: VE.tensor_scalar(bhh[:, :], bhh[:, :], 0.5, None, ALU.mult))
                run(VE, lambda: VE.tensor_scalar(snw[:, :], nw[:, 1, :], XSCALE * WS, None, ALU.mult))
                for b in range(NB):
                    run(SC, lambda: SC.activation(sqc[0:M, :], ctxt[0:M, b, :], ACT.Square,
                                                  accum_out=ssc[0:M, b:b + 1]))
                run(VE, lambda: VE.tensor_scalar(ssc[0:M, :], ssc[0:M, :], 1.0 / D, RMS_EPS, ALU.mult, ALU.add))
                run(PO, lambda: PO.tensor_tensor(rc[0:M, :], ssc[0:M, :], powh[0:M, 0:NB], ALU.pow))
                run(VE, lambda: VE.tensor_tensor(ctxt[0:M, :, :], ctxt[0:M, :, :],
                                                 rc[0:M, :].unsqueeze(2).broadcast_to((M, NB, D)), ALU.mult))
                for ch in range(DC):
                    after(PE)
                    for b in range(NB):
                        tr = PE.transpose(ps[:, b // 4, (b % 4) * M:(b % 4) * M + M],
                                          ctxt[0:M, b, ch * P:ch * P + P], ident[0:M, 0:M])
                    made(tr)
                    run(VE, lambda: VE.tensor_scalar(
                        pnT[:, ch, :].rearrange("p (k m) -> p k m", k=2), ps[:, 0:2, 0:4 * M], nw[:, 0, ch:ch + 1],
                        None, ALU.mult))
                    for w, wt in ((wn[0], wihT), (wn[1], whhT)):
                        after(PE)
                        for g in range(G3 // P):
                            tr = PE.transpose(ps[:, g // 3, (g % 3) * P:(g % 3) * P + P],
                                              w[:, g, ch * P:ch * P + P], ident[:, :])
                        made(tr)
                        run(VE, lambda: VE.tensor_copy(wt[:, ch, :].rearrange("p (k m) -> p k m", k=2),
                                                       ps[:, 0:2, 0:3 * P]))
                run(VE, lambda: VE.tensor_scalar(whh[0][:, :, :], whhT[:, :, :], WS, None, ALU.mult))
                run(VE, lambda: VE.scalar_tensor_tensor(whh[1][:, :, :], whhT[:, :, :], WS, whh[0][:, :, :],
                                                        ALU.mult, ALU.subtract))
                for e in range(DC):
                    after(PE)
                    for f in range(DC):
                        PE.matmul(ps[:, 0, 0:D], wk[:, f, e * P:e * P + P], wq[:, f, :], start=f == 0,
                                  stop=f == DC - 1)
                    for k in range(2):
                        for f in range(DC):
                            mm = PE.matmul(ps[:, 1 + k, 0:3 * P], wv[:, f, e * P:e * P + P],
                                           wihT[:, f, k * 3 * P:(k + 1) * 3 * P], start=f == 0, stop=f == DC - 1)
                    made(mm)
                    run(VE, lambda: VE.tensor_copy(wa[:, e, :], ps[:, 0, 0:D]))
                    run(VE, lambda: VE.tensor_copy(wb[:, e, :].rearrange("p (k m) -> p k m", k=2),
                                                   ps[:, 1:3, 0:3 * P]))
                half = NB * M // 2
                for d in range(DC):
                    after(PE)
                    for k in range(2):
                        for e in range(DC):
                            mm = PE.matmul(ps[:, k, 0:half], wa[:, e, d * P:d * P + P],
                                           pnT[:, e, k * half:(k + 1) * half], start=e == 0, stop=e == DC - 1)
                    made(mm)
                    run(VE, lambda: VE.tensor_scalar(kqf[:, :].rearrange("p (k m) -> p k m", k=2), ps[:, 0:2, 0:half],
                                                     snw[:, d:d + 1], None, ALU.mult))
                    run(VE, lambda: VE.tensor_copy(kq[0][:, d, :], kqf[:, :]))
                    run(VE, lambda: VE.tensor_tensor(kq[1][:, d, :], kqf[:, :], kq[0][:, d, :], ALU.subtract))
                for b in range(NB):
                    after(PE)
                    for k in range(2):
                        for e in range(DC):
                            mm = PE.matmul(ps[0:M, k, 0:3 * P], pnT[:, e, b * M:(b + 1) * M],
                                           wb[:, e, k * 3 * P:(k + 1) * 3 * P], start=e == 0, stop=e == DC - 1)
                    made(mm)
                    run(VE, lambda: VE.tensor_scalar(vwf[0:M, :].rearrange("p (k m) -> p k m", k=2),
                                                     ps[0:M, 0:2, 0:3 * P], WS, None, ALU.mult))
                    run(VE, lambda: VE.tensor_copy(vw[0][0:M, b, :], vwf[0:M, :]))
                    run(VE, lambda: VE.tensor_tensor(vw[1][0:M, b, :], vwf[0:M, :], vw[0][0:M, b, :], ALU.subtract))
                for t in range(NT):
                    after(PE)
                    for ch in range(DC):
                        tr = PE.transpose(ps[:, 0, ch * P:ch * P + P], xs[:, t, ch * P:ch * P + P], ident[:, :])
                    made(tr)
                    run(VE, lambda: VE.tensor_copy(slots[:, :, t * P:t * P + P],
                                                   ps[:, 0, 0:2 * P].rearrange("p (c t) -> p c t", c=DC)))
                nc.all_engine_barrier()

            sh = [[sb(c, f"s{i}{u}", [P, DC, GT], F16) for i in range(2)] for u in range(2)]
            sq = sb(c, "sq", [P, DC, GT])
            diag = sb(c, "diag", [P, TG, P])
            rr = sb(c, "rr", [P, GT])
            sc = sb(c, "sc", [P, BG, S])
            ex = sb(c, "ex", [P, BG, S])
            an = sb(c, "an", [P, GT])
            anh = [[sb(c, f"an{i}{u}", [P, GT], F16) for i in range(2)] for u in range(2)]
            msq = sb(c, "msq", [P, TG])
            rms = sb(c, "rms", [P, TG])
            gmx = sb(c, "gmx", [P, BG])
            gneg = sb(c, "gneg", [P, BG])
            gden = sb(c, "gden", [P, BG])
            grec = sb(c, "grec", [P, BG])
            cse = sb(c, "cse", [P, TG])
            crec = sb(c, "crec", [P, TG])
            tr_, tz, hn, t1, t2, nn, dl, uu = (sb(c, k, [P, GT]) for k in
                                               ("tr_", "tz", "hn", "t1", "t2", "nn", "dl", "uu"))
            A_sc = stage(c, "A_sc", "hi", "sq", "rr", "e0", "e1", "rr2", "anh")
            A_ve = stage(c, "A_ve", "lo", "msq", "diag", "sc", "mx", "neg", "grec", "m0", "m1", "cse", "crec",
                         "diag2", "an", "anl")
            A_po = stage(c, "A_po", "pow")
            A_pe = stage(c, "A_pe", "ss", "rb", "sc", "cs", "rb2")
            G_pe = stage(c, "G_pe", "r", "z", "hn", "xn", ahead=3)
            G_sc = stage(c, "G_sc", "tr", "tz", "hn", "nn")
            G_ve = stage(c, "G_ve", "t1", "t2", "u", "out", ahead=2 * NG)
            G_po = stage(c, "G_po", "dl")
            nc.all_engine_barrier()

            def cols(g):
                return ds(g * GT, GT)

            def attend(n, u, g, written):
                hi, lo = sh[u]
                src = slots[:, :, cols(g)]
                need(SC, G_ve, written)
                need(SC, G_pe, 2 * n - 3)
                A_sc.did("hi", SC.copy(hi[:, :, :], src))
                need(SC, A_pe, n - 1, "ss")
                settle(SC, spare[SC])
                A_sc.did("sq", SC.activation(sq[:, :, :], src, ACT.Square))
                need(VE, A_sc, n, "hi")
                A_ve.did("lo", VE.tensor_tensor(lo[:, :, :], src, hi[:, :, :], ALU.subtract))
                yield
                need(PE, A_sc, n, "sq")
                need(PE, A_sc, n - 1, "rr2")
                for t in range(TG):
                    for ch in range(DC):
                        mm = PE.matmul(ps[:, 4, t * P:t * P + P], sq[:, ch, t * P:t * P + P], ones[:, :],
                                       start=ch == 0, stop=ch == DC - 1)
                A_pe.did("ss", mm)
                need(VE, A_pe, n, "ss")
                need(VE, A_po, n - 1)
                A_ve.did("msq", VE.tensor_scalar(
                    msq[:, :].unsqueeze(2), ps[:, 4, :].rearrange("p (t n) -> p t n", n=P)[:, :, 0:1], 1.0 / D,
                    RMS_EPS, ALU.mult, ALU.add))
                need(PO, A_ve, n, "msq")
                need(PO, A_ve, n - 1, "diag")
                A_po.did("pow", PO.tensor_tensor(rms[:, :], msq[:, :], powh[:, 0:TG], ALU.pow))
                need(VE, A_po, n)
                need(VE, A_pe, n - 1, "rb2")
                A_ve.did("diag", VE.tensor_tensor(
                    diag[:, :, :], ident[:, :].unsqueeze(1).broadcast_to((P, TG, P)),
                    rms[:, :].unsqueeze(2).broadcast_to((P, TG, P)), ALU.mult))
                yield
                need(PE, A_ve, n, "diag")
                A_pe.did("rb", PE.matmul(ps[:, 5, :], ones[:, :], diag[:, :, :].rearrange("p t n -> p (t n)"),
                                         start=True, stop=True))
                need(PE, A_ve, n, "lo")
                need(PE, A_ve, n - 1, "sc")
                for k in range(BG):
                    m = ds((g * BG + k) * M, M)
                    w = [[kq[h][:, ch, m] for h in range(2)] for ch in range(DC)]
                    x = [[sh[u][h][:, ch, k * S:(k + 1) * S] for h in range(2)] for ch in range(DC)]
                    mm = three_passes(PE, ps[0:M, 6, k * S:(k + 1) * S], list(zip(w, x)))
                A_pe.did("sc", mm)
                need(SC, A_pe, n, "rb")
                need(SC, A_ve, n - 1, "an")
                A_sc.did("rr", SC.copy(rr[:, :], ps[:, 5, :]))
                need(VE, A_sc, n, "rr")
                need(VE, A_pe, n, "sc")
                need(VE, A_sc, n - 1, "e1")
                A_ve.did("sc", VE.scalar_tensor_tensor(sc[0:M, :, :].rearrange("p b n -> p (b n)"), ps[0:M, 6, :],
                                                       1 / WS, rr[0:M, :], ALU.mult, ALU.mult))
                need(VE, A_ve, n, "sc")
                A_ve.did("mx", VE.tensor_reduce(gmx[0:M, :], sc[0:M, :, :], AX, ALU.max))
                need(VE, A_ve, n, "mx")
                A_ve.did("neg", VE.tensor_scalar(gneg[0:M, :], gmx[0:M, :], -1.0, None, ALU.mult))
                need(SC, A_ve, n, "neg")
                need(SC, A_pe, n - 1, "cs")
                need(SC, A_ve, n - 1, "an")
                for k in range(BG):
                    A_sc.did(f"e{k}", SC.activation(ex[0:M, k, :], sc[0:M, k, :], ACT.Exp, bias=gneg[0:M, k:k + 1],
                                                    accum_out=gden[0:M, k:k + 1]))
                need(VE, A_sc, n, "e1")
                A_ve.did("grec", VE.reciprocal(grec[0:M, :], gden[0:M, :]))
                need(VE, A_ve, n, "grec")
                for k in range(BG):
                    A_ve.did(f"m{k}", VE.tensor_scalar(ex[0:M, k, :], ex[0:M, k, :], grec[0:M, k:k + 1], None,
                                                       ALU.mult))
                yield
                need(PE, A_ve, n, "m1")
                exf = ex[0:M, :, :].rearrange("p b n -> p (b n)")
                for t in range(TG):
                    mm = PE.matmul(ps[:, 4, t * P:t * P + P], exf[:, t * P:t * P + P], ones[0:M, :],
                                   start=True, stop=True)
                A_pe.did("cs", mm)
                need(VE, A_pe, n, "cs")
                A_ve.did("cse", VE.tensor_scalar(
                    cse[:, :].unsqueeze(2), ps[:, 4, :].rearrange("p (t n) -> p t n", n=P)[:, :, 0:1], SUM_EPS, None,
                    ALU.add))
                need(VE, A_ve, n, "cse")
                A_ve.did("crec", VE.reciprocal(crec[:, :], cse[:, :]))
                need(VE, A_ve, n, "crec")
                need(VE, A_pe, n, "rb")
                A_ve.did("diag2", VE.tensor_tensor(
                    diag[:, :, :], ident[:, :].unsqueeze(1).broadcast_to((P, TG, P)),
                    crec[:, :].unsqueeze(2).broadcast_to((P, TG, P)), ALU.mult))
                yield
                need(PE, A_ve, n, "diag2")
                need(PE, A_sc, n, "rr")
                A_pe.did("rb2", PE.matmul(ps[:, 5, :], ones[:, :], diag[:, :, :].rearrange("p t n -> p (t n)"),
                                          start=True, stop=True))
                need(SC, A_pe, n, "rb2")
                need(SC, A_ve, n, "sc")
                A_sc.did("rr2", SC.copy(rr[:, :], ps[:, 5, :]))
                need(VE, A_sc, n, "rr2")
                need(VE, A_sc, n - 1, "anh")
                A_ve.did("an", VE.tensor_tensor(an[0:M, :], exf, rr[0:M, :], ALU.mult))
                need(SC, A_ve, n, "an")
                need(SC, G_pe, 2 * n - 3)
                A_sc.did("anh", SC.copy(anh[u][0][0:M, :], an[0:M, :]))
                need(VE, A_sc, n, "anh")
                A_ve.did("anl", VE.tensor_tensor(anh[u][1][0:M, :], an[0:M, :], anh[u][0][0:M, :], ALU.subtract))
                yield

            def gate(n, u, g, bank, chunk, hidden, update):
                jobs = []
                if hidden:
                    jobs += [(whh[i][:, ch, chunk * P:chunk * P + P], sh[u][j][:, ch, :], ps[:, bank, :])
                             for ch in range(DC) for i, j in ((0, 0), (0, 1), (1, 0))]
                if update:
                    jobs += [(vw[i][0:M, ds(g * BG + k, 1), chunk * P:chunk * P + P].squeeze(1),
                              anh[u][j][0:M, k * S:(k + 1) * S], ps[:, bank, k * S:(k + 1) * S])
                             for k in range(BG) for i, j in ((0, 0), (0, 1), (1, 0))]
                for n_, (w, x, o) in enumerate(jobs):
                    first = n_ == 0
                    mm = PE.matmul(o, w, x, start=first, stop=n_ == len(jobs) - 1, skip_group_check=True)
                return mm

            def gru(n, u, g, weave):
                for ch in range(DC):
                    m = 2 * n + ch
                    need(PE, A_ve, n, "anl")
                    need(PE, G_sc, m - 1, "tr")
                    G_pe.did("r", gate(n, u, g, 0, ch, True, True))
                    need(PE, G_sc, m - 1, "tz")
                    G_pe.did("z", gate(n, u, g, 1, DC + ch, True, True))
                    next(weave, None)
                    need(PE, G_sc, m - 1, "hn")
                    G_pe.did("hn", gate(n, u, g, 2, 2 * DC + ch, True, False))
                    need(PE, G_ve, m - 1, "t2")
                    G_pe.did("xn", gate(n, u, g, 3, 2 * DC + ch, False, True))
                    need(SC, G_pe, m, "r")
                    need(SC, G_ve, m - 1, "t1")
                    G_sc.did("tr", SC.activation(tr_[:, :], ps[:, 0, :], ACT.Tanh, bias=b_tz[:, ch:ch + 1],
                                                 scale=0.5 / WS))
                    need(SC, G_pe, m, "z")
                    need(SC, G_ve, m - 1, "u")
                    G_sc.did("tz", SC.activation(tz[:, :], ps[:, 1, :], ACT.Tanh, bias=b_tz[:, DC + ch:DC + ch + 1],
                                                 scale=0.5 / WS))
                    need(SC, G_pe, m, "hn")
                    G_sc.did("hn", SC.activation(hn[:, :], ps[:, 2, :], ACT.Identity,
                                                 bias=bhh[:, 2 * DC + ch:2 * DC + ch + 1], scale=0.5 / WS))
                    need(VE, G_sc, m, "hn")
                    G_ve.did("t1", VE.scalar_tensor_tensor(t1[:, :], tr_[:, :], 1.0, hn[:, :], ALU.add, ALU.mult))
                    need(VE, G_pe, m, "xn")
                    need(VE, G_ve, m, "t1")
                    need(VE, G_sc, m - 1, "nn")
                    G_ve.did("t2", VE.scalar_tensor_tensor(t2[:, :], ps[:, 3, :], 1 / WS, t1[:, :], ALU.mult, ALU.add))
                    need(SC, G_ve, m, "t2")
                    need(SC, G_ve, m - 1, "out")
                    G_sc.did("nn", SC.activation(nn[:, :], t2[:, :], ACT.Tanh,
                                                 bias=bih[:, 2 * DC + ch:2 * DC + ch + 1]))
                    h = slots[:, ch, cols(g)]
                    need(PO, G_sc, m, "nn")
                    need(PO, G_ve, m - 1, "u")
                    G_po.did("dl", PO.tensor_tensor(dl[:, :], h, nn[:, :], ALU.subtract))
                    need(VE, G_po, m)
                    G_ve.did("u", VE.scalar_tensor_tensor(uu[:, :], tz[:, :], 1.0, dl[:, :], ALU.add, ALU.mult))
                    need(VE, G_ve, m, "u")
                    G_ve.did("out", VE.scalar_tensor_tensor(h, uu[:, :], 0.5, nn[:, :], ALU.mult, ALU.add))
                    next(weave, None)
                for _ in weave:
                    pass

            for _ in attend(0, 0, 0, -1):
                pass
            NSTEP = ITERS * NG

            def pair(n, g0, nxt, last=False):
                gru(n, 0, g0, attend(n + 1, 1, g0 + 1, 2 * (n + 1 - NG) + 1))
                gru(n + 1, 1, g0 + 1, iter(()) if last else attend(n + 2, 0, nxt, 2 * (n + 2 - NG) + 1))

            with nc.Fori(0, ITERS - 1) as it:
                with nc.Fori(0, NG // 2) as k:
                    pair(it * NG + k * 2, k * 2, 2 + k * -2)
            base = (ITERS - 1) * NG
            pair(base, 0, 2)
            pair(base + 2, 2, 0, last=True)
            nc.all_engine_barrier()

        wE = sb(top, "wE", [P, NT, E + 1])
        with ExitStack() as c:
            gw = sb(c, "gw", [P, DC, E])
            gwh = [sb(c, f"gw_{i}", [P, DC, E], F16) for i in range(2)]
            gb = sb(c, "gb", [P, E])
            stg = sb(c, "stg", [P, DC, GT])
            y = sb(c, "y", [P, TG, D])
            st = sb(c, "st", [P, TG, 6])
            mv2 = sb(c, "mv2", [P, TG, 2])
            ve2 = sb(c, "ve2", [P, TG])
            rs2 = sb(c, "rs2", [P, TG])
            lg, pe_, pr, mx8, fi, eq, w0, w1 = (sb(c, k, [P, TG, E]) for k in
                                                ("lg", "pe_", "pr", "mx8", "fi", "eq", "w0", "w1"))
            ix8 = sb(c, "ix8", [P, TG, E], U32)
            s1, s2 = (sb(c, k, [P, TG]) for k in ("s1", "s2"))
            ld = stage(c, "r_ld", unit=16)
            gcut = stage(c, "gcut", "hi", "lo", "one")
            line = stage(c, "r_line")
            nc.all_engine_barrier()
            SY.dma_start(gw[:, :, :], a["L0_ffn_gate_w"].rearrange("(c p) e -> p c e", p=P)).then_inc(ld.sem, 16)
            SY.dma_start(gb[:, :], a["L0_ffn_gate_b"].rearrange("(o d) -> o d", o=1).broadcast_to((P, E))).then_inc(
                ld.sem, 16)
            need(VE, ld, 1)
            gcut.did("hi", VE.tensor_scalar(gwh[0][:, :, :], gw[:, :, :], WS, None, ALU.mult))
            need(VE, gcut, 0, "hi")
            gcut.did("lo", VE.scalar_tensor_tensor(gwh[1][:, :, :], gw[:, :, :], WS, gwh[0][:, :, :], ALU.mult,
                                                   ALU.subtract))
            gcut.did("one", VE.memset(wE[:, :, :], 1.0))
            need(PE, gcut, 0)
            need(VE, gcut, 0)
            need(SC, gcut, 0)

            def bc(t, n=E):
                return t.unsqueeze(2).broadcast_to((P, TG, n))

            def router(g, per):
                k = [0]

                def run(engine, make, alone=False):
                    engine.wait_ge(line.sem, g * per + k[0] + 1)
                    if alone:
                        settle(engine, spare[engine])
                    k[0] += 1
                    line.did("done", make())

                tok = ds(g * TG, TG)
                run(SC, lambda: SC.copy(stg[:, :, :], slots[:, :, cols(g)]))

                def back():
                    for t in range(TG):
                        for ch in range(DC):
                            tr = PE.transpose(ps[:, t // 2, (t % 2) * D + ch * P:(t % 2) * D + ch * P + P],
                                              stg[:, ch, t * P:t * P + P], ident[:, :])
                    return tr
                run(PE, back)
                run(VE, lambda: VE.tensor_tensor(
                    y[:, :, :], ps[:, 0:2, :].rearrange("p b (t d) -> p (b t) d", d=D), xs[:, tok, :], ALU.add))
                for t in range(TG):
                    run(VE, lambda: VE.bn_stats(st[:, t, :], y[:, t, :]), alone=True)
                for t in range(TG):
                    run(VE, lambda: VE.bn_aggr(mv2[:, t, :], st[:, t, :]), alone=True)
                run(VE, lambda: VE.tensor_scalar(ve2[:, :].unsqueeze(2), mv2[:, :, 1:2], LN_EPS, None, ALU.add))
                run(PO, lambda: PO.tensor_tensor(rs2[:, :], ve2[:, :], powh[:, 0:TG], ALU.pow))
                for t in range(TG):
                    run(VE, lambda: VE.tensor_scalar(y[:, t, :], y[:, t, :], mv2[:, t, 0:1], rs2[:, t:t + 1],
                                                     ALU.subtract, ALU.mult))
                run(SC, lambda: SC.mul(xs[:, tok, :], y[:, :, :], 2.0))

                def forth():
                    for ch in range(DC):
                        for t in range(TG):
                            tr = PE.transpose(ps[:, 2 + ch, t * P:t * P + P], y[:, t, ch * P:ch * P + P], ident[:, :])
                    return tr
                run(PE, forth)
                run(SC, lambda: SC.copy(xT[0][:, :, cols(g)], ps[:, 2:4, :]))
                run(VE, lambda: VE.tensor_tensor(xT[1][:, :, cols(g)], ps[:, 2:4, :], xT[0][:, :, cols(g)],
                                                 ALU.subtract))

                def gates():
                    for t in range(TG):
                        x = [[xT[h][:, ch, ds(g * GT + t * P, P)] for h in range(2)] for ch in range(DC)]
                        w = [[gwh[h][:, ch, :] for h in range(2)] for ch in range(DC)]
                        mm = three_passes(PE, ps[:, 4, t * E:t * E + E], list(zip(x, w)))
                    return mm
                run(PE, gates)
                run(VE, lambda: VE.scalar_tensor_tensor(
                    lg[:, :, :], ps[:, 4, 0:TG * E].rearrange("p (t e) -> p t e", e=E), 1 / WS,
                    gb[:, :].unsqueeze(1).broadcast_to((P, TG, E)), ALU.mult, ALU.add))
                run(VE, lambda: VE.tensor_reduce(s1[:, :], lg[:, :, :], AX, ALU.max))
                run(VE, lambda: VE.tensor_tensor(lg[:, :, :], lg[:, :, :], bc(s1[:, :]), ALU.subtract))
                run(SC, lambda: SC.activation(pe_[:, :, :], lg[:, :, :], ACT.Exp))
                run(VE, lambda: VE.tensor_reduce(s1[:, :], pe_[:, :, :], AX, ALU.add))
                run(VE, lambda: VE.reciprocal(s2[:, :], s1[:, :]))
                run(VE, lambda: VE.tensor_tensor(pr[:, :, :], pe_[:, :, :], bc(s2[:, :]), ALU.mult))
                for t in range(TG):
                    run(VE, lambda: VE.max(mx8[:, t, :], pr[:, t, :]), alone=True)
                for t in range(TG):
                    run(VE, lambda: VE.max_index(ix8[:, t, :], mx8[:, t, :], pr[:, t, :]), alone=True)
                run(VE, lambda: VE.tensor_copy(fi[:, :, :], ix8[:, :, :]))
                run(VE, lambda: VE.tensor_tensor(s1[:, :], mx8[:, :, 0:1].squeeze(2), mx8[:, :, 1:2].squeeze(2), ALU.add))
                run(VE, lambda: VE.tensor_scalar(s1[:, :], s1[:, :], TOP_EPS, None, ALU.add))
                run(VE, lambda: VE.reciprocal(s2[:, :], s1[:, :]))
                for k_, w in ((0, w0), (1, w1)):
                    run(VE, lambda: VE.tensor_tensor(eq[:, :, :], iota[:, :].unsqueeze(1).broadcast_to((P, TG, E)),
                                                     fi[:, :, k_:k_ + 1].broadcast_to((P, TG, E)), ALU.is_equal))
                    run(VE, lambda: VE.tensor_tensor(w[:, :, :], eq[:, :, :],
                                                     mx8[:, :, k_:k_ + 1].broadcast_to((P, TG, E)), ALU.mult))
                run(VE, lambda: VE.tensor_tensor(w0[:, :, :], w0[:, :, :], w1[:, :, :], ALU.add))
                run(VE, lambda: VE.tensor_tensor(wE[:, tok, 0:E], w0[:, :, :], bc(s2[:, :]), ALU.mult))
                assert k[0] == per, k[0]

            with nc.Fori(0, NG) as g:
                router(g, ROUTER_STEPS)
            nc.all_engine_barrier()

        with ExitStack() as c:
            w1f = sb(c, "w1f", [P, DC, I])
            w2f = sb(c, "w2f", [P, IC, D])
            w1c = [[sb(c, f"w1c{u}{i}", [P, DC, I], F16) for i in range(2)] for u in range(2)]
            w2c = [[sb(c, f"w2c{u}{i}", [P, IC, D], F16) for i in range(2)] for u in range(2)]
            b1 = [sb(c, f"b1{u}", [P, IC]) for u in range(2)]
            b2 = [sb(c, f"b2{u}", [P, D]) for u in range(2)]
            hf = [sb(c, f"hf{k}", [P, GT]) for k in range(2)]
            hh = [[sb(c, f"hh{k}{i}", [P, GT], F16) for i in range(2)] for k in range(2)]
            ty = sb(c, "ty", [P, TG, D])
            ld_e = stage(c, "ld_e", unit=64)
            cut_e = stage(c, "cut_e", "h1", "l1", "h2", "l2")
            H_pe = stage(c, "H_pe")
            H_g = stage(c, "H_g", "gelu", "hi", ahead=2)
            H_lo = stage(c, "H_lo", ahead=2)
            O_pe = stage(c, "O_pe", *[f"{k}" for k in range(IC)], ahead=2 * NG)
            O_ev = stage(c, "O_ev", "b2", *[f"acc{t}" for t in range(TG)], ahead=2 * NG)
            fin = stage(c, "fin")
            nc.all_engine_barrier()

            def load(e, u, w1, w2, bb1, bb2):
                need(SY, cut_e, e - 1)
                need(SY, O_ev, (e - 2) * NG + NG - 1)
                SY.dma_start(w1f[:, :, :], w1.rearrange("(c p) n -> p c n", p=P)).then_inc(ld_e.sem, 16)
                SY.dma_start(w2f[:, :, :], w2.rearrange("(c p) n -> p c n", p=P)).then_inc(ld_e.sem, 16)
                SY.dma_start(b1[u][:, :], bb1.rearrange("(c p) -> p c", p=P),
                             allow_slow_non_contiguous=True).then_inc(ld_e.sem, 16)
                SY.dma_start(b2[u][:, :], bb2.rearrange("(o d) -> o d", o=1).broadcast_to((P, D))).then_inc(
                    ld_e.sem, 16)
                need(VE, ld_e, e)
                need(VE, O_pe, (e - 2) * NG + NG - 1)
                for k, (f, w) in enumerate(((w1f, w1c[u]), (w2f, w2c[u]))):
                    cut_e.did(f"h{k + 1}", VE.tensor_scalar(w[0][:, :, :], f[:, :, :], WS, None, ALU.mult))
                    need(VE, cut_e, e, f"h{k + 1}")
                    cut_e.did(f"l{k + 1}", VE.scalar_tensor_tensor(w[1][:, :, :], f[:, :, :], WS, w[0][:, :, :],
                                                                   ALU.mult, ALU.subtract))

            def mlp(q, e, u, g):
                need(PE, cut_e, e)

                def up(k):
                    m = q * IC + k
                    need(PE, H_g, m - 2, "gelu")
                    w = [[w1c[u][h][:, ch, k * P:k * P + P] for h in range(2)] for ch in range(DC)]
                    x = [[xT[h][:, ch, cols(g)] for h in range(2)] for ch in range(DC)]
                    H_pe.did("done", three_passes(PE, ps[:, k % 2, :], list(zip(w, x))))
                    need(SC, H_pe, m)
                    need(SC, H_lo, m - 2)
                    H_g.did("gelu", SC.activation(hf[k % 2][:, :], ps[:, k % 2, :], ACT.Gelu_apprx_tanh,
                                                  bias=b1[u][:, k:k + 1], scale=1 / WS))
                    need(SC, H_g, m, "gelu")
                    need(SC, O_pe, q if k >= 2 else q - 1, f"{(k - 2) % IC}")
                    H_g.did("hi", SC.copy(hh[k % 2][0][:, :], hf[k % 2][:, :]))
                    need(VE, H_g, m, "hi")
                    H_lo.did("done", VE.tensor_tensor(hh[k % 2][1][:, :], hf[k % 2][:, :], hh[k % 2][0][:, :],
                                                      ALU.subtract))

                def down(k):
                    m = q * IC + k
                    need(PE, H_lo, m)
                    if k == 0:
                        need(PE, O_ev, q - 1, "b2")
                    for t in range(TG):
                        o = ps[:, 4 + t, 0:D]
                        for n_, (i, j) in enumerate(((0, 0), (0, 1), (1, 0))):
                            mm = PE.matmul(o, hh[k % 2][i][:, t * P:t * P + P], w2c[u][j][:, k, :],
                                           start=k == 0 and n_ == 0, stop=k == IC - 1 and n_ == 2)
                    O_pe.did(f"{k}", mm)

                up(0)
                for k in range(1, IC):
                    up(k)
                    down(k - 1)
                down(IC - 1)
                need(VE, O_pe, q)
                need(VE, O_ev, q - 1)
                O_ev.did("b2", VE.scalar_tensor_tensor(
                    ty[:, :, :], ps[:, 4:8, 0:D], 1 / WS, b2[u][:, :].unsqueeze(1).broadcast_to((P, TG, D)),
                    ALU.mult, ALU.add))
                need(VE, O_ev, q, "b2")
                for t in range(TG):
                    x = xs[:, g * TG + t, :]
                    O_ev.did(f"acc{t}", VE.scalar_tensor_tensor(x, ty[:, t, :], wE[:, g * TG + t, ds(e, 1)], x,
                                                                ALU.mult, ALU.add))

            with nc.Fori(0, E // 2) as i:
                for u in range(2):
                    e = i * 2 + u
                    load(e, u, a["L0_ffn_ew1"][e], a["L0_ffn_ew2"][e], a["L0_ffn_eb1"][e], a["L0_ffn_eb2"][e])
                    with nc.Fori(0, NG) as g:
                        mlp(e * NG + g, e, u, g)
            load(E, 0, a["L0_ffn_sh_w1"], a["L0_ffn_sh_w2"], a["L0_ffn_sh_b1"], a["L0_ffn_sh_b2"])
            with nc.Fori(0, NG) as g:
                mlp(E * NG + g, E, 0, g)
            nc.all_engine_barrier()

        with ExitStack() as c:
            st = sb(c, "st3", [P, NT, 6])
            mv3 = sb(c, "mv3", [P, NT, 2])
            ve3 = sb(c, "ve3", [P, NT])
            rs3 = sb(c, "rs3", [P, NT])
            p3 = sb(c, "p3", [P, NT])
            f_ve = stage(c, "f_ve", "st", "ag")
            f_v1 = stage(c, "f_v1", "pow0", "eps")
            f_po = stage(c, "f_po")
            f_out = stage(c, "f_out")
            stored = stage(c, "stored", unit=16)
            nc.all_engine_barrier()
            f_v1.did("pow0", VE.memset(p3[:, :], -0.5))
            for t in range(NT):
                f_ve.did("st", VE.bn_stats(st[:, t, :], xs[:, t, :]))
                need(VE, f_ve, t, "st")
                f_ve.did("ag", VE.bn_aggr(mv3[:, t, :], st[:, t, :]))
            need(VE, f_ve, NT - 1)
            f_v1.did("eps", VE.tensor_scalar(ve3[:, :].unsqueeze(2), mv3[:, :, 1:2], LN_EPS, None, ALU.add))
            need(PO, f_v1, 0)
            f_po.did("done", PO.tensor_tensor(rs3[:, :], ve3[:, :], p3[:, :], ALU.pow))
            need(VE, f_po, 0)
            ov = out.rearrange("b (t p) d -> p (b t) d", p=P)
            for t in range(NT):
                f_out.did("done", VE.tensor_scalar(xs[:, t, :], xs[:, t, :], mv3[:, t, 0:1], rs3[:, t:t + 1],
                                                   ALU.subtract, ALU.mult))
                if t % 4 == 3:
                    need(SY, f_out, t)
                    SY.dma_start(ov[:, t - 3:t + 1, :], xs[:, t - 3:t + 1, :]).then_inc(stored.sem, 16)
            need(SY, stored, NT // 4 - 1)


ROUTER_STEPS = 47


_INS = ['x', 'ctx_1024', 'L0_attn_Wq', 'L0_attn_Wk', 'L0_attn_Wv', 'L0_attn_Wo', 'L0_attn_bo',
        'L0_xattn_Wq', 'L0_xattn_Wk', 'L0_xattn_Wv', 'L0_xattn_gru_wih', 'L0_xattn_gru_whh',
        'L0_xattn_gru_bih', 'L0_xattn_gru_bhh', 'L0_xattn_slot_norm_w', 'L0_xattn_input_norm_w',
        'L0_ffn_gate_w', 'L0_ffn_gate_b', 'L0_ffn_sh_w1', 'L0_ffn_sh_b1', 'L0_ffn_sh_w2', 'L0_ffn_sh_b2',
        'L0_ffn_ew1', 'L0_ffn_eb1', 'L0_ffn_ew2', 'L0_ffn_eb2']
_OUT = ((8, 256, 256), 'float32')


def kernel(**inputs):
    import numpy as _np
    import concourse.bacc as _bacc
    from concourse.bass_utils import run_bass_kernel_spmd as _run

    nc = _bacc.Bacc("TRN2", target_bir_lowering=False, num_devices=1)
    arrays, args = {}, {}
    for name in _INS:
        v = _np.ascontiguousarray(inputs[name])
        arrays[f"in_{name}"] = v
        args[name] = nc.dram_tensor(f"in_{name}", v.shape, mybir.dt.from_np(v.dtype), kind="ExternalInput").ap()
    out = nc.dram_tensor("out_0", _OUT[0], mybir.dt.from_np(_np.dtype(_OUT[1])), kind="ExternalOutput").ap()
    decoder_layer(nc, args, out)
    r = _run(nc, [arrays], core_ids=[0])
    return r.results[0]["out_0"]
```

```python
from contextlib import ExitStack

import concourse.bass as bass
from concourse import mybir

F32 = mybir.dt.float32
F16 = mybir.dt.float16
BF16 = mybir.dt.bfloat16
U32 = mybir.dt.uint32
ALU = mybir.AluOpType
ACT = mybir.ActivationFunctionType
AX = mybir.AxisListType.X
ds = bass.ds

P = 128
WS = 64.0
LN_EPS = 1e-5
RMS_EPS = 1e-6
SUM_EPS = 1e-6
TOP_EPS = 1e-9


class Stage:

    def __init__(self, nc, ctx, name, steps=("done",), unit=1, ahead=1):
        self.sem = ctx.enter_context(nc.semaphore(name))
        self.steps, self.unit, self.ahead = list(steps), unit, ahead
        if ahead:
            nc.gpsimd.sem_inc(self.sem, unit * len(self.steps) * ahead)

    def did(self, step, instruction):
        assert step in self.steps
        instruction.then_inc(self.sem, self.unit)

    def at(self, item, step=None):
        i = len(self.steps) - 1 if step is None else self.steps.index(step)
        return item * (self.unit * len(self.steps)) + self.unit * (len(self.steps) * self.ahead + i + 1)


def need(engine, stage, item, step=None):
    value = stage.at(item, step)
    if isinstance(value, int) and value <= 0:
        return
    engine.wait_ge(stage.sem, value)


def settle(engine, spare):
    engine.sem_inc(spare, 1)


def three_passes(pe, out, pairs, **kw):
    products = [(w[i], a[j]) for w, a in pairs for i, j in ((0, 0), (0, 1), (1, 0))]
    for n, (w, a) in enumerate(products):
        last = pe.matmul(out, w, a, start=n == 0, stop=n == len(products) - 1, **kw)
    return last


def decoder_layer(nc, a, out):
    PE, SC, VE, PO, SY = nc.tensor, nc.scalar, nc.vector, nc.gpsimd, nc.sync
    NB, S, D = a["x"].shape
    M = a["ctx_1024"].shape[1]
    INNER = a["L0_attn_Wq"].shape[1]
    HD = 64
    E, _, I = a["L0_ffn_ew1"].shape
    T = NB * S
    NT, DC, IC = T // P, D // P, I // P
    PAIRS = INNER // P
    G3 = 3 * D
    GT = 512
    NG = T // GT
    BG = GT // S
    ITERS = 3
    TG = GT // P
    NTILE = 2 * T // P + E - 1
    SCALE = float(HD) ** -0.5
    XSCALE = float(D) ** -0.5
    top = ExitStack()
    with top:
        def sb(ctx, name, shape, dt=F32):
            return ctx.enter_context(nc.sbuf_tensor(name, shape, dt))

        ps = top.enter_context(nc.psum_tensor("ps", [P, 8, 512], F32))

        def stage(ctx, name, *steps, unit=1, ahead=1):
            return Stage(nc, ctx, name, steps or ("done",), unit, ahead)

        spare = {e: top.enter_context(nc.semaphore(f"spare_{k}")) for e, k in ((SC, "sc"), (VE, "ve"))}

        ident = sb(top, "ident", [P, P])
        ones = sb(top, "ones", [P, P])
        maskf = sb(top, "maskf", [P, P])
        mask = sb(top, "mask", [P, P], BF16)
        identb = sb(top, "identb", [P, P], BF16)
        powh = sb(top, "powh", [P, 8])
        iota = sb(top, "iota", [P, E])
        iotai = sb(top, "iotai", [P, E], mybir.dt.int32)
        xs = sb(top, "xs", [P, NT, D])
        xT = [sb(top, f"xT{i}", [P, DC, T], F16) for i in range(2)]
        idx0 = sb(top, "idx0", [P, 2, NT], mybir.dt.int32)
        top_w = sb(top, "top_w", [P, 2, NT])
        tile_e = sb(top, "tile_e", [P, NTILE], mybir.dt.int32)
        mid = top.enter_context(ExitStack())
        rows_x = nc.dram_tensor("rows_x", [NTILE * P, D], F32, kind="Internal").ap()
        rows_y = nc.dram_tensor("rows_y", [NTILE * P, D], F32, kind="Internal").ap()
        zrow = sb(mid, "zrow", [P, D])

        const = stage(top, "const", "ident0", "mask0", "ones", "ident", "mask", "powh", "iota")
        constv = stage(top, "constv", "mask", "identb", "iota")
        nc.all_engine_barrier()
        const.did("ident0", PO.memset(ident[:, :], 0.0))
        const.did("mask0", PO.memset(maskf[:, :], 0.0))
        const.did("ones", PO.memset(ones[:, :], 1.0))
        need(PO, const, 0, "ones")
        const.did("ident", PO.affine_select(out=ident[:, :], in_=ident[:, :], compare_op=ALU.not_equal, fill=1.0,
                                            base=0, pattern=[[-1, P]], channel_multiplier=1))
        const.did("mask", PO.affine_select(out=maskf[:, :], in_=maskf[:, :], compare_op=ALU.is_ge,
                                           fill=-1e9 / SCALE, base=0, pattern=[[-1, P]], channel_multiplier=1))
        const.did("powh", PO.memset(powh[:, :], -0.5))
        const.did("iota", PO.iota(iotai[:, :], pattern=[[1, E]], base=0, channel_multiplier=0))
        zrow_s = stage(top, "zrow_s")
        zeroed = stage(top, "zeroed", unit=16)
        zrow_s.did("done", PO.memset(zrow[:, :], 0.0))
        need(SY, zrow_s, 0)
        SY.dma_start(rows_x.rearrange("(t p) d -> p t d", p=P),
                     zrow[:, :].unsqueeze(1).broadcast_to((P, NTILE, D))).then_inc(zeroed.sem, 16)
        need(VE, const, 0)
        constv.did("mask", VE.tensor_copy(mask[:, :], maskf[:, :]))
        constv.did("identb", VE.tensor_copy(identb[:, :], ident[:, :]))
        constv.did("iota", VE.tensor_copy(iota[:, :], iotai[:, :]))

        def cut(v, hi, lo, src, chain, names, scale=WS):
            chain.did(names[0], v.tensor_scalar(hi, src, scale, None, ALU.mult))
            return chain, names[1], (lambda: v.scalar_tensor_tensor(lo, src, scale, hi, ALU.mult, ALU.subtract))

        with ExitStack() as c:
            wqkv = [sb(c, f"wqkv{i}", [P, DC, 3, INNER], F16) for i in range(2)]
            wo = [sb(c, f"wo{i}", [P, PAIRS, D], F16) for i in range(2)]
            wst = [sb(c, f"wst{i}", [P, DC, INNER]) for i in range(2)]
            xin = [sb(c, f"xin{i}", [P, S // P, D]) for i in range(2)]
            bo = sb(c, "bo", [P, D])
            qpad = sb(c, "qpad", [P, 2, S])
            kT = sb(c, "kT", [P, S])
            v_sb = [sb(c, f"v{i}", [P, S // P, P]) for i in range(2)]
            prob = sb(c, "prob", [P, 2, 384])
            pT = sb(c, "pT", [P, 2, 384])
            oT = [sb(c, f"oT{i}", [P, PAIRS, S], F16) for i in range(2)]
            mx = sb(c, "mx", [P, 2, 2])
            nmx = sb(c, "nmx", [P, 2, 2])
            den = sb(c, "den", [P, 2, 2])
            rden = sb(c, "rden", [P, 2, 2])
            bst = sb(c, "bst", [P, 2, 6])
            mv = sb(c, "mv", [P, 2, 2])
            ve = sb(c, "ve", [P, 2])
            rstd = sb(c, "rstd", [P, 2])

            ld_w = [stage(c, f"ld_w{i}", unit=16) for i in range(2)]
            ld_x = [stage(c, f"ld_x{i}", unit=16) for i in range(2)]
            ld_xs = stage(c, "ld_xs", unit=16)
            ld_bo = stage(c, "ld_bo", unit=16)
            w_cut = stage(c, "w_cut", "hi", "lo")
            x_tr = stage(c, "x_tr", ahead=2)
            x_hi = stage(c, "x_hi", ahead=2)
            x_lo = stage(c, "x_lo", ahead=2)
            bo_add = stage(c, "bo_add")
            zero = stage(c, "zero", "qpad", "oT_hi", "oT_lo")
            nc.all_engine_barrier()

            SY.dma_start(xs[:, :, :], a["x"].rearrange("b (t p) d -> p (b t) d", p=P)).then_inc(ld_xs.sem, 16)
            bo_row = a["L0_attn_bo"].rearrange("(o d) -> o d", o=1)
            SY.dma_start(bo[:, :], bo_row.broadcast_to((P, D))).then_inc(ld_bo.sem, 16)
            zero.did("qpad", VE.memset(qpad[:, :, :], 0.0))
            srcs = [a[f"L0_attn_W{k}"].rearrange("(c p) n -> p c n", p=P) for k in "qkv"]
            srcs.append(a["L0_attn_Wo"].rearrange("(s p) n -> p s n", p=P))
            for n, src in enumerate(srcs):
                need(SC, w_cut, n - 2)
                st = wst[n % 2]
                dst = st[:, :, :] if n < 3 else st[:, :, :].rearrange("p c n -> p (c n)").rearrange(
                    "p (s n) -> p s n", s=PAIRS)
                SC.dma_start(dst, src).then_inc(ld_w[n % 2].sem, 16)
            for n in range(4):
                need(VE, ld_w[n % 2], n // 2)
                st = wst[n % 2]
                if n < 3:
                    hi, lo, src = wqkv[0][:, :, n, :], wqkv[1][:, :, n, :], st[:, :, :]
                else:
                    src = st[:, :, :].rearrange("p c n -> p (c n)")
                    hi, lo = (w[:, :, :].rearrange("p s n -> p (s n)") for w in wo)
                w_cut.did("hi", VE.tensor_scalar(hi, src, WS, None, ALU.mult))
                need(VE, w_cut, n, "hi")
                w_cut.did("lo", VE.scalar_tensor_tensor(lo, src, WS, hi, ALU.mult, ALU.subtract))
            need(PO, ld_xs, 0)
            need(PO, ld_bo, 0)
            bo_add.did("done", PO.tensor_tensor(
                xs[:, :, :], xs[:, :, :], bo[:, :].unsqueeze(1).broadcast_to((P, NT, D)), ALU.add))

            need(PE, const, 0, "ident")
            xv = a["x"].rearrange("b (t p) d -> b p t d", p=P)
            with nc.Fori(0, NB // 2) as i:
                for u in range(2):
                    b = i * 2 + u
                    need(SY, x_tr, b - 2)
                    SY.dma_start(xin[u][:, :, :], xv[b]).then_inc(ld_x[u].sem, 16)
                    need(PE, ld_x[u], i)
                    need(PE, x_lo, b - 2)
                    need(PE, x_hi, b - 2)
                    for ch in range(DC):
                        for t in range(S // P):
                            tr = PE.transpose(ps[:, u, ch * S + t * P:ch * S + t * P + P],
                                              xin[u][:, t, ch * P:ch * P + P], ident[:, :])
                    x_tr.did("done", tr)
                    pv = ps[:, u, :].rearrange("p (c t) -> p c t", c=DC)
                    need(SC, x_tr, b)
                    x_hi.did("done", SC.copy(xT[0][:, :, ds(b * S, S)], pv))
                    need(VE, x_hi, b)
                    x_lo.did("done", VE.tensor_tensor(xT[1][:, :, ds(b * S, S)], pv,
                                                      xT[0][:, :, ds(b * S, S)], ALU.subtract))

            qk_mm = stage(c, "qk_mm")
            v_mm = stage(c, "v_mm")
            s_mm = stage(c, "s_mm")
            pt_mm = stage(c, "pt_mm")
            o_mm = stage(c, "o_mm")
            y_mm = stage(c, "y_mm")
            qkv_ev = stage(c, "qkv_ev", "k", "q0", "q1")
            v_ev = stage(c, "v_ev")
            smax = stage(c, "smax", "q0", "q1", "neg")
            expo = stage(c, "expo", "h0q0", "h0q1", "h1q0", "h1q1")
            norm = stage(c, "norm", "recip", "h0q0", "h0q1", "h1q0", "h1q1")
            pt_ev = stage(c, "pt_ev")
            o_ev = stage(c, "o_ev", "hi", "lo")
            ln = stage(c, "ln", "add", "st0", "st1", "ag0", "ag1", "eps", "out0", "out1", ahead=2)
            ln_pow = stage(c, "ln_pow")
            nc.all_engine_barrier()

            def project(n, b, p, y_read):
                cols = ds(p * P, P)
                need(PE, v_ev, n - 1)
                for t in range(S // P):
                    x = [[xT[h][:, ch, ds(b * S + t * P, P)] for h in range(2)] for ch in range(DC)]
                    w = [[wqkv[h][:, ch, 2, cols] for h in range(2)] for ch in range(DC)]
                    mm = three_passes(PE, ps[:, 1, t * P:(t + 1) * P], list(zip(x, w)))
                v_mm.did("done", mm)
                need(PE, qkv_ev, n - 1)
                need(PE, ln, y_read, "add")
                for k in range(2):
                    w = [[wqkv[h][:, ch, k, cols] for h in range(2)] for ch in range(DC)]
                    x = [[xT[h][:, ch, ds(b * S, S)] for h in range(2)] for ch in range(DC)]
                    mm = three_passes(PE, ps[:, 0, k * S:(k + 1) * S], list(zip(w, x)))
                qk_mm.did("done", mm)

            def project_out(n):
                need(SC, qk_mm, n)
                need(SC, s_mm, n - 1)
                qkv_ev.did("k", SC.mul(kT[:, :], ps[:, 0, S:2 * S], 1 / WS))
                for h in range(2):
                    r = slice(HD * h, HD * h + HD)
                    qkv_ev.did(f"q{h}", SC.mul(qpad[r, h, :], ps[r, 0, 0:S], 1 / WS))

            def values_out(n, u):
                need(VE, v_mm, n)
                need(VE, o_mm, n - 2)
                v_ev.did("done", VE.tensor_scalar(v_sb[u][:, :, :], ps[:, 1, 0:S].rearrange("p (t n) -> p t n", n=P),
                                                  1 / WS, None, ALU.mult))

            def scores(m, u):
                need(PE, qkv_ev, m)
                need(PE, expo, m - 2)
                bank = (2, 6)[u]
                for h in range(2):
                    for t in range(2):
                        o = ps[:, bank + h, 0:P] if t == 0 else ps[:, bank + h, P:3 * P]
                        PE.matmul(o, qpad[:, h, t * P:t * P + P], kT[:, 0:(t + 1) * P], start=True, stop=False)
                        mm = PE.matmul(ps[:, bank + h, 2 * P * t:2 * P * t + P], identb[:, :], mask[:, :],
                                       start=False, stop=True)
                s_mm.did("done", mm)

            def maxima(m, u):
                sv = ps[:, 2:4, :] if u == 0 else ps[:, 6:8, :]
                need(VE, s_mm, m)
                need(VE, expo, m - 1)
                smax.did("q0", VE.tensor_reduce(mx[:, :, 0:1], sv[:, :, 0:P], AX, ALU.max))
                smax.did("q1", VE.tensor_reduce(mx[:, :, 1:2], sv[:, :, P:3 * P], AX, ALU.max))
                need(VE, smax, m, "q1")
                smax.did("neg", VE.tensor_scalar(nmx[:, :, :], mx[:, :, :], -SCALE, None, ALU.mult))

            def exponentials(m, u, h):
                sv = ps[:, 2:4, :] if u == 0 else ps[:, 6:8, :]
                if h == 0:
                    need(SC, smax, m)
                    need(SC, pt_mm, m - 1)
                    need(SC, norm, m - 1)
                if True:
                    for t in range(2):
                        r = slice(0, P) if t == 0 else slice(P, 3 * P)
                        expo.did(f"h{h}q{t}", SC.activation(prob[:, h, r], sv[:, h, r], ACT.Exp,
                                                            bias=nmx[:, h, t:t + 1], scale=SCALE,
                                                            accum_out=den[:, h, t:t + 1]))

            def normalise(m):
                need(VE, expo, m)
                norm.did("recip", VE.reciprocal(rden[:, :, :], den[:, :, :]))
                need(VE, norm, m, "recip")
                for h in range(2):
                    for t in range(2):
                        r = slice(0, P) if t == 0 else slice(P, 3 * P)
                        norm.did(f"h{h}q{t}", VE.tensor_scalar(prob[:, h, r], prob[:, h, r], rden[:, h, t:t + 1],
                                                               None, ALU.mult))

            def transpose_prob(m):
                need(PE, norm, m)
                need(PE, pt_ev, m - 1)
                need(PE, o_ev, m - 1)
                for h in range(2):
                    for blk in range(3):
                        mm = PE.transpose(ps[:, 4 + h, blk * P:blk * P + P], prob[:, h, blk * P:blk * P + P],
                                          ident[:, :])
                pt_mm.did("done", mm)
                need(VE, pt_mm, m)
                need(VE, o_mm, m - 1)
                pt_ev.did("done", VE.tensor_copy(pT[:, :, :], ps[:, 4:6, 0:384]))

            def weigh_values(m, u, slot, batch):
                need(PE, pt_ev, m)
                need(PE, v_ev, m)
                need(PE, o_ev, m - 1)
                for t, key, cols_ in ((0, 0, 0), (1, 0, P), (1, 1, 2 * P)):
                    for h in range(2):
                        r = slice(HD * h, HD * h + HD)
                        mm = PE.matmul(ps[r, 4 + t, 384:512], v_sb[u][:, key, r], pT[:, h, cols_:cols_ + P],
                                       start=key == 0, stop=key == t, skip_group_check=True)
                o_mm.did("done", mm)
                need(VE, o_mm, m)
                need(VE, y_mm, batch - 1)
                hi, lo = (o[:, slot, :].rearrange("p (t q) -> p t q", t=2) for o in oT)
                o_ev.did("hi", VE.tensor_copy(hi, ps[:, 4:6, 384:512]))
                need(VE, o_ev, m, "hi")
                o_ev.did("lo", VE.tensor_tensor(lo, ps[:, 4:6, 384:512], hi, ALU.subtract))

            def output_projection(b, last_item, projected):
                need(PE, o_ev, last_item)
                need(PE, qkv_ev, projected)
                for t in range(2):
                    o = [[oT[h][:, s, t * P:t * P + P] for h in range(2)] for s in range(PAIRS)]
                    w = [[wo[h][:, s, :] for h in range(2)] for s in range(PAIRS)]
                    mm = three_passes(PE, ps[:, 0, t * D:t * D + D], list(zip(o, w)))
                y_mm.did("done", mm)
                need(VE, y_mm, b)
                y = xs[:, ds(b * 2, 2), :] if not isinstance(b, int) else xs[:, 2 * b:2 * b + 2, :]
                tile = [xs[:, b * 2 + t, :] for t in range(2)]
                need(VE, ln, b - 1)
                need(VE, ln_pow, b - 1)
                ln.did("add", VE.scalar_tensor_tensor(y, ps[:, 0, :].rearrange("p (t n) -> p t n", n=D), 1 / WS, y,
                                                      ALU.mult, ALU.add))
                need(VE, ln, b, "add")
                settle(VE, spare[VE])
                for t in range(2):
                    ln.did(f"st{t}", VE.bn_stats(bst[:, t, :], tile[t]))
                need(VE, ln, b, "st1")
                settle(VE, spare[VE])
                for t in range(2):
                    ln.did(f"ag{t}", VE.bn_aggr(mv[:, t, :], bst[:, t, :]))
                need(VE, ln, b, "ag1")
                ln.did("eps", VE.tensor_scalar(ve[:, :].unsqueeze(2), mv[:, :, 1:2], LN_EPS, None, ALU.add))
                need(PO, ln, b, "eps")
                ln_pow.did("done", PO.tensor_tensor(rstd[:, :], ve[:, :], powh[:, 0:2], ALU.pow))
                need(VE, ln_pow, b)
                for t in range(2):
                    ln.did(f"out{t}", VE.tensor_scalar(tile[t], tile[t], mv[:, t, 0:1], rstd[:, t:t + 1],
                                                       ALU.subtract, ALU.mult))

            def step(n, u, b, p, qkv=True, mid=True, pv=True, pv_slot=None, pv_batch=None, y_read=-1):
                if mid:
                    scores(n - 1, 1 - u)
                    maxima(n - 1, 1 - u)
                if pv:
                    transpose_prob(n - 2)
                if qkv:
                    project(n, b, p, y_read)
                if mid:
                    exponentials(n - 1, 1 - u, 0)
                if qkv:
                    project_out(n)
                if mid:
                    exponentials(n - 1, 1 - u, 1)
                if pv:
                    weigh_values(n - 2, u, pv_slot, pv_batch)
                if qkv:
                    values_out(n, u)
                if mid:
                    normalise(n - 1)

            need(PE, w_cut, 3)
            need(PE, constv, 0)
            need(PE, zero, 0, "qpad")
            need(VE, bo_add, 0)
            need(PE, x_lo, NB - 1)

            def inner(b):
                with nc.Fori(1, PAIRS // 2) as k:
                    for u in range(2):
                        step(b * PAIRS + k * 2 + u, u, b, k * 2 + u, pv_slot=k * 2 + (u - 2), pv_batch=b, y_read=b - 1)

            step(0, 0, 0, 0, mid=False, pv=False)
            step(1, 1, 0, 1, pv=False)
            inner(0)
            with nc.Fori(1, NB) as b:
                for u in range(2):
                    step(b * PAIRS + u, u, b, u, pv_slot=PAIRS - 2 + u, pv_batch=b - 1, y_read=b - 2)
                output_projection(b - 1, b * PAIRS - 1, b * PAIRS + 1)
                inner(b)
            N = NB * PAIRS
            step(N, 0, None, None, qkv=False, pv_slot=PAIRS - 2, pv_batch=NB - 1)
            step(N + 1, 1, None, None, qkv=False, mid=False, pv_slot=PAIRS - 1, pv_batch=NB - 1)
            output_projection(NB - 1, N - 1, N - 1)
            nc.all_engine_barrier()

        slots = sb(mid, "slots", [P, DC, T])
        with ExitStack() as c:
            whh = [sb(c, f"whh{i}", [P, DC, G3], F16) for i in range(2)]
            vw = [sb(c, f"vw{i}", [P, NB, G3], F16) for i in range(2)]
            kq = [sb(c, f"kq{i}", [P, DC, NB * M], F16) for i in range(2)]
            b_tz = sb(c, "b_tz", [P, 6])
            bih = sb(c, "bih", [P, 6])
            bhh = sb(c, "bhh", [P, 6])
            with ExitStack() as q:
                wk, wq, wv = (sb(q, f"x_{k}", [P, DC, D]) for k in ("wk", "wq", "wv"))
                wn = [sb(q, f"gw{i}", [P, G3 // P, D]) for i in range(2)]
                wihT = sb(q, "wihT", [P, DC, G3])
                whhT = sb(q, "whhT", [P, DC, G3])
                wa = sb(q, "wa", [P, DC, D])
                wb = sb(q, "wb", [P, DC, G3])
                ctxt = sb(q, "ctxt", [P, NB, D])
                pnT = sb(q, "pnT", [P, DC, NB * M])
                kqf = sb(q, "kqf", [P, NB * M])
                vwf = sb(q, "vwf", [P, G3])
                sqc = sb(q, "sqc", [P, D])
                ssc = sb(q, "ssc", [P, NB])
                rc = sb(q, "rc", [P, NB])
                nw = sb(q, "nw", [P, 2, DC])
                snw = sb(q, "snw", [P, DC])
                ld = stage(q, "x_ld", unit=16)
                line = stage(q, "x_line")
                nc.all_engine_barrier()
                loads = [
                    (wk[:, :, :], a["L0_xattn_Wk"].rearrange("(c p) n -> p c n", p=P)),
                    (wq[:, :, :], a["L0_xattn_Wq"].rearrange("(c p) n -> p c n", p=P)),
                    (wv[:, :, :], a["L0_xattn_Wv"].rearrange("(c p) n -> p c n", p=P)),
                    (wn[0][:, :, :], a["L0_xattn_gru_wih"].rearrange("(c p) n -> p c n", p=P)),
                    (wn[1][:, :, :], a["L0_xattn_gru_whh"].rearrange("(c p) n -> p c n", p=P)),
                    (ctxt[0:M, :, :], a["ctx_1024"].rearrange("b m d -> m b d")),
                    (bih[:, :], a["L0_xattn_gru_bih"].rearrange("(c p) -> p c", p=P)),
                    (bhh[:, :], a["L0_xattn_gru_bhh"].rearrange("(c p) -> p c", p=P)),
                    (nw[:, 0, :], a["L0_xattn_input_norm_w"].rearrange("(c p) -> p c", p=P)),
                    (nw[:, 1, :], a["L0_xattn_slot_norm_w"].rearrange("(c p) -> p c", p=P)),
                ]
                for n, (dst, src) in enumerate(loads):
                    SY.dma_start(dst, src, allow_slow_non_contiguous=n >= 6).then_inc(ld.sem, 16)
                for eng in (PE, SC, VE):
                    need(eng, ld, len(loads) - 1)
                count = [0]

                def after(engine):
                    need(engine, line, count[0] - 1)

                def made(ins):
                    line.did("done", ins)
                    count[0] += 1

                def run(engine, make):
                    after(engine)
                    made(make())

                run(VE, lambda: VE.tensor_tensor(b_tz[:, :], bih[:, :], bhh[:, :], ALU.add))
                run(VE, lambda: VE.tensor_scalar(b_tz[:, :], b_tz[:, :], 0.5, None, ALU.mult))
                run(VE, lambda: VE.tensor_scalar(bhh[:, :], bhh[:, :], 0.5, None, ALU.mult))
                run(VE, lambda: VE.tensor_scalar(snw[:, :], nw[:, 1, :], XSCALE * WS, None, ALU.mult))
                for b in range(NB):
                    run(SC, lambda: SC.activation(sqc[0:M, :], ctxt[0:M, b, :], ACT.Square,
                                                  accum_out=ssc[0:M, b:b + 1]))
                run(VE, lambda: VE.tensor_scalar(ssc[0:M, :], ssc[0:M, :], 1.0 / D, RMS_EPS, ALU.mult, ALU.add))
                run(PO, lambda: PO.tensor_tensor(rc[0:M, :], ssc[0:M, :], powh[0:M, 0:NB], ALU.pow))
                run(VE, lambda: VE.tensor_tensor(ctxt[0:M, :, :], ctxt[0:M, :, :],
                                                 rc[0:M, :].unsqueeze(2).broadcast_to((M, NB, D)), ALU.mult))
                for ch in range(DC):
                    after(PE)
                    for b in range(NB):
                        tr = PE.transpose(ps[:, b // 4, (b % 4) * M:(b % 4) * M + M],
                                          ctxt[0:M, b, ch * P:ch * P + P], ident[0:M, 0:M])
                    made(tr)
                    run(VE, lambda: VE.tensor_scalar(
                        pnT[:, ch, :].rearrange("p (k m) -> p k m", k=2), ps[:, 0:2, 0:4 * M], nw[:, 0, ch:ch + 1],
                        None, ALU.mult))
                    for w, wt in ((wn[0], wihT), (wn[1], whhT)):
                        after(PE)
                        for g in range(G3 // P):
                            tr = PE.transpose(ps[:, g // 3, (g % 3) * P:(g % 3) * P + P],
                                              w[:, g, ch * P:ch * P + P], ident[:, :])
                        made(tr)
                        run(VE, lambda: VE.tensor_copy(wt[:, ch, :].rearrange("p (k m) -> p k m", k=2),
                                                       ps[:, 0:2, 0:3 * P]))
                run(VE, lambda: VE.tensor_scalar(whh[0][:, :, :], whhT[:, :, :], WS, None, ALU.mult))
                run(VE, lambda: VE.scalar_tensor_tensor(whh[1][:, :, :], whhT[:, :, :], WS, whh[0][:, :, :],
                                                        ALU.mult, ALU.subtract))
                for e in range(DC):
                    after(PE)
                    for f in range(DC):
                        PE.matmul(ps[:, 0, 0:D], wk[:, f, e * P:e * P + P], wq[:, f, :], start=f == 0,
                                  stop=f == DC - 1)
                    for k in range(2):
                        for f in range(DC):
                            mm = PE.matmul(ps[:, 1 + k, 0:3 * P], wv[:, f, e * P:e * P + P],
                                           wihT[:, f, k * 3 * P:(k + 1) * 3 * P], start=f == 0, stop=f == DC - 1)
                    made(mm)
                    run(VE, lambda: VE.tensor_copy(wa[:, e, :], ps[:, 0, 0:D]))
                    run(VE, lambda: VE.tensor_copy(wb[:, e, :].rearrange("p (k m) -> p k m", k=2),
                                                   ps[:, 1:3, 0:3 * P]))
                half = NB * M // 2
                for d in range(DC):
                    after(PE)
                    for k in range(2):
                        for e in range(DC):
                            mm = PE.matmul(ps[:, k, 0:half], wa[:, e, d * P:d * P + P],
                                           pnT[:, e, k * half:(k + 1) * half], start=e == 0, stop=e == DC - 1)
                    made(mm)
                    run(VE, lambda: VE.tensor_scalar(kqf[:, :].rearrange("p (k m) -> p k m", k=2), ps[:, 0:2, 0:half],
                                                     snw[:, d:d + 1], None, ALU.mult))
                    run(VE, lambda: VE.tensor_copy(kq[0][:, d, :], kqf[:, :]))
                    run(VE, lambda: VE.tensor_tensor(kq[1][:, d, :], kqf[:, :], kq[0][:, d, :], ALU.subtract))
                for b in range(NB):
                    after(PE)
                    for k in range(2):
                        for e in range(DC):
                            mm = PE.matmul(ps[0:M, k, 0:3 * P], pnT[:, e, b * M:(b + 1) * M],
                                           wb[:, e, k * 3 * P:(k + 1) * 3 * P], start=e == 0, stop=e == DC - 1)
                    made(mm)
                    run(VE, lambda: VE.tensor_scalar(vwf[0:M, :].rearrange("p (k m) -> p k m", k=2),
                                                     ps[0:M, 0:2, 0:3 * P], WS, None, ALU.mult))
                    run(VE, lambda: VE.tensor_copy(vw[0][0:M, b, :], vwf[0:M, :]))
                    run(VE, lambda: VE.tensor_tensor(vw[1][0:M, b, :], vwf[0:M, :], vw[0][0:M, b, :], ALU.subtract))
                for t in range(NT):
                    after(PE)
                    for ch in range(DC):
                        tr = PE.transpose(ps[:, 0, ch * P:ch * P + P], xs[:, t, ch * P:ch * P + P], ident[:, :])
                    made(tr)
                    run(VE, lambda: VE.tensor_copy(slots[:, :, t * P:t * P + P],
                                                   ps[:, 0, 0:2 * P].rearrange("p (c t) -> p c t", c=DC)))
                nc.all_engine_barrier()

            sh = [[sb(c, f"s{i}{u}", [P, DC, GT], F16) for i in range(2)] for u in range(2)]
            sq = sb(c, "sq", [P, DC, GT])
            diag = sb(c, "diag", [P, TG, P])
            rr = sb(c, "rr", [P, GT])
            sc = sb(c, "sc", [P, BG, S])
            ex = sb(c, "ex", [P, BG, S])
            an = sb(c, "an", [P, GT])
            anh = [[sb(c, f"an{i}{u}", [P, GT], F16) for i in range(2)] for u in range(2)]
            msq = sb(c, "msq", [P, TG])
            rms = sb(c, "rms", [P, TG])
            gmx = sb(c, "gmx", [P, BG])
            gneg = sb(c, "gneg", [P, BG])
            gden = sb(c, "gden", [P, BG])
            grec = sb(c, "grec", [P, BG])
            cse = sb(c, "cse", [P, TG])
            crec = sb(c, "crec", [P, TG])
            tr_, tz, hn, t1, t2, nn, dl, uu = (sb(c, k, [P, GT]) for k in
                                               ("tr_", "tz", "hn", "t1", "t2", "nn", "dl", "uu"))
            A_sc = stage(c, "A_sc", "hi", "sq", "rr", "e0", "e1", "rr2", "anh")
            A_ve = stage(c, "A_ve", "lo", "msq", "diag", "sc", "mx", "neg", "grec", "m0", "m1", "cse", "crec",
                         "diag2", "an", "anl")
            A_po = stage(c, "A_po", "pow")
            A_pe = stage(c, "A_pe", "ss", "rb", "sc", "cs", "rb2")
            G_pe = stage(c, "G_pe", "r", "z", "hn", "xn", ahead=3)
            G_sc = stage(c, "G_sc", "tr", "tz", "hn", "nn")
            G_ve = stage(c, "G_ve", "t1", "t2", "u", "out", ahead=2 * NG)
            G_po = stage(c, "G_po", "dl")
            nc.all_engine_barrier()

            def cols(g):
                return ds(g * GT, GT)

            def attend(n, u, g, written):
                hi, lo = sh[u]
                src = slots[:, :, cols(g)]
                need(SC, G_ve, written)
                need(SC, G_pe, 2 * n - 3)
                A_sc.did("hi", SC.copy(hi[:, :, :], src))
                need(SC, A_pe, n - 1, "ss")
                settle(SC, spare[SC])
                A_sc.did("sq", SC.activation(sq[:, :, :], src, ACT.Square))
                need(VE, A_sc, n, "hi")
                A_ve.did("lo", VE.tensor_tensor(lo[:, :, :], src, hi[:, :, :], ALU.subtract))
                yield
                need(PE, A_sc, n, "sq")
                need(PE, A_sc, n - 1, "rr2")
                for t in range(TG):
                    for ch in range(DC):
                        mm = PE.matmul(ps[:, 4, t * P:t * P + P], sq[:, ch, t * P:t * P + P], ones[:, :],
                                       start=ch == 0, stop=ch == DC - 1)
                A_pe.did("ss", mm)
                need(VE, A_pe, n, "ss")
                need(VE, A_po, n - 1)
                A_ve.did("msq", VE.tensor_scalar(
                    msq[:, :].unsqueeze(2), ps[:, 4, :].rearrange("p (t n) -> p t n", n=P)[:, :, 0:1], 1.0 / D,
                    RMS_EPS, ALU.mult, ALU.add))
                need(PO, A_ve, n, "msq")
                need(PO, A_ve, n - 1, "diag")
                A_po.did("pow", PO.tensor_tensor(rms[:, :], msq[:, :], powh[:, 0:TG], ALU.pow))
                need(VE, A_po, n)
                need(VE, A_pe, n - 1, "rb2")
                A_ve.did("diag", VE.tensor_tensor(
                    diag[:, :, :], ident[:, :].unsqueeze(1).broadcast_to((P, TG, P)),
                    rms[:, :].unsqueeze(2).broadcast_to((P, TG, P)), ALU.mult))
                yield
                need(PE, A_ve, n, "diag")
                A_pe.did("rb", PE.matmul(ps[:, 5, :], ones[:, :], diag[:, :, :].rearrange("p t n -> p (t n)"),
                                         start=True, stop=True))
                need(PE, A_ve, n, "lo")
                need(PE, A_ve, n - 1, "sc")
                for k in range(BG):
                    m = ds((g * BG + k) * M, M)
                    w = [[kq[h][:, ch, m] for h in range(2)] for ch in range(DC)]
                    x = [[sh[u][h][:, ch, k * S:(k + 1) * S] for h in range(2)] for ch in range(DC)]
                    mm = three_passes(PE, ps[0:M, 6, k * S:(k + 1) * S], list(zip(w, x)))
                A_pe.did("sc", mm)
                need(SC, A_pe, n, "rb")
                need(SC, A_ve, n - 1, "an")
                A_sc.did("rr", SC.copy(rr[:, :], ps[:, 5, :]))
                need(VE, A_sc, n, "rr")
                need(VE, A_pe, n, "sc")
                need(VE, A_sc, n - 1, "e1")
                A_ve.did("sc", VE.scalar_tensor_tensor(sc[0:M, :, :].rearrange("p b n -> p (b n)"), ps[0:M, 6, :],
                                                       1 / WS, rr[0:M, :], ALU.mult, ALU.mult))
                need(VE, A_ve, n, "sc")
                A_ve.did("mx", VE.tensor_reduce(gmx[0:M, :], sc[0:M, :, :], AX, ALU.max))
                need(VE, A_ve, n, "mx")
                A_ve.did("neg", VE.tensor_scalar(gneg[0:M, :], gmx[0:M, :], -1.0, None, ALU.mult))
                need(SC, A_ve, n, "neg")
                need(SC, A_pe, n - 1, "cs")
                need(SC, A_ve, n - 1, "an")
                for k in range(BG):
                    A_sc.did(f"e{k}", SC.activation(ex[0:M, k, :], sc[0:M, k, :], ACT.Exp, bias=gneg[0:M, k:k + 1],
                                                    accum_out=gden[0:M, k:k + 1]))
                need(VE, A_sc, n, "e1")
                A_ve.did("grec", VE.reciprocal(grec[0:M, :], gden[0:M, :]))
                need(VE, A_ve, n, "grec")
                for k in range(BG):
                    A_ve.did(f"m{k}", VE.tensor_scalar(ex[0:M, k, :], ex[0:M, k, :], grec[0:M, k:k + 1], None,
                                                       ALU.mult))
                yield
                need(PE, A_ve, n, "m1")
                exf = ex[0:M, :, :].rearrange("p b n -> p (b n)")
                for t in range(TG):
                    mm = PE.matmul(ps[:, 4, t * P:t * P + P], exf[:, t * P:t * P + P], ones[0:M, :],
                                   start=True, stop=True)
                A_pe.did("cs", mm)
                need(VE, A_pe, n, "cs")
                A_ve.did("cse", VE.tensor_scalar(
                    cse[:, :].unsqueeze(2), ps[:, 4, :].rearrange("p (t n) -> p t n", n=P)[:, :, 0:1], SUM_EPS, None,
                    ALU.add))
                need(VE, A_ve, n, "cse")
                A_ve.did("crec", VE.reciprocal(crec[:, :], cse[:, :]))
                need(VE, A_ve, n, "crec")
                need(VE, A_pe, n, "rb")
                A_ve.did("diag2", VE.tensor_tensor(
                    diag[:, :, :], ident[:, :].unsqueeze(1).broadcast_to((P, TG, P)),
                    crec[:, :].unsqueeze(2).broadcast_to((P, TG, P)), ALU.mult))
                yield
                need(PE, A_ve, n, "diag2")
                need(PE, A_sc, n, "rr")
                A_pe.did("rb2", PE.matmul(ps[:, 5, :], ones[:, :], diag[:, :, :].rearrange("p t n -> p (t n)"),
                                          start=True, stop=True))
                need(SC, A_pe, n, "rb2")
                need(SC, A_ve, n, "sc")
                A_sc.did("rr2", SC.copy(rr[:, :], ps[:, 5, :]))
                need(VE, A_sc, n, "rr2")
                need(VE, A_sc, n - 1, "anh")
                A_ve.did("an", VE.tensor_tensor(an[0:M, :], exf, rr[0:M, :], ALU.mult))
                need(SC, A_ve, n, "an")
                need(SC, G_pe, 2 * n - 3)
                A_sc.did("anh", SC.copy(anh[u][0][0:M, :], an[0:M, :]))
                need(VE, A_sc, n, "anh")
                A_ve.did("anl", VE.tensor_tensor(anh[u][1][0:M, :], an[0:M, :], anh[u][0][0:M, :], ALU.subtract))
                yield

            def gate(n, u, g, bank, chunk, hidden, update):
                jobs = []
                if hidden:
                    jobs += [(whh[i][:, ch, chunk * P:chunk * P + P], sh[u][j][:, ch, :], ps[:, bank, :])
                             for ch in range(DC) for i, j in ((0, 0), (0, 1), (1, 0))]
                if update:
                    jobs += [(vw[i][0:M, ds(g * BG + k, 1), chunk * P:chunk * P + P].squeeze(1),
                              anh[u][j][0:M, k * S:(k + 1) * S], ps[:, bank, k * S:(k + 1) * S])
                             for k in range(BG) for i, j in ((0, 0), (0, 1), (1, 0))]
                for n_, (w, x, o) in enumerate(jobs):
                    first = n_ == 0
                    mm = PE.matmul(o, w, x, start=first, stop=n_ == len(jobs) - 1, skip_group_check=True)
                return mm

            def gru(n, u, g, weave):
                for ch in range(DC):
                    m = 2 * n + ch
                    need(PE, A_ve, n, "anl")
                    need(PE, G_sc, m - 1, "tr")
                    G_pe.did("r", gate(n, u, g, 0, ch, True, True))
                    need(PE, G_sc, m - 1, "tz")
                    G_pe.did("z", gate(n, u, g, 1, DC + ch, True, True))
                    next(weave, None)
                    need(PE, G_sc, m - 1, "hn")
                    G_pe.did("hn", gate(n, u, g, 2, 2 * DC + ch, True, False))
                    need(PE, G_ve, m - 1, "t2")
                    G_pe.did("xn", gate(n, u, g, 3, 2 * DC + ch, False, True))
                    need(SC, G_pe, m, "r")
                    need(SC, G_ve, m - 1, "t1")
                    G_sc.did("tr", SC.activation(tr_[:, :], ps[:, 0, :], ACT.Tanh, bias=b_tz[:, ch:ch + 1],
                                                 scale=0.5 / WS))
                    need(SC, G_pe, m, "z")
                    need(SC, G_ve, m - 1, "u")
                    G_sc.did("tz", SC.activation(tz[:, :], ps[:, 1, :], ACT.Tanh, bias=b_tz[:, DC + ch:DC + ch + 1],
                                                 scale=0.5 / WS))
                    need(SC, G_pe, m, "hn")
                    G_sc.did("hn", SC.activation(hn[:, :], ps[:, 2, :], ACT.Identity,
                                                 bias=bhh[:, 2 * DC + ch:2 * DC + ch + 1], scale=0.5 / WS))
                    need(VE, G_sc, m, "hn")
                    G_ve.did("t1", VE.scalar_tensor_tensor(t1[:, :], tr_[:, :], 1.0, hn[:, :], ALU.add, ALU.mult))
                    need(VE, G_pe, m, "xn")
                    need(VE, G_ve, m, "t1")
                    need(VE, G_sc, m - 1, "nn")
                    G_ve.did("t2", VE.scalar_tensor_tensor(t2[:, :], ps[:, 3, :], 1 / WS, t1[:, :], ALU.mult, ALU.add))
                    need(SC, G_ve, m, "t2")
                    need(SC, G_ve, m - 1, "out")
                    G_sc.did("nn", SC.activation(nn[:, :], t2[:, :], ACT.Tanh,
                                                 bias=bih[:, 2 * DC + ch:2 * DC + ch + 1]))
                    h = slots[:, ch, cols(g)]
                    need(PO, G_sc, m, "nn")
                    need(PO, G_ve, m - 1, "u")
                    G_po.did("dl", PO.tensor_tensor(dl[:, :], h, nn[:, :], ALU.subtract))
                    need(VE, G_po, m)
                    G_ve.did("u", VE.scalar_tensor_tensor(uu[:, :], tz[:, :], 1.0, dl[:, :], ALU.add, ALU.mult))
                    need(VE, G_ve, m, "u")
                    G_ve.did("out", VE.scalar_tensor_tensor(h, uu[:, :], 0.5, nn[:, :], ALU.mult, ALU.add))
                    next(weave, None)
                for _ in weave:
                    pass

            for _ in attend(0, 0, 0, -1):
                pass
            NSTEP = ITERS * NG

            def pair(n, g0, nxt, last=False):
                gru(n, 0, g0, attend(n + 1, 1, g0 + 1, 2 * (n + 1 - NG) + 1))
                gru(n + 1, 1, g0 + 1, iter(()) if last else attend(n + 2, 0, nxt, 2 * (n + 2 - NG) + 1))

            with nc.Fori(0, ITERS - 1) as it:
                with nc.Fori(0, NG // 2) as k:
                    pair(it * NG + k * 2, k * 2, 2 + k * -2)
            base = (ITERS - 1) * NG
            pair(base, 0, 2)
            pair(base + 2, 2, 0, last=True)
            nc.all_engine_barrier()

        with ExitStack() as c:
            gw = sb(c, "gw", [P, DC, E])
            gwh = [sb(c, f"gw_{i}", [P, DC, E], F16) for i in range(2)]
            gb = sb(c, "gb", [P, E])
            stg = sb(c, "stg", [P, DC, GT])
            y = sb(c, "y", [P, TG, D])
            st = sb(c, "st", [P, TG, 6])
            mv2 = sb(c, "mv2", [P, TG, 2])
            ve2 = sb(c, "ve2", [P, TG])
            rs2 = sb(c, "rs2", [P, TG])
            lg, pe_, pr, mx8, fi, w0 = (sb(c, k, [P, NT, E]) for k in ("lg", "pe_", "pr", "mx8", "fi", "w0"))
            hot = [sb(c, f"hot{k}", [P, NT, E]) for k in range(2)]
            both, before, cnt = (sb(c, k, [P, NT, E]) for k in ("both", "before", "cnt"))
            tri = sb(c, "tri", [P, P])
            ix8 = sb(c, "ix8", [P, NT, E], U32)
            s1, s2 = (sb(c, k, [P, NT]) for k in ("s1", "s2"))
            slot = sb(c, "slot", [P, 2, NT])
            total, tiles, first, ends = (sb(c, k, [P, E]) for k in ("total", "tiles", "first", "ends"))
            ramp_i = sb(c, "ramp_i", [P, NTILE], mybir.dt.int32)
            ramp = sb(c, "ramp", [P, NTILE])
            steps128 = sb(c, "steps128", [P, NT])
            cmp1 = sb(c, "cmp1", [P, E, NT])
            cmp2 = sb(c, "cmp2", [P, NTILE, E])
            te_f = sb(c, "te_f", [P, NTILE])
            ld = stage(c, "r_ld", unit=16)
            gcut = stage(c, "gcut", "hi", "lo")
            tri_s = stage(c, "tri_s", "ones", "cut", "ramp")
            line = stage(c, "r_line")
            nc.all_engine_barrier()
            SY.dma_start(gw[:, :, :], a["L0_ffn_gate_w"].rearrange("(c p) e -> p c e", p=P)).then_inc(ld.sem, 16)
            SY.dma_start(gb[:, :], a["L0_ffn_gate_b"].rearrange("(o d) -> o d", o=1).broadcast_to((P, E))).then_inc(
                ld.sem, 16)
            tri_s.did("ones", PO.memset(tri[:, :], 1.0))
            need(PO, tri_s, 0, "ones")
            tri_s.did("cut", PO.affine_select(out=tri[:, :], in_=tri[:, :], compare_op=ALU.is_gt, fill=0.0, base=0,
                                              pattern=[[1, P]], channel_multiplier=-1))
            tri_s.did("ramp", PO.iota(ramp_i[:, :], pattern=[[1, NTILE]], base=0, channel_multiplier=0))
            need(VE, ld, 1)
            gcut.did("hi", VE.tensor_scalar(gwh[0][:, :, :], gw[:, :, :], WS, None, ALU.mult))
            need(VE, gcut, 0, "hi")
            gcut.did("lo", VE.scalar_tensor_tensor(gwh[1][:, :, :], gw[:, :, :], WS, gwh[0][:, :, :], ALU.mult,
                                                   ALU.subtract))
            need(PE, gcut, 0)
            need(VE, gcut, 0)
            need(SC, gcut, 0)

            def bc(t, n=E):
                return t.unsqueeze(2).broadcast_to((P, t.shape[1], n))

            class Line:
                def __init__(self, start):
                    self.start, self.k = start, 0

                def run(self, engine, make, alone=False):
                    engine.wait_ge(line.sem, self.start + self.k + 1)
                    if alone:
                        settle(engine, spare[engine])
                    self.k += 1
                    line.did("done", make())

            def last_of(f, n):
                for t in range(n):
                    ins = f(t)
                return ins

            def second_norm(g):
                line_g = Line(g * NORM_STEPS)
                run = line_g.run
                tok = ds(g * TG, TG)
                run(SC, lambda: SC.copy(stg[:, :, :], slots[:, :, cols(g)]))

                def back():
                    for t in range(TG):
                        for ch in range(DC):
                            tr = PE.transpose(ps[:, t // 2, (t % 2) * D + ch * P:(t % 2) * D + ch * P + P],
                                              stg[:, ch, t * P:t * P + P], ident[:, :])
                    return tr
                run(PE, back)
                run(VE, lambda: VE.tensor_tensor(
                    y[:, :, :], ps[:, 0:2, :].rearrange("p b (t d) -> p (b t) d", d=D), xs[:, tok, :], ALU.add))
                run(VE, lambda: last_of(lambda t: VE.bn_stats(st[:, t, :], y[:, t, :]), TG), alone=True)
                run(VE, lambda: last_of(lambda t: VE.bn_aggr(mv2[:, t, :], st[:, t, :]), TG), alone=True)
                run(VE, lambda: VE.tensor_scalar(ve2[:, :].unsqueeze(2), mv2[:, :, 1:2], LN_EPS, None, ALU.add))
                run(PO, lambda: PO.tensor_tensor(rs2[:, :], ve2[:, :], powh[:, 0:TG], ALU.pow))
                run(VE, lambda: last_of(lambda t: VE.tensor_scalar(
                    y[:, t, :], y[:, t, :], mv2[:, t, 0:1], rs2[:, t:t + 1], ALU.subtract, ALU.mult), TG))

                def forth():
                    for ch in range(DC):
                        for t in range(TG):
                            tr = PE.transpose(ps[:, 2 + ch, t * P:t * P + P], y[:, t, ch * P:ch * P + P], ident[:, :])
                    return tr
                run(PE, forth)
                run(SC, lambda: SC.copy(xT[0][:, :, cols(g)], ps[:, 2:4, :]))
                run(VE, lambda: VE.tensor_tensor(xT[1][:, :, cols(g)], ps[:, 2:4, :], xT[0][:, :, cols(g)],
                                                 ALU.subtract))

                def gates():
                    for t in range(TG):
                        x = [[xT[h][:, ch, ds(g * GT + t * P, P)] for h in range(2)] for ch in range(DC)]
                        w = [[gwh[h][:, ch, :] for h in range(2)] for ch in range(DC)]
                        mm = three_passes(PE, ps[:, 4, t * E:t * E + E], list(zip(x, w)))
                    return mm
                run(PE, gates)
                run(VE, lambda: VE.scalar_tensor_tensor(
                    lg[:, tok, :], ps[:, 4, 0:TG * E].rearrange("p (t e) -> p t e", e=E), 1 / WS,
                    gb[:, :].unsqueeze(1).broadcast_to((P, TG, E)), ALU.mult, ALU.add))
                run(SC, lambda: SC.copy(xs[:, tok, :], y[:, :, :]))
                assert line_g.k == NORM_STEPS, line_g.k

            with nc.Fori(0, NG) as g:
                second_norm(g)
            route = Line(NG * NORM_STEPS)
            run = route.run
            run(VE, lambda: VE.tensor_reduce(s1[:, :], lg[:, :, :], AX, ALU.max))
            run(VE, lambda: VE.tensor_tensor(lg[:, :, :], lg[:, :, :], bc(s1[:, :]), ALU.subtract))
            run(SC, lambda: SC.activation(pe_[:, :, :], lg[:, :, :], ACT.Exp))
            run(VE, lambda: VE.tensor_reduce(s1[:, :], pe_[:, :, :], AX, ALU.add))
            run(VE, lambda: VE.reciprocal(s2[:, :], s1[:, :]))
            run(VE, lambda: VE.tensor_tensor(pr[:, :, :], pe_[:, :, :], bc(s2[:, :]), ALU.mult))
            run(VE, lambda: last_of(lambda t: VE.max(mx8[:, t, :], pr[:, t, :]), NT))
            run(VE, lambda: last_of(lambda t: VE.max_index(ix8[:, t, :], mx8[:, t, :], pr[:, t, :]), NT))
            run(VE, lambda: VE.tensor_copy(fi[:, :, :], ix8[:, :, :]))
            run(VE, lambda: last_of(lambda k: VE.tensor_tensor(
                hot[k][:, :, :], iota[:, :].unsqueeze(1).broadcast_to((P, NT, E)),
                fi[:, :, k:k + 1].broadcast_to((P, NT, E)), ALU.is_equal), 2))
            run(VE, lambda: VE.tensor_tensor(both[:, :, :], hot[0][:, :, :], hot[1][:, :, :], ALU.add))

            def counts():
                rhs = both[:, :, :].rearrange("p t e -> p (t e)")
                PE.matmul(ps[:, 0, 0:P], tri[:, :], rhs, start=True, stop=True)
                return PE.matmul(ps[:, 1, 0:P], ones[:, :], rhs, start=True, stop=True)
            need(PE, tri_s, 0)
            run(PE, counts)
            run(VE, lambda: VE.tensor_tensor(s1[:, :], mx8[:, :, 0], mx8[:, :, 1], ALU.add))
            run(VE, lambda: VE.tensor_scalar(s1[:, :], s1[:, :], TOP_EPS, None, ALU.add))
            run(VE, lambda: VE.reciprocal(s2[:, :], s1[:, :]))
            run(VE, lambda: last_of(lambda k: VE.tensor_tensor(top_w[:, k, :], mx8[:, :, k], s2[:, :], ALU.mult), 2))
            run(VE, lambda: VE.tensor_copy(cnt[:, :, :].rearrange("p t e -> p (t e)"), ps[:, 1, 0:P]))
            run(VE, lambda: VE.memset(before[:, 0, :], 0.0))
            for t in range(1, NT):
                run(VE, lambda: VE.tensor_tensor(before[:, t, :], before[:, t - 1, :], cnt[:, t - 1, :], ALU.add))
            run(VE, lambda: VE.tensor_tensor(total[:, :], before[:, NT - 1, :], cnt[:, NT - 1, :], ALU.add))
            need(VE, tri_s, 0)
            run(VE, lambda: VE.tensor_copy(ramp[:, :], ramp_i[:, :]))
            run(VE, lambda: VE.tensor_scalar(steps128[:, :], ramp[:, 0:NT], float(P), None, ALU.mult))
            run(VE, lambda: VE.tensor_tensor(cmp1[:, :, :], bc(total[:, :], NT),
                                             steps128[:, :].unsqueeze(1).broadcast_to((P, E, NT)), ALU.is_gt))
            run(VE, lambda: VE.tensor_reduce(tiles[:, :], cmp1[:, :, :], AX, ALU.add))
            run(VE, lambda: VE.tensor_copy(ends[:, 0:1], tiles[:, 0:1]))
            for e in range(1, E):
                run(VE, lambda: VE.tensor_tensor(ends[:, e:e + 1], ends[:, e - 1:e], tiles[:, e:e + 1], ALU.add))
            run(VE, lambda: VE.tensor_tensor(first[:, :], ends[:, :], tiles[:, :], ALU.subtract))
            run(VE, lambda: VE.tensor_scalar(first[:, :], first[:, :], float(P), None, ALU.mult))
            run(VE, lambda: VE.tensor_tensor(before[:, :, :], before[:, :, :],
                                             first[:, :].unsqueeze(1).broadcast_to((P, NT, E)), ALU.add))
            run(VE, lambda: VE.tensor_tensor(before[:, :, :].rearrange("p t e -> p (t e)"), ps[:, 0, 0:P],
                                             before[:, :, :].rearrange("p t e -> p (t e)"), ALU.add))
            for k in range(2):
                run(VE, lambda: VE.tensor_tensor(w0[:, :, :], hot[k][:, :, :], before[:, :, :], ALU.mult))
                run(VE, lambda: VE.tensor_reduce(slot[:, k, :], w0[:, :, :], AX, ALU.add))
            run(VE, lambda: VE.tensor_copy(idx0[:, :, :], slot[:, :, :]))
            run(VE, lambda: VE.tensor_tensor(cmp2[:, :, :], bc(ramp[:, :], E),
                                             ends[:, :].unsqueeze(1).broadcast_to((P, NTILE, E)), ALU.is_ge))
            run(VE, lambda: VE.tensor_reduce(te_f[:, :], cmp2[:, :, :], AX, ALU.add))
            run(VE, lambda: VE.tensor_scalar(te_f[:, :], te_f[:, :], float(E - 1), None, ALU.min))
            run(VE, lambda: VE.tensor_copy(tile_e[:, :], te_f[:, :]))
            nc.all_engine_barrier()
        mid.close()

        with ExitStack() as c:
            e1 = [sb(c, f"e1_{i}", [P, E, DC, I], F16) for i in range(2)]
            e2 = [sb(c, f"e2_{i}", [P, E, IC, D], F16) for i in range(2)]
            sw = sb(c, "sw", [P, 8 * I], F16)
            piece = [sb(c, f"piece{k}", [P, I]) for k in range(4)]
            work = sb(c, "work", [P, 4 * GT])
            b1s = sb(c, "b1s", [P, IC])
            b1e = sb(c, "b1e", [P, E, IC])
            b2s = sb(c, "b2s", [P, D])

            def half(t, k, n, dt=F16):
                v = t[:, :] if t.dtype == dt else t[:, :].bitcast(dt)
                return v[:, k * n:(k + 1) * n]
            s1c = [half(sw, i, 2 * I).rearrange("p (c n) -> p c n", c=DC) for i in range(2)]
            s2c = [half(sw, 2 + i, 2 * I).rearrange("p (c n) -> p c n", c=IC) for i in range(2)]
            hf = [half(work, k, GT, F32) for k in range(2)]
            hh = [[half(work, 4 + 2 * k + i, GT) for i in range(2)] for k in range(2)]
            b2e = half(sw, 1, 4 * I).bitcast(F32).rearrange("p (e d) -> p e d", e=E)
            zf = half(sw, 0, 2 * I).bitcast(F32)
            xg = [half(sw, 4 + u, 2 * D).bitcast(F32) for u in range(2)]
            xgT = [[half(sw, 12 + 2 * u + i, D).rearrange("p (c t) -> p c t", c=DC) for i in range(2)]
                   for u in range(2)]
            he = [[half(work, 2 * u + i, I).rearrange("p (k t) -> p k t", k=IC) for i in range(2)] for u in range(2)]
            yo = [sb(c, f"yo{u}", [P, D]) for u in range(2)]

            ld_p = [stage(c, f"ld_p{k}", unit=16) for k in range(4)]
            ld_b = stage(c, "ld_b", unit=16)
            cut_s = stage(c, "cut_s", "hi", "lo")
            cut_p = stage(c, "cut_p", "hi", "lo", ahead=5)
            scat = stage(c, "scat", unit=16, ahead=0)
            H_pe = stage(c, "H_pe")
            H_g = stage(c, "H_g", "gelu", "hi", ahead=2)
            H_lo = stage(c, "H_lo", ahead=2)
            O_pe = stage(c, "O_pe", *[f"{k}" for k in range(IC)], ahead=2)
            O_ev = stage(c, "O_ev", "base", "acc", ahead=2)
            nc.all_engine_barrier()

            need(PO, zeroed, 0)
            for k in range(2):
                for t in range(NT):
                    PO.indirect_dma_start(rows_x, bass.IndirectOffsetOnAxis(ap=idx0[:, k, t:t + 1], axis=0),
                                          xs[:, t, :], None).then_inc(scat.sem, 16)

            SY.dma_start(b1s[:, :], a["L0_ffn_sh_b1"].rearrange("(c p) -> p c", p=P),
                         allow_slow_non_contiguous=True).then_inc(ld_b.sem, 16)
            SY.dma_start(b2s[:, :], a["L0_ffn_sh_b2"].rearrange("(o d) -> o d", o=1).broadcast_to((P, D))).then_inc(
                ld_b.sem, 16)
            SY.dma_start(b1e[:, :, :].rearrange("p e c -> p (e c)"),
                         a["L0_ffn_eb1"].rearrange("e (c p) -> p (e c)", p=P),
                         allow_slow_non_contiguous=True).then_inc(ld_b.sem, 16)

            def piece_of(w1, w2, j):
                if j < DC:
                    return w1.rearrange("(c p) n -> p c n", p=P)[:, j, :]
                j -= DC
                return w2.rearrange("(c p) n -> p c n", p=P)[:, j * IC // 2:(j + 1) * IC // 2, :]

            def fetch(q, j, w1, w2):
                if not isinstance(q, int):
                    need(SY, cut_p, (q - 2) * 4 + j)
                dst = piece[j][:, :] if j < DC else piece[j][:, :].rearrange("p (c n) -> p c n", n=D)
                SY.dma_start(dst, piece_of(w1, w2, j)).then_inc(ld_p[j].sem, 16)

            def cut_piece(q, j, st, item, hi, lo):
                need(VE, ld_p[j], q)
                src = piece[j][:, :]
                st.did("hi", VE.tensor_scalar(hi, src, WS, None, ALU.mult))
                need(VE, st, item, "hi")
                st.did("lo", VE.scalar_tensor_tensor(lo, src, WS, hi, ALU.mult, ALU.subtract))

            def fetch_expert(e):
                for j in range(4):
                    fetch(e + 1, j, a["L0_ffn_ew1"][e], a["L0_ffn_ew2"][e])

            def cut_expert(e, j):
                flat = [[w[i][:, e, :, :].rearrange("p c n -> p (c n)") for i in range(2)] for w in (e1, e2)]
                hi, lo = (v[:, (j % 2) * I:(j % 2 + 1) * I] for v in flat[j // 2])
                cut_piece(e + 1, j, cut_p, e * 4 + j, hi, lo)

            for j in range(4):
                fetch(0, j, a["L0_ffn_sh_w1"], a["L0_ffn_sh_w2"])
            for j in range(4):
                k = j // 2 * 2
                hi, lo = (half(sw, 2 * (k + i) + j % 2, I) for i in range(2))
                cut_piece(0, j, cut_s, j, hi, lo)
            need(PE, cut_s, 3)
            need(SY, cut_s, 3)
            need(SC, ld_b, 2)
            need(VE, ld_b, 2)

            def shared(g):
                def up(k):
                    m = g * IC + k
                    need(PE, H_g, m - 2, "gelu")
                    w = [[s1c[h][:, ch, k * P:k * P + P] for h in range(2)] for ch in range(DC)]
                    x = [[xT[h][:, ch, cols(g)] for h in range(2)] for ch in range(DC)]
                    H_pe.did("done", three_passes(PE, ps[:, k % 2, :], list(zip(w, x))))
                    need(SC, H_pe, m)
                    need(SC, H_lo, m - 2)
                    H_g.did("gelu", SC.activation(hf[k % 2], ps[:, k % 2, :], ACT.Gelu_apprx_tanh,
                                                  bias=b1s[:, k:k + 1], scale=1 / WS))
                    need(SC, H_g, m, "gelu")
                    need(SC, O_pe, g if k >= 2 else g - 1, f"{(k - 2) % IC}")
                    H_g.did("hi", SC.copy(hh[k % 2][0], hf[k % 2]))
                    need(VE, H_g, m, "hi")
                    H_lo.did("done", VE.tensor_tensor(hh[k % 2][1], hf[k % 2], hh[k % 2][0], ALU.subtract))
                    cut_expert(g * 2 + k // 4, k % 4)

                def down(k):
                    m = g * IC + k
                    need(PE, H_lo, m)
                    if k == 0:
                        need(PE, O_ev, g - 1)
                    for t in range(TG):
                        o = ps[:, 4 + t, 0:D]
                        for n_, (i, j) in enumerate(((0, 0), (0, 1), (1, 0))):
                            mm = PE.matmul(o, hh[k % 2][i][:, t * P:t * P + P], s2c[j][:, k, :],
                                           start=k == 0 and n_ == 0, stop=k == IC - 1 and n_ == 2)
                    O_pe.did(f"{k}", mm)

                fetch_expert(g * 2)
                fetch_expert(g * 2 + 1)
                up(0)
                for k in range(1, IC):
                    up(k)
                    down(k - 1)
                down(IC - 1)
                x = xs[:, ds(g * TG, TG), :]
                O_ev.did("base", VE.scalar_tensor_tensor(x, x, 2.0, b2s[:, :].unsqueeze(1).broadcast_to((P, TG, D)),
                                                         ALU.mult, ALU.add))
                need(VE, O_pe, g)
                need(VE, O_ev, g, "base")
                O_ev.did("acc", VE.scalar_tensor_tensor(x, ps[:, 4:8, 0:D], 1 / WS, x, ALU.mult, ALU.add))

            need(VE, scat, 2 * NT - 1)
            with nc.Fori(0, NG) as g:
                shared(g)

            X_ld = [stage(c, f"X_ld{u}", unit=16) for u in range(2)]
            Y_st = [stage(c, f"Y_st{u}", unit=16) for u in range(2)]
            ld_b2 = stage(c, "ld_b2", unit=16)
            T_pe = stage(c, "T_pe", ahead=3)
            T_hi = stage(c, "T_hi", ahead=2)
            T_lo = stage(c, "T_lo", ahead=2)
            U_pe = stage(c, "U_pe", "0", "1", ahead=3)
            U_z = stage(c, "U_z", "0", "1", ahead=3)
            U_g = stage(c, "U_g", "g0", "g1", "hi", ahead=3)
            U_lo = stage(c, "U_lo", ahead=2)
            D_pe = stage(c, "D_pe", ahead=3)
            D_ev = stage(c, "D_ev", ahead=3)
            nc.all_engine_barrier()
            SY.dma_start(b2e, a["L0_ffn_eb2"].rearrange("(o e) d -> o e d", o=1).broadcast_to((P, E, D))).then_inc(
                ld_b2.sem, 16)
            need(VE, ld_b2, 0)
            rx = rows_x.rearrange("(t p) d -> t p d", p=P)
            ry = rows_y.rearrange("(t p) d -> t p d", p=P)

            def load_rows(i, u):
                need(SY, T_pe, i - 2)
                SY.dma_start(xg[u], rx[i]).then_inc(X_ld[u].sem, 16)

            def turn(i, u, half_i):
                need(PE, X_ld[u], half_i)
                need(PE, T_lo, i - 1)
                for ch in range(DC):
                    mm = PE.transpose(ps[:, 7, ch * P:ch * P + P], xg[u][:, ch * P:ch * P + P], ident[:, :])
                T_pe.did("done", mm)
                pv = ps[:, 7, 0:D].rearrange("p (c t) -> p c t", c=DC)
                need(SC, T_pe, i)
                need(SC, U_pe, i - 2)
                T_hi.did("done", SC.copy(xgT[u][0], pv))
                need(VE, T_hi, i)
                T_lo.did("done", VE.tensor_tensor(xgT[u][1], pv, xgT[u][0], ALU.subtract))

            def expert_of(i):
                return [e.value_load(tile_e[0:1, ds(i, 1)], min_val=0, max_val=E - 1) for e in (PE, VE)]

            def front(i, u, te, tv):
                need(PE, T_lo, i)
                for q in range(2):
                    need(PE, U_z, i - 2, str(q))
                    for k in range(4 * q, 4 * q + 4):
                        w = [[e1[h][:, ds(te, 1), ch, k * P:k * P + P].squeeze(1) for h in range(2)]
                             for ch in range(DC)]
                        x = [[xgT[u][h][:, ch, :] for h in range(2)] for ch in range(DC)]
                        mm = three_passes(PE, ps[:, 2 * u + q, (k % 4) * P:(k % 4) * P + P], list(zip(w, x)))
                    U_pe.did(str(q), mm)
                for q in range(2):
                    z = zf[:, q * GT:(q + 1) * GT]
                    need(VE, U_pe, i, str(q))
                    need(VE, U_lo, i - 1)
                    bias = b1e[:, ds(tv, 1), 4 * q:4 * q + 4].squeeze(1).unsqueeze(2).broadcast_to((P, 4, P))
                    U_z.did(str(q), VE.scalar_tensor_tensor(z.rearrange("p (k t) -> p k t", k=4),
                                                            ps[:, 2 * u + q, :].rearrange("p (k t) -> p k t", k=4),
                                                            1 / WS, bias, ALU.mult, ALU.add))
                    need(SC, U_z, i, str(q))
                    U_g.did(f"g{q}", SC.activation(z, z, ACT.Gelu_apprx_tanh))
                zz = zf.rearrange("p (k t) -> p k t", k=IC)
                need(SC, U_g, i, "g1")
                need(SC, D_pe, i - 2)
                U_g.did("hi", SC.copy(he[u][0], zz))
                need(VE, U_g, i)
                U_lo.did("done", VE.tensor_tensor(he[u][1], zz, he[u][0], ALU.subtract))

            def back(i, u, half_i, te, tv):
                need(PE, U_lo, i)
                need(PE, D_ev, i - 2)
                h = [[he[u][j][:, k, :] for j in range(2)] for k in range(IC)]
                w = [[e2[j][:, ds(te, 1), k, :].squeeze(1) for j in range(2)] for k in range(IC)]
                D_pe.did("done", three_passes(PE, ps[:, 4 + u, 0:D], list(zip(h, w))))
                need(VE, D_pe, i)
                need(VE, Y_st[u], half_i - 1)
                D_ev.did("done", VE.scalar_tensor_tensor(yo[u][:, :], ps[:, 4 + u, 0:D], 1 / WS,
                                                         b2e[:, ds(tv, 1), :].squeeze(1), ALU.mult, ALU.add))
                need(SY, D_ev, i)
                SY.dma_start(ry[i], yo[u][:, :]).then_inc(Y_st[u].sem, 16)

            need(PE, cut_p, 4 * E - 1)
            load_rows(0, 0)
            load_rows(1, 1)
            turn(0, 0, 0)
            front(0, 0, *expert_of(0))
            turn(1, 1, 0)

            def expert_step(i, u, half_i):
                this, following = expert_of(i), expert_of(i + 1)
                load_rows(i + 2, u)
                front(i + 1, 1 - u, *following)
                turn(i + 2, u, half_i + 1)
                back(i, u, half_i, *this)

            with nc.Fori(0, NTILE // 2 - 1) as h:
                expert_step(h * 2, 0, h)
                expert_step(h * 2 + 1, 1, h)
            i = NTILE - 3
            expert_step(i, 0, i // 2)
            this, following = expert_of(i + 1), expert_of(i + 2)
            front(i + 2, 0, *following)
            back(i + 1, 1, i // 2, *this)
            back(i + 2, 0, i // 2 + 1, *following)

            gat = [stage(c, f"gat{k}", unit=16, ahead=0) for k in range(4)]
            C_ve = stage(c, "C_ve")
            nc.all_engine_barrier()
            need(PO, Y_st[0], NTILE // 2)
            need(PO, Y_st[1], NTILE // 2 - 1)
            for n in range(2 * NT):
                t, k = n // 2, n % 2
                buf = piece[n % 4][:, 0:D]
                need(PO, C_ve, n - 4)
                PO.indirect_dma_start(buf, None, rows_y,
                                      bass.IndirectOffsetOnAxis(ap=idx0[:, k, t:t + 1], axis=0)).then_inc(
                    gat[n % 4].sem, 16)
                need(VE, gat[n % 4], n // 4)
                need(VE, C_ve, n - 1)
                C_ve.did("done", VE.scalar_tensor_tensor(xs[:, t, :], buf, top_w[:, k, t:t + 1], xs[:, t, :],
                                                         ALU.mult, ALU.add))
            nc.all_engine_barrier()

        with ExitStack() as c:
            st = sb(c, "st3", [P, NT, 6])
            mv3 = sb(c, "mv3", [P, NT, 2])
            ve3 = sb(c, "ve3", [P, NT])
            rs3 = sb(c, "rs3", [P, NT])
            p3 = sb(c, "p3", [P, NT])
            f_ve = stage(c, "f_ve", "st", "ag")
            f_v1 = stage(c, "f_v1", "pow0", "eps")
            f_po = stage(c, "f_po")
            f_out = stage(c, "f_out")
            stored = stage(c, "stored", unit=16)
            nc.all_engine_barrier()
            f_v1.did("pow0", VE.memset(p3[:, :], -0.5))
            for t in range(NT):
                f_ve.did("st", VE.bn_stats(st[:, t, :], xs[:, t, :]))
                need(VE, f_ve, t, "st")
                f_ve.did("ag", VE.bn_aggr(mv3[:, t, :], st[:, t, :]))
            need(VE, f_ve, NT - 1)
            f_v1.did("eps", VE.tensor_scalar(ve3[:, :].unsqueeze(2), mv3[:, :, 1:2], LN_EPS, None, ALU.add))
            need(PO, f_v1, 0)
            f_po.did("done", PO.tensor_tensor(rs3[:, :], ve3[:, :], p3[:, :], ALU.pow))
            need(VE, f_po, 0)
            ov = out.rearrange("b (t p) d -> p (b t) d", p=P)
            for t in range(NT):
                f_out.did("done", VE.tensor_scalar(xs[:, t, :], xs[:, t, :], mv3[:, t, 0:1], rs3[:, t:t + 1],
                                                   ALU.subtract, ALU.mult))
                if t % 4 == 3:
                    need(SY, f_out, t)
                    SY.dma_start(ov[:, t - 3:t + 1, :], xs[:, t - 3:t + 1, :]).then_inc(stored.sem, 16)
            need(SY, stored, NT // 4 - 1)


NORM_STEPS = 14


_INS = ['x', 'ctx_1024', 'L0_attn_Wq', 'L0_attn_Wk', 'L0_attn_Wv', 'L0_attn_Wo', 'L0_attn_bo',
        'L0_xattn_Wq', 'L0_xattn_Wk', 'L0_xattn_Wv', 'L0_xattn_gru_wih', 'L0_xattn_gru_whh',
        'L0_xattn_gru_bih', 'L0_xattn_gru_bhh', 'L0_xattn_slot_norm_w', 'L0_xattn_input_norm_w',
        'L0_ffn_gate_w', 'L0_ffn_gate_b', 'L0_ffn_sh_w1', 'L0_ffn_sh_b1', 'L0_ffn_sh_w2', 'L0_ffn_sh_b2',
        'L0_ffn_ew1', 'L0_ffn_eb1', 'L0_ffn_ew2', 'L0_ffn_eb2']
_OUT = ((8, 256, 256), 'float32')


def kernel(**inputs):
    import numpy as _np
    import concourse.bacc as _bacc
    from concourse.bass_utils import run_bass_kernel_spmd as _run

    nc = _bacc.Bacc("TRN2", target_bir_lowering=False, num_devices=1)
    arrays, args = {}, {}
    for name in _INS:
        v = _np.ascontiguousarray(inputs[name])
        arrays[f"in_{name}"] = v
        args[name] = nc.dram_tensor(f"in_{name}", v.shape, mybir.dt.from_np(v.dtype), kind="ExternalInput").ap()
    out = nc.dram_tensor("out_0", _OUT[0], mybir.dt.from_np(_np.dtype(_OUT[1])), kind="ExternalOutput").ap()
    decoder_layer(nc, args, out)
    r = _run(nc, [arrays], core_ids=[0])
    return r.results[0]["out_0"]
```

```python
from contextlib import ExitStack

import concourse.bass as bass
from concourse import mybir

F32 = mybir.dt.float32
F16 = mybir.dt.float16
BF16 = mybir.dt.bfloat16
U32 = mybir.dt.uint32
ALU = mybir.AluOpType
ACT = mybir.ActivationFunctionType
AX = mybir.AxisListType.X
ds = bass.ds

P = 128
WS = 64.0
LN_EPS = 1e-5
RMS_EPS = 1e-6
SUM_EPS = 1e-6
TOP_EPS = 1e-9


class Stage:

    def __init__(self, nc, ctx, name, steps=("done",), unit=1, ahead=1):
        self.sem = ctx.enter_context(nc.semaphore(name))
        self.steps, self.unit, self.ahead = list(steps), unit, ahead
        if ahead:
            nc.gpsimd.sem_inc(self.sem, unit * len(self.steps) * ahead)

    def did(self, step, instruction):
        assert step in self.steps
        instruction.then_inc(self.sem, self.unit)

    def at(self, item, step=None):
        i = len(self.steps) - 1 if step is None else self.steps.index(step)
        return item * (self.unit * len(self.steps)) + self.unit * (len(self.steps) * self.ahead + i + 1)


def need(engine, stage, item, step=None):
    value = stage.at(item, step)
    if isinstance(value, int) and value <= 0:
        return
    engine.wait_ge(stage.sem, value)


def settle(engine, spare):
    engine.sem_inc(spare, 1)


def three_passes(pe, out, pairs, **kw):
    products = [(w[i], a[j]) for w, a in pairs for i, j in ((0, 0), (0, 1), (1, 0))]
    for n, (w, a) in enumerate(products):
        last = pe.matmul(out, w, a, start=n == 0, stop=n == len(products) - 1, **kw)
    return last


def decoder_layer(nc, a, out):
    PE, SC, VE, PO, SY = nc.tensor, nc.scalar, nc.vector, nc.gpsimd, nc.sync
    NB, S, D = a["x"].shape
    M = a["ctx_1024"].shape[1]
    INNER = a["L0_attn_Wq"].shape[1]
    HD = 64
    E, _, I = a["L0_ffn_ew1"].shape
    T = NB * S
    NT, DC, IC = T // P, D // P, I // P
    PAIRS = INNER // P
    G3 = 3 * D
    GT = 512
    NG = T // GT
    BG = GT // S
    ITERS = 3
    TG = GT // P
    NTILE = 2 * T // P + E - 1
    SCALE = float(HD) ** -0.5
    XSCALE = float(D) ** -0.5
    top = ExitStack()
    with top:
        def sb(ctx, name, shape, dt=F32):
            return ctx.enter_context(nc.sbuf_tensor(name, shape, dt))

        ps = top.enter_context(nc.psum_tensor("ps", [P, 8, 512], F32))

        def stage(ctx, name, *steps, unit=1, ahead=1):
            return Stage(nc, ctx, name, steps or ("done",), unit, ahead)

        spare = {e: top.enter_context(nc.semaphore(f"spare_{k}")) for e, k in ((SC, "sc"), (VE, "ve"))}

        ident = sb(top, "ident", [P, P])
        ones = sb(top, "ones", [P, P])
        maskf = sb(top, "maskf", [P, P])
        mask = sb(top, "mask", [P, P], BF16)
        identb = sb(top, "identb", [P, P], BF16)
        powh = sb(top, "powh", [P, 8])
        iota = sb(top, "iota", [P, E])
        iotai = sb(top, "iotai", [P, E], mybir.dt.int32)
        xs = sb(top, "xs", [P, NT, D])
        xT = [sb(top, f"xT{i}", [P, DC, T], F16) for i in range(2)]
        idx0 = sb(top, "idx0", [P, 2, NT], mybir.dt.int32)
        top_w = sb(top, "top_w", [P, 2, NT])
        tile_e = sb(top, "tile_e", [P, NTILE], mybir.dt.int32)
        mid = top.enter_context(ExitStack())
        rows_x = nc.dram_tensor("rows_x", [NTILE * P, D], F32, kind="Internal").ap()
        rows_y = nc.dram_tensor("rows_y", [NTILE * P, D], F32, kind="Internal").ap()
        zrow = sb(mid, "zrow", [P, D])

        const = stage(top, "const", "ident0", "mask0", "ones", "ident", "mask", "powh", "iota")
        constv = stage(top, "constv", "mask", "identb", "iota")
        nc.all_engine_barrier()
        const.did("ident0", PO.memset(ident[:, :], 0.0))
        const.did("mask0", PO.memset(maskf[:, :], 0.0))
        const.did("ones", PO.memset(ones[:, :], 1.0))
        need(PO, const, 0, "ones")
        const.did("ident", PO.affine_select(out=ident[:, :], in_=ident[:, :], compare_op=ALU.not_equal, fill=1.0,
                                            base=0, pattern=[[-1, P]], channel_multiplier=1))
        const.did("mask", PO.affine_select(out=maskf[:, :], in_=maskf[:, :], compare_op=ALU.is_ge,
                                           fill=-1e9 / SCALE, base=0, pattern=[[-1, P]], channel_multiplier=1))
        const.did("powh", PO.memset(powh[:, :], -0.5))
        const.did("iota", PO.iota(iotai[:, :], pattern=[[1, E]], base=0, channel_multiplier=0))
        zrow_s = stage(top, "zrow_s")
        zeroed = stage(top, "zeroed", unit=16)
        zrow_s.did("done", PO.memset(zrow[:, :], 0.0))
        need(VE, const, 0)
        constv.did("mask", VE.tensor_copy(mask[:, :], maskf[:, :]))
        constv.did("identb", VE.tensor_copy(identb[:, :], ident[:, :]))
        constv.did("iota", VE.tensor_copy(iota[:, :], iotai[:, :]))

        with ExitStack() as c:
            wqkv = [sb(c, f"wqkv{i}", [P, DC, 3, INNER], F16) for i in range(2)]
            wo = [sb(c, f"wo{i}", [P, PAIRS, D], F16) for i in range(2)]
            wst = [sb(c, f"wst{i}", [P, DC, INNER]) for i in range(2)]
            xin = [sb(c, f"xin{i}", [P, S // P, D]) for i in range(2)]
            bo = sb(c, "bo", [P, D])
            qpad = sb(c, "qpad", [P, 2, S])
            kT = sb(c, "kT", [P, S])
            v_sb = [sb(c, f"v{i}", [P, S // P, P]) for i in range(2)]
            prob = sb(c, "prob", [P, 2, 384])
            pT = sb(c, "pT", [P, 2, 384])
            oT = [sb(c, f"oT{i}", [P, PAIRS, S], F16) for i in range(2)]
            mx = sb(c, "mx", [P, 2, 2])
            nmx = sb(c, "nmx", [P, 2, 2])
            den = sb(c, "den", [P, 2, 2])
            rden = sb(c, "rden", [P, 2, 2])
            bst = sb(c, "bst", [P, 2, 6])
            mv = sb(c, "mv", [P, 2, 2])
            ve = sb(c, "ve", [P, 2])
            rstd = sb(c, "rstd", [P, 2])

            ld_w = [stage(c, f"ld_w{i}", unit=16) for i in range(2)]
            ld_x = [stage(c, f"ld_x{i}", unit=16) for i in range(2)]
            ld_xs = stage(c, "ld_xs", unit=16)
            ld_bo = stage(c, "ld_bo", unit=16)
            w_cut = stage(c, "w_cut", "hi", "lo")
            x_tr = stage(c, "x_tr", ahead=2)
            x_hi = stage(c, "x_hi", ahead=2)
            x_lo = stage(c, "x_lo", ahead=2)
            bo_add = stage(c, "bo_add")
            zero = stage(c, "zero", "qpad", "oT_hi", "oT_lo")
            nc.all_engine_barrier()

            SY.dma_start(xs[:, :, :], a["x"].rearrange("b (t p) d -> p (b t) d", p=P)).then_inc(ld_xs.sem, 16)
            bo_row = a["L0_attn_bo"].rearrange("(o d) -> o d", o=1)
            SY.dma_start(bo[:, :], bo_row.broadcast_to((P, D))).then_inc(ld_bo.sem, 16)
            zero.did("qpad", VE.memset(qpad[:, :, :], 0.0))
            srcs = [a[f"L0_attn_W{k}"].rearrange("(c p) n -> p c n", p=P) for k in "qkv"]
            srcs.append(a["L0_attn_Wo"].rearrange("(s p) n -> p s n", p=P))
            for n, src in enumerate(srcs):
                need(SC, w_cut, n - 2)
                st = wst[n % 2]
                dst = st[:, :, :] if n < 3 else st[:, :, :].rearrange("p c n -> p (c n)").rearrange(
                    "p (s n) -> p s n", s=PAIRS)
                SC.dma_start(dst, src).then_inc(ld_w[n % 2].sem, 16)
            for n in range(4):
                need(VE, ld_w[n % 2], n // 2)
                st = wst[n % 2]
                if n < 3:
                    hi, lo, src = wqkv[0][:, :, n, :], wqkv[1][:, :, n, :], st[:, :, :]
                else:
                    src = st[:, :, :].rearrange("p c n -> p (c n)")
                    hi, lo = (w[:, :, :].rearrange("p s n -> p (s n)") for w in wo)
                w_cut.did("hi", VE.tensor_scalar(hi, src, WS, None, ALU.mult))
                need(VE, w_cut, n, "hi")
                w_cut.did("lo", VE.scalar_tensor_tensor(lo, src, WS, hi, ALU.mult, ALU.subtract))
            need(PO, ld_xs, 0)
            need(PO, ld_bo, 0)
            bo_add.did("done", PO.tensor_tensor(
                xs[:, :, :], xs[:, :, :], bo[:, :].unsqueeze(1).broadcast_to((P, NT, D)), ALU.add))

            need(PE, const, 0, "ident")
            xv = a["x"].rearrange("b (t p) d -> b p t d", p=P)
            with nc.Fori(0, NB // 2) as i:
                for u in range(2):
                    b = i * 2 + u
                    need(SY, x_tr, b - 2)
                    SY.dma_start(xin[u][:, :, :], xv[b]).then_inc(ld_x[u].sem, 16)
                    need(PE, ld_x[u], i)
                    need(PE, x_lo, b - 2)
                    need(PE, x_hi, b - 2)
                    for ch in range(DC):
                        for t in range(S // P):
                            tr = PE.transpose(ps[:, u, ch * S + t * P:ch * S + t * P + P],
                                              xin[u][:, t, ch * P:ch * P + P], ident[:, :])
                    x_tr.did("done", tr)
                    pv = ps[:, u, :].rearrange("p (c t) -> p c t", c=DC)
                    need(SC, x_tr, b)
                    x_hi.did("done", SC.copy(xT[0][:, :, ds(b * S, S)], pv))
                    need(VE, x_hi, b)
                    x_lo.did("done", VE.tensor_tensor(xT[1][:, :, ds(b * S, S)], pv,
                                                      xT[0][:, :, ds(b * S, S)], ALU.subtract))

            need(SY, zrow_s, 0)
            SY.dma_start(rows_x.rearrange("(t p) d -> p t d", p=P),
                         zrow[:, :].unsqueeze(1).broadcast_to((P, NTILE, D))).then_inc(zeroed.sem, 16)

            qk_mm = stage(c, "qk_mm")
            v_mm = stage(c, "v_mm")
            s_mm = stage(c, "s_mm")
            pt_mm = stage(c, "pt_mm")
            o_mm = stage(c, "o_mm")
            y_mm = stage(c, "y_mm")
            qkv_ev = stage(c, "qkv_ev", "k", "q0", "q1")
            v_ev = stage(c, "v_ev")
            smax = stage(c, "smax", "q0", "q1", "neg")
            expo = stage(c, "expo", "h0q0", "h0q1", "h1q0", "h1q1")
            norm = stage(c, "norm", "recip", "h0q0", "h0q1", "h1q0", "h1q1")
            pt_ev = stage(c, "pt_ev")
            o_ev = stage(c, "o_ev", "hi", "lo")
            ln = stage(c, "ln", "add", "st0", "st1", "ag0", "ag1", "eps", "out0", "out1", ahead=2)
            ln_pow = stage(c, "ln_pow")
            nc.all_engine_barrier()

            def project(n, b, p, y_read):
                cols = ds(p * P, P)
                need(PE, qkv_ev, n - 1)
                need(PE, ln, y_read, "add")
                for k in range(2):
                    w = [[wqkv[h][:, ch, k, cols] for h in range(2)] for ch in range(DC)]
                    x = [[xT[h][:, ch, ds(b * S, S)] for h in range(2)] for ch in range(DC)]
                    mm = three_passes(PE, ps[:, 0, k * S:(k + 1) * S], list(zip(w, x)))
                qk_mm.did("done", mm)
                need(PE, v_ev, n - 1)
                for t in range(S // P):
                    x = [[xT[h][:, ch, ds(b * S + t * P, P)] for h in range(2)] for ch in range(DC)]
                    w = [[wqkv[h][:, ch, 2, cols] for h in range(2)] for ch in range(DC)]
                    mm = three_passes(PE, ps[:, 1, t * P:(t + 1) * P], list(zip(x, w)))
                v_mm.did("done", mm)

            def project_out(n):
                need(SC, qk_mm, n)
                need(SC, s_mm, n - 1)
                qkv_ev.did("k", SC.mul(kT[:, :], ps[:, 0, S:2 * S], 1 / WS))
                for h in range(2):
                    r = slice(HD * h, HD * h + HD)
                    qkv_ev.did(f"q{h}", SC.mul(qpad[r, h, :], ps[r, 0, 0:S], 1 / WS))

            def values_out(n, u):
                need(VE, v_mm, n)
                need(VE, o_mm, n - 2)
                v_ev.did("done", VE.tensor_scalar(v_sb[u][:, :, :], ps[:, 1, 0:S].rearrange("p (t n) -> p t n", n=P),
                                                  1 / WS, None, ALU.mult))

            def scores(m, u):
                need(PE, qkv_ev, m)
                need(PE, expo, m - 2)
                bank = (2, 6)[u]
                for h in range(2):
                    for t in range(2):
                        o = ps[:, bank + h, 0:P] if t == 0 else ps[:, bank + h, P:3 * P]
                        PE.matmul(o, qpad[:, h, t * P:t * P + P], kT[:, 0:(t + 1) * P], start=True, stop=False)
                        mm = PE.matmul(ps[:, bank + h, 2 * P * t:2 * P * t + P], identb[:, :], mask[:, :],
                                       start=False, stop=True)
                s_mm.did("done", mm)

            def maxima(m, u):
                sv = ps[:, 2:4, :] if u == 0 else ps[:, 6:8, :]
                need(VE, s_mm, m)
                need(VE, expo, m - 1)
                smax.did("q0", VE.tensor_reduce(mx[:, :, 0:1], sv[:, :, 0:P], AX, ALU.max))
                smax.did("q1", VE.tensor_reduce(mx[:, :, 1:2], sv[:, :, P:3 * P], AX, ALU.max))
                need(VE, smax, m, "q1")
                smax.did("neg", VE.tensor_scalar(nmx[:, :, :], mx[:, :, :], -SCALE, None, ALU.mult))

            def exponentials(m, u, h):
                sv = ps[:, 2:4, :] if u == 0 else ps[:, 6:8, :]
                if h == 0:
                    need(SC, smax, m)
                    need(SC, pt_mm, m - 1)
                    need(SC, norm, m - 1)
                for t in range(2):
                    r = slice(0, P) if t == 0 else slice(P, 3 * P)
                    expo.did(f"h{h}q{t}", SC.activation(prob[:, h, r], sv[:, h, r], ACT.Exp,
                                                        bias=nmx[:, h, t:t + 1], scale=SCALE,
                                                        accum_out=den[:, h, t:t + 1]))

            def normalise(m):
                need(VE, expo, m)
                norm.did("recip", VE.reciprocal(rden[:, :, :], den[:, :, :]))
                need(VE, norm, m, "recip")
                for h in range(2):
                    for t in range(2):
                        r = slice(0, P) if t == 0 else slice(P, 3 * P)
                        norm.did(f"h{h}q{t}", VE.tensor_scalar(prob[:, h, r], prob[:, h, r], rden[:, h, t:t + 1],
                                                               None, ALU.mult))

            def transpose_prob(m):
                need(PE, norm, m)
                need(PE, pt_ev, m - 1)
                need(PE, o_ev, m - 1)
                for h in range(2):
                    for blk in range(3):
                        mm = PE.transpose(ps[:, 4 + h, blk * P:blk * P + P], prob[:, h, blk * P:blk * P + P],
                                          ident[:, :])
                pt_mm.did("done", mm)
                need(VE, pt_mm, m)
                need(VE, o_mm, m - 1)
                pt_ev.did("done", VE.tensor_copy(pT[:, :, :], ps[:, 4:6, 0:384]))

            def weigh_values(m, u, slot, batch):
                need(PE, pt_ev, m)
                need(PE, v_ev, m)
                need(PE, o_ev, m - 1)
                for t, key, cols_ in ((0, 0, 0), (1, 0, P), (1, 1, 2 * P)):
                    for h in range(2):
                        r = slice(HD * h, HD * h + HD)
                        mm = PE.matmul(ps[r, 4 + t, 384:512], v_sb[u][:, key, r], pT[:, h, cols_:cols_ + P],
                                       start=key == 0, stop=key == t, skip_group_check=True)
                o_mm.did("done", mm)
                need(VE, o_mm, m)
                need(VE, y_mm, batch - 1)
                hi, lo = (o[:, slot, :].rearrange("p (t q) -> p t q", t=2) for o in oT)
                o_ev.did("hi", VE.tensor_copy(hi, ps[:, 4:6, 384:512]))
                need(VE, o_ev, m, "hi")
                o_ev.did("lo", VE.tensor_tensor(lo, ps[:, 4:6, 384:512], hi, ALU.subtract))

            def output_projection(b, last_item, projected):
                need(PE, o_ev, last_item)
                need(PE, qkv_ev, projected)
                for t in range(2):
                    o = [[oT[h][:, s, t * P:t * P + P] for h in range(2)] for s in range(PAIRS)]
                    w = [[wo[h][:, s, :] for h in range(2)] for s in range(PAIRS)]
                    mm = three_passes(PE, ps[:, 0, t * D:t * D + D], list(zip(o, w)))
                y_mm.did("done", mm)
                need(VE, y_mm, b)
                y = xs[:, ds(b * 2, 2), :] if not isinstance(b, int) else xs[:, 2 * b:2 * b + 2, :]
                tile = [xs[:, b * 2 + t, :] for t in range(2)]
                need(VE, ln, b - 1)
                need(VE, ln_pow, b - 1)
                ln.did("add", VE.scalar_tensor_tensor(y, ps[:, 0, :].rearrange("p (t n) -> p t n", n=D), 1 / WS, y,
                                                      ALU.mult, ALU.add))
                need(VE, ln, b, "add")
                settle(VE, spare[VE])
                for t in range(2):
                    ln.did(f"st{t}", VE.bn_stats(bst[:, t, :], tile[t]))
                need(VE, ln, b, "st1")
                settle(VE, spare[VE])
                for t in range(2):
                    ln.did(f"ag{t}", VE.bn_aggr(mv[:, t, :], bst[:, t, :]))
                need(VE, ln, b, "ag1")
                ln.did("eps", VE.tensor_scalar(ve[:, :].unsqueeze(2), mv[:, :, 1:2], LN_EPS, None, ALU.add))
                need(PO, ln, b, "eps")
                ln_pow.did("done", PO.tensor_tensor(rstd[:, :], ve[:, :], powh[:, 0:2], ALU.pow))
                need(VE, ln_pow, b)
                for t in range(2):
                    ln.did(f"out{t}", VE.tensor_scalar(tile[t], tile[t], mv[:, t, 0:1], rstd[:, t:t + 1],
                                                       ALU.subtract, ALU.mult))

            def step(n, u, b, p, qkv=True, mid=True, pv=True, pv_slot=None, pv_batch=None, y_read=-1):
                if mid:
                    scores(n - 1, 1 - u)
                    maxima(n - 1, 1 - u)
                if pv:
                    transpose_prob(n - 2)
                if qkv:
                    project(n, b, p, y_read)
                if mid:
                    exponentials(n - 1, 1 - u, 0)
                if qkv:
                    project_out(n)
                if mid:
                    exponentials(n - 1, 1 - u, 1)
                if pv:
                    weigh_values(n - 2, u, pv_slot, pv_batch)
                if qkv:
                    values_out(n, u)
                if mid:
                    normalise(n - 1)

            need(PE, w_cut, 3)
            need(PE, constv, 0)
            need(PE, zero, 0, "qpad")
            need(VE, bo_add, 0)
            need(PE, x_lo, NB - 1)

            def inner(b):
                with nc.Fori(1, PAIRS // 2) as k:
                    for u in range(2):
                        step(b * PAIRS + k * 2 + u, u, b, k * 2 + u, pv_slot=k * 2 + (u - 2), pv_batch=b, y_read=b - 1)

            step(0, 0, 0, 0, mid=False, pv=False)
            step(1, 1, 0, 1, pv=False)
            inner(0)
            with nc.Fori(1, NB) as b:
                for u in range(2):
                    step(b * PAIRS + u, u, b, u, pv_slot=PAIRS - 2 + u, pv_batch=b - 1, y_read=b - 2)
                output_projection(b - 1, b * PAIRS - 1, b * PAIRS + 1)
                inner(b)
            N = NB * PAIRS
            step(N, 0, None, None, qkv=False, pv_slot=PAIRS - 2, pv_batch=NB - 1)
            step(N + 1, 1, None, None, qkv=False, mid=False, pv_slot=PAIRS - 1, pv_batch=NB - 1)
            output_projection(NB - 1, N - 1, N - 1)
            nc.all_engine_barrier()

        slots = sb(mid, "slots", [P, DC, T])
        with ExitStack() as c:
            whh = [sb(c, f"whh{i}", [P, DC, G3], F16) for i in range(2)]
            vw = [sb(c, f"vw{i}", [P, NB, G3], F16) for i in range(2)]
            kq = [sb(c, f"kq{i}", [P, DC, NB * M], F16) for i in range(2)]
            b_tz = sb(c, "b_tz", [P, 6])
            bih = sb(c, "bih", [P, 6])
            bhh = sb(c, "bhh", [P, 6])
            with ExitStack() as q:
                wk, wq, wv = (sb(q, f"x_{k}", [P, DC, D]) for k in ("wk", "wq", "wv"))
                wn = [sb(q, f"gw{i}", [P, G3 // P, D]) for i in range(2)]
                wihT = sb(q, "wihT", [P, DC, G3])
                whhT = sb(q, "whhT", [P, DC, G3])
                wa = sb(q, "wa", [P, DC, D])
                wb = sb(q, "wb", [P, DC, G3])
                ctxt = sb(q, "ctxt", [P, NB, D])
                pnT = sb(q, "pnT", [P, DC, NB * M])
                kqf = sb(q, "kqf", [P, NB * M])
                sqc = sb(q, "sqc", [P, D])
                ssc = sb(q, "ssc", [P, NB])
                rc = sb(q, "rc", [P, NB])
                nw = sb(q, "nw", [P, 2, DC])
                snw = sb(q, "snw", [P, DC])
                ld = stage(q, "x_ld", unit=16)
                line = stage(q, "x_line")
                V_pe = stage(q, "V_pe")
                V_ve = stage(q, "V_ve", "hi", "lo")
                X_pe = stage(q, "X_pe")
                X_cp = stage(q, "X_cp")
                nc.all_engine_barrier()
                loads = [
                    (wk[:, :, :], a["L0_xattn_Wk"].rearrange("(c p) n -> p c n", p=P)),
                    (wq[:, :, :], a["L0_xattn_Wq"].rearrange("(c p) n -> p c n", p=P)),
                    (wv[:, :, :], a["L0_xattn_Wv"].rearrange("(c p) n -> p c n", p=P)),
                    (wn[0][:, :, :], a["L0_xattn_gru_wih"].rearrange("(c p) n -> p c n", p=P)),
                    (wn[1][:, :, :], a["L0_xattn_gru_whh"].rearrange("(c p) n -> p c n", p=P)),
                    (ctxt[0:M, :, :], a["ctx_1024"].rearrange("b m d -> m b d")),
                    (bih[:, :], a["L0_xattn_gru_bih"].rearrange("(c p) -> p c", p=P)),
                    (bhh[:, :], a["L0_xattn_gru_bhh"].rearrange("(c p) -> p c", p=P)),
                    (nw[:, 0, :], a["L0_xattn_input_norm_w"].rearrange("(c p) -> p c", p=P)),
                    (nw[:, 1, :], a["L0_xattn_slot_norm_w"].rearrange("(c p) -> p c", p=P)),
                ]
                for n, (dst, src) in enumerate(loads):
                    SY.dma_start(dst, src, allow_slow_non_contiguous=n >= 6).then_inc(ld.sem, 16)
                for eng in (PE, SC, VE):
                    need(eng, ld, len(loads) - 1)
                count = [0]

                def after(engine):
                    need(engine, line, count[0] - 1)

                def made(ins):
                    line.did("done", ins)
                    count[0] += 1

                def run(engine, make):
                    after(engine)
                    made(make())

                run(VE, lambda: VE.tensor_tensor(b_tz[:, :], bih[:, :], bhh[:, :], ALU.add))
                run(VE, lambda: VE.tensor_scalar(b_tz[:, :], b_tz[:, :], 0.5, None, ALU.mult))
                run(VE, lambda: VE.tensor_scalar(bhh[:, :], bhh[:, :], 0.5, None, ALU.mult))
                run(VE, lambda: VE.tensor_scalar(snw[:, :], nw[:, 1, :], XSCALE * WS, None, ALU.mult))
                for b in range(NB):
                    run(SC, lambda: SC.activation(sqc[0:M, :], ctxt[0:M, b, :], ACT.Square,
                                                  accum_out=ssc[0:M, b:b + 1]))
                run(VE, lambda: VE.tensor_scalar(ssc[0:M, :], ssc[0:M, :], 1.0 / D, RMS_EPS, ALU.mult, ALU.add))
                run(PO, lambda: PO.tensor_tensor(rc[0:M, :], ssc[0:M, :], powh[0:M, 0:NB], ALU.pow))
                run(VE, lambda: VE.tensor_tensor(ctxt[0:M, :, :], ctxt[0:M, :, :],
                                                 rc[0:M, :].unsqueeze(2).broadcast_to((M, NB, D)), ALU.mult))
                for ch in range(DC):
                    after(PE)
                    for b in range(NB):
                        tr = PE.transpose(ps[:, b // 4, (b % 4) * M:(b % 4) * M + M],
                                          ctxt[0:M, b, ch * P:ch * P + P], ident[0:M, 0:M])
                    made(tr)
                    run(VE, lambda: VE.tensor_scalar(
                        pnT[:, ch, :].rearrange("p (k m) -> p k m", k=2), ps[:, 0:2, 0:4 * M], nw[:, 0, ch:ch + 1],
                        None, ALU.mult))
                    for w, wt in ((wn[0], wihT), (wn[1], whhT)):
                        after(PE)
                        for g in range(G3 // P):
                            tr = PE.transpose(ps[:, g // 3, (g % 3) * P:(g % 3) * P + P],
                                              w[:, g, ch * P:ch * P + P], ident[:, :])
                        made(tr)
                        run(VE, lambda: VE.tensor_copy(wt[:, ch, :].rearrange("p (k m) -> p k m", k=2),
                                                       ps[:, 0:2, 0:3 * P]))
                run(VE, lambda: VE.tensor_scalar(whh[0][:, :, :], whhT[:, :, :], WS, None, ALU.mult))
                run(VE, lambda: VE.scalar_tensor_tensor(whh[1][:, :, :], whhT[:, :, :], WS, whh[0][:, :, :],
                                                        ALU.mult, ALU.subtract))
                for e in range(DC):
                    after(PE)
                    for f in range(DC):
                        PE.matmul(ps[:, 0, 0:D], wk[:, f, e * P:e * P + P], wq[:, f, :], start=f == 0,
                                  stop=f == DC - 1)
                    for k in range(2):
                        for f in range(DC):
                            mm = PE.matmul(ps[:, 1 + k, 0:3 * P], wv[:, f, e * P:e * P + P],
                                           wihT[:, f, k * 3 * P:(k + 1) * 3 * P], start=f == 0, stop=f == DC - 1)
                    made(mm)
                    run(VE, lambda: VE.tensor_copy(wa[:, e, :], ps[:, 0, 0:D]))
                    run(VE, lambda: VE.tensor_copy(wb[:, e, :].rearrange("p (k m) -> p k m", k=2),
                                                   ps[:, 1:3, 0:3 * P]))
                half = NB * M // 2
                for d in range(DC):
                    after(PE)
                    for k in range(2):
                        for e in range(DC):
                            mm = PE.matmul(ps[:, k, 0:half], wa[:, e, d * P:d * P + P],
                                           pnT[:, e, k * half:(k + 1) * half], start=e == 0, stop=e == DC - 1)
                    made(mm)
                    run(VE, lambda: VE.tensor_scalar(kqf[:, :].rearrange("p (k m) -> p k m", k=2), ps[:, 0:2, 0:half],
                                                     snw[:, d:d + 1], None, ALU.mult))
                    run(VE, lambda: VE.tensor_copy(kq[0][:, d, :], kqf[:, :]))
                    run(VE, lambda: VE.tensor_tensor(kq[1][:, d, :], kqf[:, :], kq[0][:, d, :], ALU.subtract))
                after(PE)
                for b in range(NB):
                    pair = slice(2 * (b % 2), 2 * (b % 2) + 2)
                    need(PE, V_ve, b - 2)
                    for k in range(2):
                        for e in range(DC):
                            mm = PE.matmul(ps[0:M, pair.start + k, 0:3 * P], pnT[:, e, b * M:(b + 1) * M],
                                           wb[:, e, k * 3 * P:(k + 1) * 3 * P], start=e == 0, stop=e == DC - 1)
                    V_pe.did("done", mm)
                    hi, lo = (vw[i][0:M, b, :].rearrange("p (k m) -> p k m", k=2) for i in range(2))
                    need(VE, V_pe, b)
                    V_ve.did("hi", VE.tensor_scalar(hi, ps[0:M, pair, 0:3 * P], WS, None, ALU.mult))
                    need(VE, V_ve, b, "hi")
                    V_ve.did("lo", VE.scalar_tensor_tensor(lo, ps[0:M, pair, 0:3 * P], WS, hi, ALU.mult,
                                                           ALU.subtract))
                for g in range(NG):
                    pair = slice(4 + 2 * (g % 2), 6 + 2 * (g % 2))
                    need(PE, X_cp, g - 2)
                    for ch in range(DC):
                        for t in range(TG):
                            tr = PE.transpose(ps[:, pair.start + ch, t * P:t * P + P],
                                              xs[:, g * TG + t, ch * P:ch * P + P], ident[:, :])
                    X_pe.did("done", tr)
                    need(SC, X_pe, g)
                    X_cp.did("done", SC.copy(slots[:, :, g * GT:(g + 1) * GT], ps[:, pair, :]))
                nc.all_engine_barrier()

            sh = [[sb(c, f"s{i}{g}", [P, DC, GT], F16) for i in range(2)] for g in range(NG)]
            sq = sb(c, "sq", [P, DC, GT])
            diag = [sb(c, f"diag{i}", [P, TG, P]) for i in range(2)]
            rr = [sb(c, f"rr{i}", [P, GT]) for i in range(2)]
            sc = sb(c, "sc", [P, BG, S])
            ex = sb(c, "ex", [P, BG, S])
            an = sb(c, "an", [P, GT])
            anh = [[sb(c, f"an{i}{u}", [P, GT], F16) for i in range(2)] for u in range(2)]
            msq = sb(c, "msq", [P, TG])
            rms = sb(c, "rms", [P, TG])
            gmx = sb(c, "gmx", [P, BG])
            gneg = sb(c, "gneg", [P, BG])
            gden = sb(c, "gden", [P, BG])
            grec = sb(c, "grec", [P, BG])
            cse = sb(c, "cse", [P, TG])
            crec = sb(c, "crec", [P, TG])
            tr_, tz, hn, t1, t2, nn, dl = (sb(c, k, [P, GT]) for k in ("tr_", "tz", "hn", "t1", "t2", "nn", "dl"))
            R_sc = stage(c, "R_sc", "hi", "sq", "rr", ahead=2)
            R_ve = stage(c, "R_ve", "lo", "msq", "diag", "sc", ahead=2)
            R_po = stage(c, "R_po", ahead=2)
            R_pe = stage(c, "R_pe", "ss", "rb", "sc", ahead=2)
            A_sc = stage(c, "A_sc", "e0", "e1", "rr", "hi", ahead=2)
            A_ve = stage(c, "A_ve", "mx", "neg", "recip", "m0", "m1", "cse", "crec", "diag", "an", "lo", ahead=2)
            A_pe = stage(c, "A_pe", "cs", "rb", ahead=2)
            G_pe = stage(c, "G_pe", "r", "z", "hn", "xn", ahead=2 * NG)
            G_sc = stage(c, "G_sc", "tr", "tz", "hn", "nn", ahead=2)
            G_ve = stage(c, "G_ve", "t1", "t2", "u", "out", ahead=2 * NG)
            G_po = stage(c, "G_po", ahead=2)
            nc.all_engine_barrier()

            def along_free(dst, values):
                return VE.tensor_tensor(dst[:, :, :], ident[:, :].unsqueeze(1).broadcast_to((P, TG, P)),
                                        values[:, :].unsqueeze(2).broadcast_to((P, TG, P)), ALU.mult)

            def first_of_tiles(bank):
                return ps[:, bank, :].rearrange("p (t n) -> p t n", n=P)[:, :, 0:1]

            def r_parts(n, g):
                hi, lo = sh[g]
                src = slots[:, :, g * GT:(g + 1) * GT]
                need(SC, G_ve, 2 * (n - NG) + 1)
                need(SC, G_pe, 2 * (n - NG) + 1)
                R_sc.did("hi", SC.copy(hi[:, :, :], src))
                need(SC, R_pe, n - 1, "ss")
                R_sc.did("sq", SC.activation(sq[:, :, :], src, ACT.Square))
                need(VE, R_sc, n, "hi")
                R_ve.did("lo", VE.tensor_tensor(lo[:, :, :], src, hi[:, :, :], ALU.subtract))

            def r_norm(n, g):
                need(PE, R_sc, n, "sq")
                need(PE, A_ve, n - 2, "cse")
                for t in range(TG):
                    for ch in range(DC):
                        mm = PE.matmul(ps[:, 4, t * P:t * P + P], sq[:, ch, t * P:t * P + P], ones[:, :],
                                       start=ch == 0, stop=ch == DC - 1)
                R_pe.did("ss", mm)
                need(VE, R_pe, n, "ss")
                need(VE, R_po, n - 1)
                R_ve.did("msq", VE.tensor_scalar(msq[:, :].unsqueeze(2), first_of_tiles(4), 1.0 / D, RMS_EPS,
                                                 ALU.mult, ALU.add))
                need(PO, R_ve, n, "msq")
                need(PO, R_ve, n - 1, "diag")
                R_po.did("done", PO.tensor_tensor(rms[:, :], msq[:, :], powh[:, 0:TG], ALU.pow))
                need(VE, R_po, n)
                need(VE, R_pe, n - 1, "rb")
                R_ve.did("diag", along_free(diag[0], rms))

            def r_scores(n, g):
                need(PE, R_ve, n, "diag")
                need(PE, A_sc, n - 2, "rr")
                R_pe.did("rb", PE.matmul(ps[:, 5, :], ones[:, :], diag[0][:, :, :].rearrange("p t n -> p (t n)"),
                                         start=True, stop=True))
                need(PE, R_ve, n, "lo")
                need(PE, R_ve, n - 1, "sc")
                for k in range(BG):
                    m = slice((g * BG + k) * M, (g * BG + k + 1) * M)
                    w = [[kq[h][:, ch, m] for h in range(2)] for ch in range(DC)]
                    x = [[sh[g][h][:, ch, k * S:(k + 1) * S] for h in range(2)] for ch in range(DC)]
                    mm = three_passes(PE, ps[0:M, 6, k * S:(k + 1) * S], list(zip(w, x)))
                R_pe.did("sc", mm)
                need(SC, R_pe, n, "rb")
                need(SC, R_ve, n - 1, "sc")
                R_sc.did("rr", SC.copy(rr[0][:, :], ps[:, 5, :]))
                need(VE, R_sc, n, "rr")
                need(VE, R_pe, n, "sc")
                need(VE, A_sc, n - 1, "e1")
                R_ve.did("sc", VE.scalar_tensor_tensor(sc[0:M, :, :].rearrange("p b n -> p (b n)"), ps[0:M, 6, :],
                                                       1 / WS, rr[0][0:M, :], ALU.mult, ALU.mult))

            exf = ex[0:M, :, :].rearrange("p b n -> p (b n)")

            def a_softmax(n):
                need(VE, R_ve, n, "sc")
                A_ve.did("mx", VE.tensor_reduce(gmx[0:M, :], sc[0:M, :, :], AX, ALU.max))
                need(VE, A_ve, n, "mx")
                need(VE, A_sc, n - 1, "e1")
                A_ve.did("neg", VE.tensor_scalar(gneg[0:M, :], gmx[0:M, :], -1.0, None, ALU.mult))
                need(SC, A_ve, n, "neg")
                need(SC, A_ve, n - 1, "an")
                for k in range(BG):
                    A_sc.did(f"e{k}", SC.activation(ex[0:M, k, :], sc[0:M, k, :], ACT.Exp, bias=gneg[0:M, k:k + 1],
                                                    accum_out=gden[0:M, k:k + 1]))
                need(VE, A_sc, n, "e1")
                A_ve.did("recip", VE.reciprocal(grec[0:M, :], gden[0:M, :]))
                need(VE, A_ve, n, "recip")
                for k in range(BG):
                    A_ve.did(f"m{k}", VE.tensor_scalar(ex[0:M, k, :], ex[0:M, k, :], grec[0:M, k:k + 1], None,
                                                       ALU.mult))

            def a_sums(n, r_behind=True):
                need(PE, A_ve, n, "m1")
                if r_behind:
                    need(PE, R_ve, n + 1, "msq")
                for t in range(TG):
                    mm = PE.matmul(ps[:, 4, t * P:t * P + P], exf[:, t * P:t * P + P], ones[0:M, :],
                                   start=True, stop=True)
                A_pe.did("cs", mm)
                need(VE, A_pe, n, "cs")
                A_ve.did("cse", VE.tensor_scalar(cse[:, :].unsqueeze(2), first_of_tiles(4), SUM_EPS, None, ALU.add))
                need(VE, A_ve, n, "cse")
                A_ve.did("crec", VE.reciprocal(crec[:, :], cse[:, :]))
                need(VE, A_ve, n, "crec")
                need(VE, A_pe, n - 1, "rb")
                A_ve.did("diag", along_free(diag[1], crec))

            def a_weights(n, u, r_behind=True):
                need(PE, A_ve, n, "diag")
                if r_behind:
                    need(PE, R_sc, n + 1, "rr")
                A_pe.did("rb", PE.matmul(ps[:, 5, :], ones[:, :], diag[1][:, :, :].rearrange("p t n -> p (t n)"),
                                         start=True, stop=True))
                need(SC, A_pe, n, "rb")
                need(SC, A_ve, n - 1, "an")
                A_sc.did("rr", SC.copy(rr[1][:, :], ps[:, 5, :]))
                need(VE, A_sc, n, "rr")
                need(VE, A_sc, n - 1, "hi")
                A_ve.did("an", VE.tensor_tensor(an[0:M, :], exf, rr[1][0:M, :], ALU.mult))
                need(SC, A_ve, n, "an")
                need(SC, G_pe, 2 * (n - 2) + 1)
                A_sc.did("hi", SC.copy(anh[u][0][0:M, :], an[0:M, :]))
                need(VE, A_sc, n, "hi")
                A_ve.did("lo", VE.tensor_tensor(anh[u][1][0:M, :], an[0:M, :], anh[u][0][0:M, :], ALU.subtract))

            def gate(n, u, g, bank, chunk, hidden, update):
                jobs = []
                if hidden:
                    jobs += [(whh[i][:, ch, chunk * P:chunk * P + P], sh[g][j][:, ch, :], ps[:, bank, :])
                             for ch in range(DC) for i, j in ((0, 0), (0, 1), (1, 0))]
                n_hidden = len(jobs)
                if update:
                    jobs += [(vw[i][0:M, g * BG + k, chunk * P:chunk * P + P],
                              anh[u][j][0:M, k * S:(k + 1) * S], ps[:, bank, k * S:(k + 1) * S])
                             for k in range(BG) for i, j in ((0, 0), (0, 1), (1, 0))]
                for n_, (w, x, o) in enumerate(jobs):
                    if n_ == n_hidden:
                        need(PE, A_ve, n, "lo")
                    mm = PE.matmul(o, w, x, start=n_ == 0, stop=n_ == len(jobs) - 1, skip_group_check=True)
                return mm

            def gru_rz(n, u, g, ch):
                m = 2 * n + ch
                need(PE, G_sc, m - 1, "tr")
                G_pe.did("r", gate(n, u, g, 0, ch, True, True))
                need(PE, G_sc, m - 1, "tz")
                G_pe.did("z", gate(n, u, g, 1, DC + ch, True, True))
                need(SC, G_pe, m, "r")
                need(SC, G_ve, m - 1, "t1")
                G_sc.did("tr", SC.activation(tr_[:, :], ps[:, 0, :], ACT.Tanh, bias=b_tz[:, ch:ch + 1],
                                             scale=0.5 / WS))
                need(SC, G_pe, m, "z")
                need(SC, G_ve, m - 1, "u")
                G_sc.did("tz", SC.activation(tz[:, :], ps[:, 1, :], ACT.Tanh, bias=b_tz[:, DC + ch:DC + ch + 1],
                                             scale=0.5 / WS))

            def gru_n(n, u, g, ch):
                m = 2 * n + ch
                need(PE, G_sc, m - 1, "hn")
                G_pe.did("hn", gate(n, u, g, 2, 2 * DC + ch, True, False))
                need(PE, G_ve, m - 1, "t2")
                G_pe.did("xn", gate(n, u, g, 3, 2 * DC + ch, False, True))
                need(SC, G_pe, m, "hn")
                G_sc.did("hn", SC.activation(hn[:, :], ps[:, 2, :], ACT.Identity,
                                             bias=bhh[:, 2 * DC + ch:2 * DC + ch + 1], scale=0.5 / WS))
                need(VE, G_sc, m, "hn")
                G_ve.did("t1", VE.scalar_tensor_tensor(t1[:, :], tr_[:, :], 1.0, hn[:, :], ALU.add, ALU.mult))
                need(VE, G_pe, m, "xn")
                need(VE, G_ve, m, "t1")
                need(VE, G_sc, m - 1, "nn")
                G_ve.did("t2", VE.scalar_tensor_tensor(t2[:, :], ps[:, 3, :], 1 / WS, t1[:, :], ALU.mult, ALU.add))

            def gru_out(n, u, g, ch):
                m = 2 * n + ch
                need(SC, G_ve, m, "t2")
                need(SC, G_ve, m - 1, "out")
                G_sc.did("nn", SC.activation(nn[:, :], t2[:, :], ACT.Tanh, bias=bih[:, 2 * DC + ch:2 * DC + ch + 1]))
                h = slots[:, ch, g * GT:(g + 1) * GT]
                need(PO, G_sc, m, "nn")
                need(PO, G_ve, m - 1, "out")
                G_po.did("done", PO.tensor_tensor(dl[:, :], h, nn[:, :], ALU.subtract))
                need(VE, G_po, m)
                G_ve.did("u", VE.scalar_tensor_tensor(dl[:, :], tz[:, :], 1.0, dl[:, :], ALU.add, ALU.mult))
                need(VE, G_ve, m, "u")
                G_ve.did("out", VE.scalar_tensor_tensor(h, dl[:, :], 0.5, nn[:, :], ALU.mult, ALU.add))

            def step(n, g, r_next=True, a_next=True):
                u, g2 = g % 2, (g + 2) % NG
                if a_next:
                    a_softmax(n + 1)
                if r_next:
                    r_parts(n + 2, g2)
                gru_rz(n, u, g, 0)
                if r_next:
                    r_norm(n + 2, g2)
                gru_n(n, u, g, 0)
                if a_next:
                    a_sums(n + 1, r_next)
                gru_out(n, u, g, 0)
                gru_rz(n, u, g, 1)
                if r_next:
                    r_scores(n + 2, g2)
                if a_next:
                    a_weights(n + 1, 1 - u, r_next)
                gru_n(n, u, g, 1)
                gru_out(n, u, g, 1)

            r_parts(0, 0)
            r_norm(0, 0)
            r_scores(0, 0)
            a_softmax(0)
            r_parts(1, 1)
            r_norm(1, 1)
            r_scores(1, 1)
            a_sums(0)
            a_weights(0, 0)
            with nc.Fori(0, ITERS - 1) as it:
                for g in range(NG):
                    step(it * NG + g, g)
            for g in range(NG):
                step((ITERS - 1) * NG + g, g, r_next=g < NG - 2, a_next=g < NG - 1)
            nc.all_engine_barrier()

        with ExitStack() as c:
            gw = sb(c, "gw", [P, DC, E])
            gwh = [sb(c, f"gw_{i}", [P, DC, E], F16) for i in range(2)]
            gb = sb(c, "gb", [P, E])
            stg_ = [sb(c, f"stg{u}", [P, DC, GT]) for u in range(2)]
            y_ = [sb(c, f"y{u}", [P, TG, D]) for u in range(2)]
            st_ = [sb(c, f"st{u}", [P, TG, 6]) for u in range(2)]
            mv2_ = [sb(c, f"mv2{u}", [P, TG, 2]) for u in range(2)]
            ve2_ = [sb(c, f"ve2{u}", [P, TG]) for u in range(2)]
            rs2_ = [sb(c, f"rs2{u}", [P, TG]) for u in range(2)]
            lg, pe_, pr, mx8, fi, w0 = (sb(c, k, [P, NT, E]) for k in ("lg", "pe_", "pr", "mx8", "fi", "w0"))
            hot = [sb(c, f"hot{k}", [P, NT, E]) for k in range(2)]
            both, before, cnt = (sb(c, k, [P, NT, E]) for k in ("both", "before", "cnt"))
            tri = sb(c, "tri", [P, P])
            ix8 = sb(c, "ix8", [P, NT, E], U32)
            s1, s2 = (sb(c, k, [P, NT]) for k in ("s1", "s2"))
            slot = sb(c, "slot", [P, 2, NT])
            total, tiles, first, ends = (sb(c, k, [P, E]) for k in ("total", "tiles", "first", "ends"))
            ramp_i = sb(c, "ramp_i", [P, NTILE], mybir.dt.int32)
            ramp = sb(c, "ramp", [P, NTILE])
            steps128 = sb(c, "steps128", [P, NT])
            cmp1 = sb(c, "cmp1", [P, E, NT])
            cmp2 = sb(c, "cmp2", [P, NTILE, E])
            te_f = sb(c, "te_f", [P, NTILE])
            ld = stage(c, "r_ld", unit=16)
            gcut = stage(c, "gcut", "hi", "lo")
            tri_s = stage(c, "tri_s", "ones", "cut", "ramp")
            norm_line = [stage(c, f"norm_line{u}") for u in range(2)]
            line = stage(c, "r_line")
            nc.all_engine_barrier()
            SY.dma_start(gw[:, :, :], a["L0_ffn_gate_w"].rearrange("(c p) e -> p c e", p=P)).then_inc(ld.sem, 16)
            SY.dma_start(gb[:, :], a["L0_ffn_gate_b"].rearrange("(o d) -> o d", o=1).broadcast_to((P, E))).then_inc(
                ld.sem, 16)
            tri_s.did("ones", PO.memset(tri[:, :], 1.0))
            need(PO, tri_s, 0, "ones")
            tri_s.did("cut", PO.affine_select(out=tri[:, :], in_=tri[:, :], compare_op=ALU.is_gt, fill=0.0, base=0,
                                              pattern=[[1, P]], channel_multiplier=-1))
            tri_s.did("ramp", PO.iota(ramp_i[:, :], pattern=[[1, NTILE]], base=0, channel_multiplier=0))
            need(VE, ld, 1)
            gcut.did("hi", VE.tensor_scalar(gwh[0][:, :, :], gw[:, :, :], WS, None, ALU.mult))
            need(VE, gcut, 0, "hi")
            gcut.did("lo", VE.scalar_tensor_tensor(gwh[1][:, :, :], gw[:, :, :], WS, gwh[0][:, :, :], ALU.mult,
                                                   ALU.subtract))
            need(PE, gcut, 0)
            need(VE, gcut, 0)
            need(SC, gcut, 0)

            def bc(t, n=E):
                return t.unsqueeze(2).broadcast_to((P, t.shape[1], n))

            class Line:
                def __init__(self, stage_, start):
                    self.stage, self.start, self.k = stage_, start, 0

                def run(self, engine, make, alone=False):
                    engine.wait_ge(self.stage.sem, self.start + self.k + 1)
                    if alone:
                        settle(engine, spare[engine])
                    self.k += 1
                    self.stage.did("done", make())

            def last_of(f, n):
                for t in range(n):
                    ins = f(t)
                return ins

            def cols(g):
                return ds(g * GT, GT)

            def second_norm(g, u):
                steps = []

                def run(engine, make, alone=False):
                    steps.append((engine, make, alone))

                stg, y, st, mv2, ve2, rs2 = (b[u] for b in (stg_, y_, st_, mv2_, ve2_, rs2_))
                pair, gate_bank = slice(3 * u, 3 * u + 2), 3 * u + 2
                tok = ds(g * TG, TG)
                run(SC, lambda: SC.copy(stg[:, :, :], slots[:, :, cols(g)]))

                def back():
                    for t in range(TG):
                        for ch in range(DC):
                            tr = PE.transpose(ps[:, pair.start + t // 2, (t % 2) * D + ch * P:(t % 2) * D + ch * P + P],
                                              stg[:, ch, t * P:t * P + P], ident[:, :])
                    return tr
                run(PE, back)
                run(VE, lambda: VE.tensor_tensor(
                    y[:, :, :], ps[:, pair, :].rearrange("p b (t d) -> p (b t) d", d=D), xs[:, tok, :], ALU.add))
                run(VE, lambda: last_of(lambda t: VE.bn_stats(st[:, t, :], y[:, t, :]), TG), alone=True)
                run(VE, lambda: last_of(lambda t: VE.bn_aggr(mv2[:, t, :], st[:, t, :]), TG), alone=True)
                run(VE, lambda: VE.tensor_scalar(ve2[:, :].unsqueeze(2), mv2[:, :, 1:2], LN_EPS, None, ALU.add))
                run(PO, lambda: PO.tensor_tensor(rs2[:, :], ve2[:, :], powh[:, 0:TG], ALU.pow))
                run(VE, lambda: last_of(lambda t: VE.tensor_scalar(
                    y[:, t, :], y[:, t, :], mv2[:, t, 0:1], rs2[:, t:t + 1], ALU.subtract, ALU.mult), TG))

                def forth():
                    for ch in range(DC):
                        for t in range(TG):
                            tr = PE.transpose(ps[:, pair.start + ch, t * P:t * P + P], y[:, t, ch * P:ch * P + P], ident[:, :])
                    return tr
                run(PE, forth)
                run(SC, lambda: SC.copy(xT[0][:, :, cols(g)], ps[:, pair, :]))
                run(VE, lambda: VE.tensor_tensor(xT[1][:, :, cols(g)], ps[:, pair, :], xT[0][:, :, cols(g)],
                                                 ALU.subtract))

                def gates():
                    for t in range(TG):
                        x = [[xT[h][:, ch, ds(g * GT + t * P, P)] for h in range(2)] for ch in range(DC)]
                        w = [[gwh[h][:, ch, :] for h in range(2)] for ch in range(DC)]
                        mm = three_passes(PE, ps[:, gate_bank, t * E:t * E + E], list(zip(x, w)))
                    return mm
                run(PE, gates)
                run(VE, lambda: VE.scalar_tensor_tensor(
                    lg[:, tok, :], ps[:, gate_bank, 0:TG * E].rearrange("p (t e) -> p t e", e=E), 1 / WS,
                    gb[:, :].unsqueeze(1).broadcast_to((P, TG, E)), ALU.mult, ALU.add))
                run(SC, lambda: SC.copy(xs[:, tok, :], y[:, :, :]))
                return steps

            with nc.Fori(0, NG // 2) as h:
                lines = [Line(norm_line[u], h * NORM_STEPS) for u in range(2)]
                for steps in zip(second_norm(h * 2, 0), second_norm(h * 2 + 1, 1), strict=True):
                    for line_g, step_ in zip(lines, steps):
                        line_g.run(*step_)
                assert lines[0].k == NORM_STEPS, lines[0].k
            for eng in (PE, SC, VE, PO):
                for u in range(2):
                    need(eng, norm_line[u], NG // 2 * NORM_STEPS - 1)
            route = Line(line, 0)
            run = route.run
            run(VE, lambda: VE.tensor_reduce(s1[:, :], lg[:, :, :], AX, ALU.max))
            run(VE, lambda: VE.tensor_tensor(lg[:, :, :], lg[:, :, :], bc(s1[:, :]), ALU.subtract))
            run(SC, lambda: SC.activation(pe_[:, :, :], lg[:, :, :], ACT.Exp))
            run(VE, lambda: VE.tensor_reduce(s1[:, :], pe_[:, :, :], AX, ALU.add))
            run(VE, lambda: VE.reciprocal(s2[:, :], s1[:, :]))
            run(VE, lambda: VE.tensor_tensor(pr[:, :, :], pe_[:, :, :], bc(s2[:, :]), ALU.mult))
            run(VE, lambda: last_of(lambda t: VE.max(mx8[:, t, :], pr[:, t, :]), NT))
            run(VE, lambda: last_of(lambda t: VE.max_index(ix8[:, t, :], mx8[:, t, :], pr[:, t, :]), NT))
            run(VE, lambda: VE.tensor_copy(fi[:, :, :], ix8[:, :, :]))
            run(VE, lambda: last_of(lambda k: VE.tensor_tensor(
                hot[k][:, :, :], iota[:, :].unsqueeze(1).broadcast_to((P, NT, E)),
                fi[:, :, k:k + 1].broadcast_to((P, NT, E)), ALU.is_equal), 2))
            run(VE, lambda: VE.tensor_tensor(both[:, :, :], hot[0][:, :, :], hot[1][:, :, :], ALU.add))

            def counts():
                rhs = both[:, :, :].rearrange("p t e -> p (t e)")
                PE.matmul(ps[:, 0, 0:P], tri[:, :], rhs, start=True, stop=True)
                return PE.matmul(ps[:, 1, 0:P], ones[:, :], rhs, start=True, stop=True)
            need(PE, tri_s, 0)
            run(PE, counts)
            run(VE, lambda: VE.tensor_tensor(s1[:, :], mx8[:, :, 0], mx8[:, :, 1], ALU.add))
            run(VE, lambda: VE.tensor_scalar(s1[:, :], s1[:, :], TOP_EPS, None, ALU.add))
            run(VE, lambda: VE.reciprocal(s2[:, :], s1[:, :]))
            run(VE, lambda: last_of(lambda k: VE.tensor_tensor(top_w[:, k, :], mx8[:, :, k], s2[:, :], ALU.mult), 2))
            run(VE, lambda: VE.tensor_copy(cnt[:, :, :].rearrange("p t e -> p (t e)"), ps[:, 1, 0:P]))
            run(VE, lambda: VE.memset(before[:, 0, :], 0.0))
            for t in range(1, NT):
                run(VE, lambda: VE.tensor_tensor(before[:, t, :], before[:, t - 1, :], cnt[:, t - 1, :], ALU.add))
            run(VE, lambda: VE.tensor_tensor(total[:, :], before[:, NT - 1, :], cnt[:, NT - 1, :], ALU.add))
            need(VE, tri_s, 0)
            run(VE, lambda: VE.tensor_copy(ramp[:, :], ramp_i[:, :]))
            run(VE, lambda: VE.tensor_scalar(steps128[:, :], ramp[:, 0:NT], float(P), None, ALU.mult))
            run(VE, lambda: VE.tensor_tensor(cmp1[:, :, :], bc(total[:, :], NT),
                                             steps128[:, :].unsqueeze(1).broadcast_to((P, E, NT)), ALU.is_gt))
            run(VE, lambda: VE.tensor_reduce(tiles[:, :], cmp1[:, :, :], AX, ALU.add))
            run(VE, lambda: VE.tensor_copy(ends[:, 0:1], tiles[:, 0:1]))
            for e in range(1, E):
                run(VE, lambda: VE.tensor_tensor(ends[:, e:e + 1], ends[:, e - 1:e], tiles[:, e:e + 1], ALU.add))
            run(VE, lambda: VE.tensor_tensor(first[:, :], ends[:, :], tiles[:, :], ALU.subtract))
            run(VE, lambda: VE.tensor_scalar(first[:, :], first[:, :], float(P), None, ALU.mult))
            run(VE, lambda: VE.tensor_tensor(before[:, :, :], before[:, :, :],
                                             first[:, :].unsqueeze(1).broadcast_to((P, NT, E)), ALU.add))
            run(VE, lambda: VE.tensor_tensor(before[:, :, :].rearrange("p t e -> p (t e)"), ps[:, 0, 0:P],
                                             before[:, :, :].rearrange("p t e -> p (t e)"), ALU.add))
            for k in range(2):
                run(VE, lambda: VE.tensor_tensor(w0[:, :, :], hot[k][:, :, :], before[:, :, :], ALU.mult))
                run(VE, lambda: VE.tensor_reduce(slot[:, k, :], w0[:, :, :], AX, ALU.add))
            run(VE, lambda: VE.tensor_copy(idx0[:, :, :], slot[:, :, :]))
            run(VE, lambda: VE.tensor_tensor(cmp2[:, :, :], bc(ramp[:, :], E),
                                             ends[:, :].unsqueeze(1).broadcast_to((P, NTILE, E)), ALU.is_ge))
            run(VE, lambda: VE.tensor_reduce(te_f[:, :], cmp2[:, :, :], AX, ALU.add))
            run(VE, lambda: VE.tensor_scalar(te_f[:, :], te_f[:, :], float(E - 1), None, ALU.min))
            run(VE, lambda: VE.tensor_copy(tile_e[:, :], te_f[:, :]))
            nc.all_engine_barrier()
        mid.close()

        with ExitStack() as c:
            e1 = [sb(c, f"e1_{i}", [P, E, DC, I], F16) for i in range(2)]
            e2 = [sb(c, f"e2_{i}", [P, E, IC, D], F16) for i in range(2)]
            sw = sb(c, "sw", [P, 8 * I], F16)
            piece = [sb(c, f"piece{k}", [P, I]) for k in range(4)]
            work = sb(c, "work", [P, 4 * GT])
            b1s = sb(c, "b1s", [P, IC])
            b1e = sb(c, "b1e", [P, E, IC])
            b2s = sb(c, "b2s", [P, D])

            def half(t, k, n, dt=F16):
                v = t[:, :] if t.dtype == dt else t[:, :].bitcast(dt)
                return v[:, k * n:(k + 1) * n]
            s1c = [half(sw, i, 2 * I).rearrange("p (c n) -> p c n", c=DC) for i in range(2)]
            s2c = [half(sw, 2 + i, 2 * I).rearrange("p (c n) -> p c n", c=IC) for i in range(2)]
            hf = [half(work, k, GT, F32) for k in range(2)]
            hh = [[half(work, 4 + 2 * k + i, GT) for i in range(2)] for k in range(2)]
            b2e = half(sw, 1, 4 * I).bitcast(F32).rearrange("p (e d) -> p e d", e=E)
            zf = half(sw, 0, 2 * I).bitcast(F32)
            xg = [half(sw, 4 + u, 2 * D).bitcast(F32) for u in range(2)]
            xgT = [[half(sw, 12 + 2 * u + i, D).rearrange("p (c t) -> p c t", c=DC) for i in range(2)]
                   for u in range(2)]
            he = [[half(work, 2 * u + i, I).rearrange("p (k t) -> p k t", k=IC) for i in range(2)] for u in range(2)]
            yo = [sb(c, f"yo{u}", [P, D]) for u in range(2)]

            ld_p = [stage(c, f"ld_p{k}", unit=16) for k in range(4)]
            ld_b = stage(c, "ld_b", unit=16)
            cut_s = stage(c, "cut_s", "hi", "lo")
            cut_p = stage(c, "cut_p", "hi", "lo", ahead=5)
            scat = stage(c, "scat", unit=16, ahead=0)
            H_pe = stage(c, "H_pe")
            H_g = stage(c, "H_g", "gelu", "hi", ahead=2)
            H_lo = stage(c, "H_lo", ahead=2)
            O_pe = stage(c, "O_pe", *[f"{k}" for k in range(IC)], ahead=2)
            O_ev = stage(c, "O_ev", "base", "acc", ahead=2)
            nc.all_engine_barrier()

            need(PO, zeroed, 0)
            for k in range(2):
                for t in range(NT):
                    PO.indirect_dma_start(rows_x, bass.IndirectOffsetOnAxis(ap=idx0[:, k, t:t + 1], axis=0),
                                          xs[:, t, :], None).then_inc(scat.sem, 16)

            def piece_of(w1, w2, j):
                if j < DC:
                    return w1.rearrange("(c p) n -> p c n", p=P)[:, j, :]
                j -= DC
                return w2.rearrange("(c p) n -> p c n", p=P)[:, j * IC // 2:(j + 1) * IC // 2, :]

            def fetch(q, j, w1, w2):
                if not isinstance(q, int):
                    need(SY, cut_p, (q - 2) * 4 + j)
                dst = piece[j][:, :] if j < DC else piece[j][:, :].rearrange("p (c n) -> p c n", n=D)
                SY.dma_start(dst, piece_of(w1, w2, j)).then_inc(ld_p[j].sem, 16)

            for j in range(4):
                fetch(0, j, a["L0_ffn_sh_w1"], a["L0_ffn_sh_w2"])
            SY.dma_start(b1s[:, :], a["L0_ffn_sh_b1"].rearrange("(c p) -> p c", p=P),
                         allow_slow_non_contiguous=True).then_inc(ld_b.sem, 16)
            SY.dma_start(b2s[:, :], a["L0_ffn_sh_b2"].rearrange("(o d) -> o d", o=1).broadcast_to((P, D))).then_inc(
                ld_b.sem, 16)
            SY.dma_start(b1e[:, :, :].rearrange("p e c -> p (e c)"),
                         a["L0_ffn_eb1"].rearrange("e (c p) -> p (e c)", p=P),
                         allow_slow_non_contiguous=True).then_inc(ld_b.sem, 16)

            def cut_piece(q, j, st, item, hi, lo):
                need(VE, ld_p[j], q)
                src = piece[j][:, :]
                st.did("hi", VE.tensor_scalar(hi, src, WS, None, ALU.mult))
                need(VE, st, item, "hi")
                st.did("lo", VE.scalar_tensor_tensor(lo, src, WS, hi, ALU.mult, ALU.subtract))

            def fetch_expert(e):
                for j in range(4):
                    fetch(e + 1, j, a["L0_ffn_ew1"][e], a["L0_ffn_ew2"][e])

            def cut_expert(e, j):
                flat = [[w[i][:, e, :, :].rearrange("p c n -> p (c n)") for i in range(2)] for w in (e1, e2)]
                hi, lo = (v[:, (j % 2) * I:(j % 2 + 1) * I] for v in flat[j // 2])
                cut_piece(e + 1, j, cut_p, e * 4 + j, hi, lo)

            for j in range(4):
                k = j // 2 * 2
                hi, lo = (half(sw, 2 * (k + i) + j % 2, I) for i in range(2))
                cut_piece(0, j, cut_s, j, hi, lo)
            need(PE, cut_s, 3)
            need(SY, cut_s, 3)
            need(SC, ld_b, 2)
            need(VE, ld_b, 2)

            def shared(g):
                def up(k):
                    m = g * IC + k
                    need(PE, H_g, m - 2, "gelu")
                    w = [[s1c[h][:, ch, k * P:k * P + P] for h in range(2)] for ch in range(DC)]
                    x = [[xT[h][:, ch, cols(g)] for h in range(2)] for ch in range(DC)]
                    H_pe.did("done", three_passes(PE, ps[:, k % 2, :], list(zip(w, x))))
                    need(SC, H_pe, m)
                    need(SC, H_lo, m - 2)
                    H_g.did("gelu", SC.activation(hf[k % 2], ps[:, k % 2, :], ACT.Gelu_apprx_tanh,
                                                  bias=b1s[:, k:k + 1], scale=1 / WS))
                    need(SC, H_g, m, "gelu")
                    need(SC, O_pe, g if k >= 2 else g - 1, f"{(k - 2) % IC}")
                    H_g.did("hi", SC.copy(hh[k % 2][0], hf[k % 2]))
                    need(VE, H_g, m, "hi")
                    H_lo.did("done", VE.tensor_tensor(hh[k % 2][1], hf[k % 2], hh[k % 2][0], ALU.subtract))
                    cut_expert(g * 2 + k // 4, k % 4)

                def down(k):
                    m = g * IC + k
                    need(PE, H_lo, m)
                    if k == 0:
                        need(PE, O_ev, g - 1)
                    for t in range(TG):
                        o = ps[:, 4 + t, 0:D]
                        for n_, (i, j) in enumerate(((0, 0), (0, 1), (1, 0))):
                            mm = PE.matmul(o, hh[k % 2][i][:, t * P:t * P + P], s2c[j][:, k, :],
                                           start=k == 0 and n_ == 0, stop=k == IC - 1 and n_ == 2)
                    O_pe.did(f"{k}", mm)

                fetch_expert(g * 2)
                fetch_expert(g * 2 + 1)
                up(0)
                for k in range(1, IC):
                    up(k)
                    down(k - 1)
                down(IC - 1)
                x = xs[:, ds(g * TG, TG), :]
                need(VE, scat, 2 * NT - 1)
                O_ev.did("base", VE.scalar_tensor_tensor(x, x, 2.0, b2s[:, :].unsqueeze(1).broadcast_to((P, TG, D)),
                                                         ALU.mult, ALU.add))
                need(VE, O_pe, g)
                need(VE, O_ev, g, "base")
                O_ev.did("acc", VE.scalar_tensor_tensor(x, ps[:, 4:8, 0:D], 1 / WS, x, ALU.mult, ALU.add))

            with nc.Fori(0, NG) as g:
                shared(g)

            X_ld = [stage(c, f"X_ld{u}", unit=16) for u in range(2)]
            Y_st = [stage(c, f"Y_st{u}", unit=16) for u in range(2)]
            ld_b2 = stage(c, "ld_b2", unit=16)
            T_pe = stage(c, "T_pe", ahead=3)
            T_hi = stage(c, "T_hi", ahead=2)
            T_lo = stage(c, "T_lo", ahead=2)
            U_pe = stage(c, "U_pe", "0", "1", ahead=3)
            U_z = stage(c, "U_z", "0", "1", ahead=3)
            U_g = stage(c, "U_g", "g0", "g1", "hi", ahead=3)
            U_lo = stage(c, "U_lo", ahead=2)
            D_pe = stage(c, "D_pe", ahead=3)
            D_ev = stage(c, "D_ev", ahead=3)
            nc.all_engine_barrier()
            SY.dma_start(b2e, a["L0_ffn_eb2"].rearrange("(o e) d -> o e d", o=1).broadcast_to((P, E, D))).then_inc(
                ld_b2.sem, 16)
            need(VE, ld_b2, 0)
            rx = rows_x.rearrange("(t p) d -> t p d", p=P)
            ry = rows_y.rearrange("(t p) d -> t p d", p=P)

            def load_rows(i, u):
                need(SY, T_pe, i - 2)
                SY.dma_start(xg[u], rx[i]).then_inc(X_ld[u].sem, 16)

            def turn(i, u, half_i):
                need(PE, X_ld[u], half_i)
                need(PE, T_lo, i - 1)
                for ch in range(DC):
                    mm = PE.transpose(ps[:, 7, ch * P:ch * P + P], xg[u][:, ch * P:ch * P + P], ident[:, :])
                T_pe.did("done", mm)
                pv = ps[:, 7, 0:D].rearrange("p (c t) -> p c t", c=DC)
                need(SC, T_pe, i)
                need(SC, U_pe, i - 2)
                T_hi.did("done", SC.copy(xgT[u][0], pv))
                need(VE, T_hi, i)
                T_lo.did("done", VE.tensor_tensor(xgT[u][1], pv, xgT[u][0], ALU.subtract))

            def expert_of(i):
                return [e.value_load(tile_e[0:1, ds(i, 1)], min_val=0, max_val=E - 1) for e in (PE, VE)]

            def front(i, u, te, tv):
                need(PE, T_lo, i)
                for q in range(2):
                    need(PE, U_z, i - 2, str(q))
                    for k in range(4 * q, 4 * q + 4):
                        w = [[e1[h][:, ds(te, 1), ch, k * P:k * P + P].squeeze(1) for h in range(2)]
                             for ch in range(DC)]
                        x = [[xgT[u][h][:, ch, :] for h in range(2)] for ch in range(DC)]
                        mm = three_passes(PE, ps[:, 2 * u + q, (k % 4) * P:(k % 4) * P + P], list(zip(w, x)))
                    U_pe.did(str(q), mm)
                for q in range(2):
                    z = zf[:, q * GT:(q + 1) * GT]
                    need(VE, U_pe, i, str(q))
                    need(VE, U_lo, i - 1)
                    bias = b1e[:, ds(tv, 1), 4 * q:4 * q + 4].squeeze(1).unsqueeze(2).broadcast_to((P, 4, P))
                    U_z.did(str(q), VE.scalar_tensor_tensor(z.rearrange("p (k t) -> p k t", k=4),
                                                            ps[:, 2 * u + q, :].rearrange("p (k t) -> p k t", k=4),
                                                            1 / WS, bias, ALU.mult, ALU.add))
                    need(SC, U_z, i, str(q))
                    U_g.did(f"g{q}", SC.activation(z, z, ACT.Gelu_apprx_tanh))
                zz = zf.rearrange("p (k t) -> p k t", k=IC)
                need(SC, U_g, i, "g1")
                need(SC, D_pe, i - 2)
                U_g.did("hi", SC.copy(he[u][0], zz))
                need(VE, U_g, i)
                U_lo.did("done", VE.tensor_tensor(he[u][1], zz, he[u][0], ALU.subtract))

            def back(i, u, half_i, te, tv):
                need(PE, U_lo, i)
                need(PE, D_ev, i - 2)
                h = [[he[u][j][:, k, :] for j in range(2)] for k in range(IC)]
                w = [[e2[j][:, ds(te, 1), k, :].squeeze(1) for j in range(2)] for k in range(IC)]
                D_pe.did("done", three_passes(PE, ps[:, 4 + u, 0:D], list(zip(h, w))))
                need(VE, D_pe, i)
                need(VE, Y_st[u], half_i - 1)
                D_ev.did("done", VE.scalar_tensor_tensor(yo[u][:, :], ps[:, 4 + u, 0:D], 1 / WS,
                                                         b2e[:, ds(tv, 1), :].squeeze(1), ALU.mult, ALU.add))
                need(SY, D_ev, i)
                SY.dma_start(ry[i], yo[u][:, :]).then_inc(Y_st[u].sem, 16)

            need(PE, cut_p, 4 * E - 1)
            load_rows(0, 0)
            load_rows(1, 1)
            turn(0, 0, 0)
            turn(1, 1, 0)
            load_rows(2, 0)
            front(0, 0, *expert_of(0))

            def expert_step(i, u, half_i, this, following, load=True):
                if load:
                    load_rows(i + 3, 1 - u)
                turn(i + 2, u, half_i + 1)
                front(i + 1, 1 - u, *following)
                back(i, u, half_i, *this)

            assert (NTILE - 3) % 4 == 0
            with nc.Fori(0, (NTILE - 3) // 4) as h:
                e = [expert_of(h * 4 + k) for k in range(5)]
                for k in range(4):
                    expert_step(h * 4 + k, k % 2, h * 2 + k // 2, e[k], e[k + 1])
            i = NTILE - 3
            e = [expert_of(i + k) for k in range(3)]
            expert_step(i, 0, i // 2, e[0], e[1], load=False)
            front(i + 2, 0, *e[2])
            back(i + 1, 1, i // 2, *e[1])
            back(i + 2, 0, i // 2 + 1, *e[2])

            gat = [stage(c, f"gat{k}", unit=16, ahead=0) for k in range(4)]
            C_ve = stage(c, "C_ve")
            N_st = stage(c, "N_st", "st", "ag")
            N_ve = stage(c, "N_ve", "eps", *(f"n{t}" for t in range(TG)))
            N_po = stage(c, "N_po")
            stored = stage(c, "stored", unit=16)
            st3, mv3, ve3, rs3 = (sb(c, k, [P, n * TG, w])
                                  for k, n, w in (("st3", 2, 6), ("mv3", 2, 2), ("ve3", 1, 1), ("rs3", 1, 1)))
            nc.all_engine_barrier()
            need(PO, Y_st[0], NTILE // 2)
            need(PO, Y_st[1], NTILE // 2 - 1)
            ov = out.rearrange("b (t p) d -> p (b t) d", p=P)

            def scales(q):
                need(PO, N_ve, q, "eps")
                N_po.did("done", PO.tensor_tensor(rs3[:, :, 0], ve3[:, :, 0], powh[:, 0:TG], ALU.pow))

            def normalised(q):
                need(VE, N_po, q)
                for t in range(TG):
                    x = xs[:, q * TG + t, :]
                    j = q % 2 * TG + t
                    N_ve.did(f"n{t}", VE.tensor_scalar(x, x, mv3[:, j, 0:1], rs3[:, t, 0:1], ALU.subtract,
                                                     ALU.mult))
                need(SY, N_ve, q)
                SY.dma_start(ov[:, q * TG:(q + 1) * TG, :], xs[:, q * TG:(q + 1) * TG, :]).then_inc(stored.sem, 16)

            for n in range(2 * NT):
                t, k = n // 2, n % 2
                buf = piece[n % 4][:, 0:D]
                need(PO, C_ve, n - 4)
                PO.indirect_dma_start(buf, None, rows_y,
                                      bass.IndirectOffsetOnAxis(ap=idx0[:, k, t:t + 1], axis=0)).then_inc(
                    gat[n % 4].sem, 16)
                if n % (2 * TG) == 4 and t > TG:
                    scales(t // TG - 1)
                if n % (2 * TG) == 5 and t > TG:
                    normalised(t // TG - 1)
                need(VE, gat[n % 4], n // 4)
                need(VE, C_ve, n - 1)
                C_ve.did("done", VE.scalar_tensor_tensor(xs[:, t, :], buf, top_w[:, k, t:t + 1], xs[:, t, :],
                                                         ALU.mult, ALU.add))
                if k == 1:
                    j = t % (2 * TG)
                    need(VE, C_ve, n)
                    need(VE, N_ve, t // TG - 2)
                    N_st.did("st", VE.bn_stats(st3[:, j, :], xs[:, t, :]))
                    need(VE, N_st, t, "st")
                    N_st.did("ag", VE.bn_aggr(mv3[:, j, :], st3[:, j, :]))
                if n % (2 * TG) == 2 * TG - 1:
                    need(VE, N_st, t)
                    half_b = slice(t // TG % 2 * TG, t // TG % 2 * TG + TG)
                    N_ve.did("eps", VE.tensor_scalar(ve3[:, :, :], mv3[:, half_b, 1:2], LN_EPS, None, ALU.add))
            scales(NG - 1)
            normalised(NG - 1)
            need(SY, stored, NG - 1)


NORM_STEPS = 14


_INS = ['x', 'ctx_1024', 'L0_attn_Wq', 'L0_attn_Wk', 'L0_attn_Wv', 'L0_attn_Wo', 'L0_attn_bo',
        'L0_xattn_Wq', 'L0_xattn_Wk', 'L0_xattn_Wv', 'L0_xattn_gru_wih', 'L0_xattn_gru_whh',
        'L0_xattn_gru_bih', 'L0_xattn_gru_bhh', 'L0_xattn_slot_norm_w', 'L0_xattn_input_norm_w',
        'L0_ffn_gate_w', 'L0_ffn_gate_b', 'L0_ffn_sh_w1', 'L0_ffn_sh_b1', 'L0_ffn_sh_w2', 'L0_ffn_sh_b2',
        'L0_ffn_ew1', 'L0_ffn_eb1', 'L0_ffn_ew2', 'L0_ffn_eb2']
_OUT = ((8, 256, 256), 'float32')


def kernel(**inputs):
    import numpy as _np
    import concourse.bacc as _bacc
    from concourse.bass_utils import run_bass_kernel_spmd as _run

    nc = _bacc.Bacc("TRN2", target_bir_lowering=False, num_devices=1)
    arrays, args = {}, {}
    for name in _INS:
        v = _np.ascontiguousarray(inputs[name])
        arrays[f"in_{name}"] = v
        args[name] = nc.dram_tensor(f"in_{name}", v.shape, mybir.dt.from_np(v.dtype), kind="ExternalInput").ap()
    out = nc.dram_tensor("out_0", _OUT[0], mybir.dt.from_np(_np.dtype(_OUT[1])), kind="ExternalOutput").ap()
    decoder_layer(nc, args, out)
    r = _run(nc, [arrays], core_ids=[0])
    return r.results[0]["out_0"]
```
